# Optimizing a Trainium2 kernel written in Bass

```python
import numpy as np
import jax
import jax.numpy as jnp

def _softmax(x, axis=-1):
    return jax.nn.softmax(x, axis=axis)

def _gelu(x):
    return jax.nn.gelu(x, approximate=True)

def _silu(x):
    return jax.nn.silu(x)

def _sigmoid(x):
    return jax.nn.sigmoid(x)

def _layernorm(x, axis=-1, eps=1e-05):
    m = jnp.mean(x, axis=axis, keepdims=True)
    v = jnp.var(x, axis=axis, keepdims=True)
    return (x - m) / jnp.sqrt(v + eps)

def _scatter_add(tgt, idx, src, axis=0):
    return tgt.at[idx].add(src)

def _segment_sum(src, seg, n):
    return jax.ops.segment_sum(src, seg, n)
kernel_name = 'mk_decoder_preln_d1_seqx_r4_6d44ad'

def setup_inputs(seed: int=0):
    np.random.seed(seed)
    _w = jnp.asarray

    def _rec_inputs():
        import jax
        import jax.numpy as jnp
        _rk = jax.random.key(seed)
        x = -0.0003929 + 0.9999 * jax.random.normal(jax.random.fold_in(_rk, 1), (8, 512, 512), jnp.float32)
        _lenS = 512 - jax.random.randint(jax.random.fold_in(_rk, 7), (8,), 0, max(1, 512 // 4) + 1, jnp.int32)
        _lenS2 = 64 - jax.random.randint(jax.random.fold_in(_rk, 8), (8,), 0, max(1, 64 // 4) + 1, jnp.int32)
        _ctx_1024P = jax.random.normal(jax.random.fold_in(_rk, 11), (8, 16, 256), jnp.float32)
        _ctx_1024c = jax.random.dirichlet(jax.random.fold_in(_rk, 511), 0.3 * jnp.ones((16,), jnp.float32), (8, 64))
        _ctx_1024t = jnp.einsum('bsk,bkd->bsd', _ctx_1024c, _ctx_1024P)
        _ctx_1024t = _ctx_1024t * jax.lax.rsqrt(jnp.mean(jnp.square(_ctx_1024t)) + 1e-12) * 0.953939
        ctx_1024 = -0.000494167 + 1.00018 * (_ctx_1024t + 0.3 * jax.random.normal(jax.random.fold_in(_rk, 611), (8, 64, 256), jnp.float32))
        _validS = jnp.arange(512)[None, :] < _lenS[:, None]
        _validS2 = jnp.arange(64)[None, :] < _lenS2[:, None]
        _causal = jnp.tril(jnp.ones((512, 512), dtype=bool))
        mask_BxS2_bf1 = jnp.ones((8, 64), dtype=bool)
        return (x, ctx_1024, mask_BxS2_bf1)
    x, ctx_1024, mask_BxS2_bf1 = _rec_inputs()

    def _L0_attn_setup():
        import jax, jax.numpy as jnp
        import numpy as np
        D_MODEL = 512
        N_HEADS = 16
        HEAD_DIM = D_MODEL // N_HEADS
        B, T = (2, 512)
        key = jax.random.key(seed)
        ks = jax.random.split(key, 9)
        s = 0.02
        x = jax.random.normal(ks[0], (B, T, D_MODEL), dtype=jnp.float32)
        Wq = jax.random.normal(ks[1], (N_HEADS, D_MODEL, HEAD_DIM), dtype=jnp.float32) * s
        bq = jax.random.normal(ks[2], (N_HEADS, HEAD_DIM), dtype=jnp.float32) * s
        Wk = jax.random.normal(ks[3], (N_HEADS, D_MODEL, HEAD_DIM), dtype=jnp.float32) * s
        bk = jax.random.normal(ks[4], (N_HEADS, HEAD_DIM), dtype=jnp.float32) * s
        Wv = jax.random.normal(ks[5], (N_HEADS, D_MODEL, HEAD_DIM), dtype=jnp.float32) * s
        bv = jax.random.normal(ks[6], (N_HEADS, HEAD_DIM), dtype=jnp.float32) * s
        Wo = jax.random.normal(ks[7], (D_MODEL, D_MODEL), dtype=jnp.float32) * s
        bo = jax.random.normal(ks[8], (D_MODEL,), dtype=jnp.float32) * s
        return {'x': x, 'Wq': Wq, 'bq': bq, 'Wk': Wk, 'bk': bk, 'Wv': Wv, 'bv': bv, 'Wo': Wo, 'bo': bo}
    _L0_attn_all = _L0_attn_setup()
    _L0_attn_in = {k: v for k, v in _L0_attn_all.items() if k in ('Wq', 'bq', 'Wk', 'bk', 'Wv', 'bv', 'Wo', 'bo')}
    del _L0_attn_all

    def _L0_xattn_setup():
        import jax, jax.numpy as jnp
        import numpy as np
        N_HEADS = 16
        N_KV_HEADS = 8
        HEAD_DIM = 128
        D_TEXT = 512
        D_VISION = 256
        GROUPS = N_HEADS // N_KV_HEADS
        key = jax.random.key(seed)
        ks = jax.random.split(key, 6)
        B, T_text, T_vis = (4, 512, 144)
        text_hidden = jax.random.normal(ks[0], (B, T_text, D_TEXT), dtype=jnp.float32)
        vision_tokens = jax.random.normal(ks[1], (B, T_vis, D_VISION), dtype=jnp.float32)
        vision_mask = jnp.ones((B, T_vis), dtype=bool)
        s = 0.02
        Wq = jax.random.normal(ks[2], (D_TEXT, N_HEADS * HEAD_DIM), dtype=jnp.float32) * s
        Wk = jax.random.normal(ks[3], (D_VISION, N_KV_HEADS * HEAD_DIM), dtype=jnp.float32) * s
        Wv = jax.random.normal(ks[4], (D_VISION, N_KV_HEADS * HEAD_DIM), dtype=jnp.float32) * s
        Wo = jax.random.normal(ks[5], (N_HEADS * HEAD_DIM, D_TEXT), dtype=jnp.float32) * s
        return {'text_hidden': text_hidden, 'vision_tokens': vision_tokens, 'vision_mask': vision_mask, 'Wq': Wq, 'Wk': Wk, 'Wv': Wv, 'Wo': Wo}
    _L0_xattn_all = _L0_xattn_setup()
    _L0_xattn_in = {k: v for k, v in _L0_xattn_all.items() if k in ('Wq', 'Wk', 'Wv', 'Wo')}
    del _L0_xattn_all

    def _L0_ffn_setup():
        import jax, jax.numpy as jnp
        import numpy as np
        B, S, D, R, E = (4, 512, 512, 64, 8)
        SCALING = 64.0 / 16.0
        key = jax.random.key(seed)
        k1, k2, k3, k4 = jax.random.split(key, 4)
        x = jax.random.normal(k1, (B, S, D), dtype=jnp.float32)
        A = jax.random.normal(k2, (E, R, D), dtype=jnp.float32) * 0.02
        Bw = jax.random.normal(k3, (E, D, R), dtype=jnp.float32) * 0.02
        Wg = jax.random.normal(k4, (E, D), dtype=jnp.float32) * 0.02
        return {'x': x, 'A': A, 'Bw': Bw, 'Wg': Wg}
    _L0_ffn_all = _L0_ffn_setup()
    _L0_ffn_in = {k: v for k, v in _L0_ffn_all.items() if k in ('A', 'Bw', 'Wg')}
    del _L0_ffn_all
    return {'x': x, 'ctx_1024': ctx_1024, 'mask_BxS2_bf1': mask_BxS2_bf1, 'L0_attn_Wq': _L0_attn_in['Wq'], 'L0_attn_bq': _L0_attn_in['bq'], 'L0_attn_Wk': _L0_attn_in['Wk'], 'L0_attn_bk': _L0_attn_in['bk'], 'L0_attn_Wv': _L0_attn_in['Wv'], 'L0_attn_bv': _L0_attn_in['bv'], 'L0_attn_Wo': _L0_attn_in['Wo'], 'L0_attn_bo': _L0_attn_in['bo'], 'L0_xattn_Wq': _L0_xattn_in['Wq'], 'L0_xattn_Wk': _L0_xattn_in['Wk'], 'L0_xattn_Wv': _L0_xattn_in['Wv'], 'L0_xattn_Wo': _L0_xattn_in['Wo'], 'L0_ffn_A': _L0_ffn_in['A'], 'L0_ffn_Bw': _L0_ffn_in['Bw'], 'L0_ffn_Wg': _L0_ffn_in['Wg']}

def reference(x, ctx_1024, mask_BxS2_bf1, L0_attn_Wq, L0_attn_bq, L0_attn_Wk, L0_attn_bk, L0_attn_Wv, L0_attn_bv, L0_attn_Wo, L0_attn_bo, L0_xattn_Wq, L0_xattn_Wk, L0_xattn_Wv, L0_xattn_Wo, L0_ffn_A, L0_ffn_Bw, L0_ffn_Wg):
    import jax
    import jax.numpy as jnp

    def _L0_attn_ref(x, Wq, bq, Wk, bk, Wv, bv, Wo, bo):
        import jax, jax.numpy as jnp
        import numpy as np
        D_MODEL = 512
        N_HEADS = 16
        HEAD_DIM = D_MODEL // N_HEADS
        B, T = (2, 512)
        Bn, Tn, C = x.shape
        H, _, D = Wq.shape
        scale = D ** (-0.5)
        q = jnp.einsum('btc,hcd->bhtd', x, Wq) + bq[None, :, None, :]
        k = jnp.einsum('btc,hcd->bhtd', x, Wk) + bk[None, :, None, :]
        v = jnp.einsum('btc,hcd->bhtd', x, Wv) + bv[None, :, None, :]
        scores = jnp.einsum('bhtd,bhsd->bhts', q, k) * scale
        neg = jnp.finfo(scores.dtype).min
        causal = jnp.triu(jnp.full((Tn, Tn), neg, dtype=scores.dtype), k=1)
        probs = jax.nn.softmax(scores + causal, axis=-1)
        y = jnp.einsum('bhts,bhsd->bhtd', probs, v)
        y = y.transpose(0, 2, 1, 3).reshape(Bn, Tn, H * D)
        return y @ Wo + bo

    def _L0_xattn_ref(text_hidden, vision_tokens, vision_mask, Wq, Wk, Wv, Wo):
        import jax, jax.numpy as jnp
        import numpy as np
        N_HEADS = 16
        N_KV_HEADS = 8
        HEAD_DIM = 128
        D_TEXT = 512
        D_VISION = 256
        GROUPS = N_HEADS // N_KV_HEADS
        B, T_text, _ = text_hidden.shape
        T_vis = vision_tokens.shape[1]
        scale = jnp.float32(np.sqrt(HEAD_DIM))
        q = (text_hidden @ Wq).reshape(B, T_text, N_HEADS, HEAD_DIM).transpose(0, 2, 1, 3)
        k = (vision_tokens @ Wk).reshape(B, T_vis, N_KV_HEADS, HEAD_DIM).transpose(0, 2, 1, 3)
        v = (vision_tokens @ Wv).reshape(B, T_vis, N_KV_HEADS, HEAD_DIM).transpose(0, 2, 1, 3)
        k = jnp.repeat(k, GROUPS, axis=1)
        v = jnp.repeat(v, GROUPS, axis=1)
        scores = jnp.einsum('bhtd,bhsd->bhts', q, k) / scale
        mask = vision_mask[:, None, None, :]
        scores = jnp.where(mask, scores, -jnp.inf)
        attn = jax.nn.softmax(scores, axis=-1)
        attn = jnp.nan_to_num(attn, nan=0.0)
        out = jnp.einsum('bhts,bhsd->bhtd', attn, v)
        out = out.transpose(0, 2, 1, 3).reshape(B, T_text, N_HEADS * HEAD_DIM)
        return out @ Wo

    def _L0_ffn_ref(x, A, Bw, Wg):
        import jax, jax.numpy as jnp
        import numpy as np
        B, S, D, R, E = (4, 512, 512, 64, 8)
        SCALING = 64.0 / 16.0
        bsz, seq_len, dim = x.shape
        xf = x.reshape(-1, dim)
        logits = jnp.einsum('nd,ed->ne', xf, Wg)
        prob = jax.nn.softmax(logits, axis=-1)
        gate = jnp.argmax(prob, axis=-1)
        prob_sel = jnp.take_along_axis(prob, gate[:, None], axis=1)
        mask = jax.nn.one_hot(gate, E, dtype=xf.dtype)
        h = jnp.einsum('nd,erd->ner', xf, A)
        h = h * mask[:, :, None]
        y = jnp.einsum('ner,eor->no', h, Bw)
        y = y * SCALING * prob_sel
        return y.reshape(bsz, seq_len, -1)
    x = x + _L0_attn_ref(_layernorm(x, axis=-1), L0_attn_Wq, L0_attn_bq, L0_attn_Wk, L0_attn_bk, L0_attn_Wv, L0_attn_bv, L0_attn_Wo, L0_attn_bo)
    x = x + _L0_xattn_ref(_layernorm(x, axis=-1), ctx_1024, mask_BxS2_bf1, L0_xattn_Wq, L0_xattn_Wk, L0_xattn_Wv, L0_xattn_Wo)
    x = x + _L0_ffn_ref(_layernorm(x, axis=-1), L0_ffn_A, L0_ffn_Bw, L0_ffn_Wg)
    return x

_drawn_inputs = setup_inputs


def setup_inputs(seed=0):
    import zlib

    import numpy as np

    out = dict(_drawn_inputs(seed))
    spreads = {}
    factors = {'L0_attn_Wq': 8.0,
     'L0_attn_bq': 8.0,
     'L0_attn_Wk': 8.0,
     'L0_attn_bk': 8.0,
     'L0_attn_bv': 5.294,
     'L0_attn_bo': 2.729,
     'L0_xattn_Wq': 5.755,
     'L0_xattn_Wk': 5.935}
    for name, (base, spread) in spreads.items():
        noise = np.random.default_rng([zlib.crc32(name.encode()), seed]).standard_normal(out[name].shape)
        drawn = base * np.exp(spread * noise) if base else spread * noise
        out[name] = jnp.asarray(drawn.astype(out[name].dtype))
    for name, factor in factors.items():
        out[name] = (out[name] * factor).astype(out[name].dtype)
    return out
```

```python
import concourse.bass as bass
from concourse import mybir
from concourse.alu_op_type import AluOpType as ALU
from contextlib import ExitStack

F32 = mybir.dt.float32
F32R = mybir.dt.float32r
F16 = mybir.dt.float16
BF16 = mybir.dt.bfloat16
U8 = mybir.dt.uint8
ACT = mybir.ActivationFunctionType
AX = mybir.AxisListType.X

P = 128
B, T, D = 8, 512, 512
TT = T // P
KT = D // P
H, HD = 16, D // 16
QUADS = H * HD // P
HQ = H // QUADS
XH, XG, XD = 16, 8, 128
S = 64
DC = 256
CT = DC // P
E, R = 8, 64
SCALING = 4.0
EPS = 1e-5
MASKED = -1e30



def raw(ap):
    return ap.bitcast(F32)


def product(nc, out, lhs, rhs, start, stop):
    pairs = [(lhs[0], rhs[0]), (lhs[0], rhs[1]), (lhs[1], rhs[0])]
    for n, (a, b) in enumerate(pairs):
        last = nc.tensor.matmul(out, a, b, start=start and n == 0, stop=stop and n == 2)
    return last


def wait_all(engine, *waits):
    values = [v if isinstance(v, int) else engine.snap(v) for _, v in waits]
    for (sem, _), v in zip(waits, values):
        engine.wait_ge(sem, v)


def cross_products(nc, w_group, ctx_t, m_dram, vw_dram):
    HH = XH // XG
    BP = B // 2
    KV = 2 * CT * XD
    COLS = KV + 2 * HH * D
    USES, BANKS = 2 + HH * KT + BP * HH, 6
    assert USES % BANKS == 0
    BS = B * S

    with ExitStack() as ctx:
        def sb(name, shape, dt):
            return ctx.enter_context(nc.sbuf_tensor("c_" + name, shape, dt))

        def sem(name):
            return ctx.enter_context(nc.semaphore("c_" + name))

        c_raw = sb("c_raw", [P, CT, BS], F32)
        c_hi, c_lo = (sb(f"c_{n}", [P, CT, BS], F32R) for n in ("hi", "lo"))
        w_raw = sb("w_raw", [P, 2, COLS], F32)
        w_hi, w_lo = (sb(f"w_{n}", [P, 2, COLS], F32R) for n in ("hi", "lo"))
        kv_hi, kv_lo = (sb(f"kv_{n}", [P, 2, 2, BS], F32R) for n in ("hi", "lo"))
        m_out = sb("m_out", [P, B, KT, HH, S], F32)
        vw_out = sb("vw_out", [P, BP, HH, D], F32)
        bank = [ctx.enter_context(nc.psum_tensor(f"c_bank{n}", [P, 512], F32)) for n in range(BANKS)]

        ctx_loaded, ctx_hi_ready, ctx_lo_ready = sem("ctx_loaded"), sem("ctx_hi"), sem("ctx_lo")
        w_loaded = [sem(f"w{n}_loaded") for n in range(2)]
        w_hi_ready, w_lo_ready = sem("w_hi_ready"), sem("w_lo_ready")
        bank_full = sem("bank_full")
        kv_hi_ready, kv_lo_ready = sem("kv_hi_ready"), sem("kv_lo_ready")
        m_by_act, m_by_dve = sem("m_by_act"), sem("m_by_dve")
        vw_by_act, vw_by_dve = sem("vw_by_act"), sem("vw_by_dve")
        m_stored, vw_stored = sem("m_stored"), sem("vw_stored")

        block = ctx.enter_context(nc.Block())

        def wslice(w, par, kind):
            if kind in "kv":
                at = 0 if kind == "k" else KV // 2
                return w[:, par, at:at + KV // 2].rearrange("p (t d) -> p t d", t=CT)
            at = KV + (HH * D if kind == "o" else 0)
            return w[:, par, at:at + HH * D].rearrange("p (h c) -> p h c", h=HH)

        @block.sync
        def _(sp):
            sp.dma_start(c_raw[:, :, :], ctx_t).then_inc(ctx_loaded, 16)
            sp.dma_start(w_raw[:, 0, :], w_group[0]).then_inc(w_loaded[0], 16)
            sp.dma_start(w_raw[:, 1, :], w_group[1]).then_inc(w_loaded[1], 16)

            def store(n, par):
                wait_all(sp, (m_by_act, n * 4 + 4), (m_by_dve, n * 4 + 4))
                sp.dma_start(m_dram[:, :, bass.ds(n, 1), :].rearrange("b p g m -> p b (g m)"),
                             m_out[:, :, :, :, :].rearrange("p b t h s -> p b (t h s)")).then_inc(m_stored, 16)
                wait_all(sp, (vw_by_act, n * 4 + 4), (vw_by_dve, n * 4 + 4))
                rows = vw_dram[:, :, bass.ds(n, 1), :].rearrange("(bp b2) (h s) g e -> b2 h s bp (g e)", b2=2, h=HH)
                for b2 in range(2):
                    for h in range(HH):
                        sp.dma_start(rows[b2, h], vw_out[b2 * S:(b2 + 1) * S, :, h, :]).then_inc(vw_stored, 16)

            sp.sem_inc(m_stored, 16)
            sp.sem_inc(vw_stored, 64)
            with sp.Fori(0, XG // 2 - 1) as i:
                for par in range(2):
                    n = i * 2 + par
                    wait_all(sp, (w_hi_ready, n + 1), (w_lo_ready, n + 1))
                    sp.dma_start(w_raw[:, par, :], w_group[bass.ds(n + 2, 1)].rearrange("g p w -> p (g w)")).then_inc(w_loaded[par], 16)
                    store(n, par)
            for par in range(2):
                store(XG - 2 + par, par)
            sp.wait_ge(m_stored, XG * 16 + 16)
            sp.wait_ge(vw_stored, XG * 64 + 64)

        @block.gpsimd
        def _(pool):
            with pool.Fori(0, XG // 2) as i:
                for par in range(2):
                    pool.wait_ge(w_hi_ready, i * 2 + par + 1)
                    nc.gpsimd.tensor_tensor(w_lo[:, par, :], w_raw[:, par, :], raw(w_hi[:, par, :]),
                                            ALU.subtract).then_inc(w_lo_ready, 1)

        @block.scalar
        def _(act):
            def split_hi(pair, par):
                act.wait_ge(w_loaded[par], pair * 16 + 16)
                nc.scalar.activation(w_hi[:, par, :], w_raw[:, par, :], ACT.Copy).then_inc(w_hi_ready, 1)

            def group(pair, par, more):
                n = pair * 2 + par
                for kv in range(2):
                    act.wait_ge(bank_full, n * USES + kv + 1)
                    nc.scalar.activation(kv_hi[:, par, kv, :], bank[kv][:, :], ACT.Copy,
                                         scale=XD ** -0.5 if kv == 0 else 1.0).then_inc(kv_hi_ready, 1)
                if more:
                    split_hi(pair + par, 1 - par)
                act.wait_ge(m_stored, n * 16 + 16)
                for u in range(2, 2 + HH * KT, 2):
                    h, t = divmod(u - 2, KT)
                    act.wait_ge(bank_full, n * USES + u + 1)
                    nc.scalar.activation(m_out[:, :, t, h, :], bank[u % BANKS][:, :].rearrange("p (b s) -> p b s", b=B),
                                         ACT.Copy).then_inc(m_by_act, 1)
                act.wait_ge(vw_stored, n * 64 + 64)
                for u in range(2 + HH * KT, USES, 2):
                    bp, h = divmod(u - 2 - HH * KT, HH)
                    act.wait_ge(bank_full, n * USES + u + 1)
                    nc.scalar.activation(vw_out[:, bp, h, :], bank[u % BANKS][:, :], ACT.Copy).then_inc(vw_by_act, 1)

            act.wait_ge(ctx_loaded, 16)
            nc.scalar.activation(c_hi[:, :, :], c_raw[:, :, :], ACT.Copy).then_inc(ctx_hi_ready, 1)
            split_hi(0, 0)
            with act.Fori(0, XG // 2 - 1) as i:
                group(i, 0, True)
                group(i, 1, True)
            group(XG // 2 - 1, 0, True)
            group(XG // 2 - 1, 1, False)

        @block.vector
        def _(dve):
            dve.wait_ge(ctx_hi_ready, 1)
            nc.vector.tensor_tensor(c_lo[:, :, :], c_raw[:, :, :], raw(c_hi[:, :, :]), ALU.subtract).then_inc(ctx_lo_ready, 1)
            with dve.Fori(0, XG // 2) as i:
                for par in range(2):
                    n = i * 2 + par
                    for kv in range(2):
                        dve.wait_ge(kv_hi_ready, n * 2 + kv + 1)
                        nc.vector.scalar_tensor_tensor(kv_lo[:, par, kv, :], bank[kv][:, :], XD ** -0.5 if kv == 0 else 1.0,
                                                       raw(kv_hi[:, par, kv, :]), ALU.mult, ALU.subtract)\
                            .then_inc(kv_lo_ready, 1)
                    dve.wait_ge(m_stored, n * 16 + 16)
                    for u in range(3, 2 + HH * KT, 2):
                        h, t = divmod(u - 2, KT)
                        dve.wait_ge(bank_full, n * USES + u + 1)
                        nc.vector.tensor_copy(m_out[:, :, t, h, :], bank[u % BANKS][:, :].rearrange("p (b s) -> p b s", b=B))\
                            .then_inc(m_by_dve, 1)
                    dve.wait_ge(vw_stored, n * 64 + 64)
                    for u in range(3 + HH * KT, USES, 2):
                        bp, h = divmod(u - 2 - HH * KT, HH)
                        dve.wait_ge(bank_full, n * USES + u + 1)
                        nc.vector.tensor_copy(vw_out[:, bp, h, :], bank[u % BANKS][:, :]).then_inc(vw_by_dve, 1)

        @block.tensor
        def _(pe):
            pe.wait_ge(ctx_lo_ready, 1)

            def group(n, par, first):
                pe.wait_ge(w_lo_ready, n + 1)

                def drained(u):
                    before, m = (u - BANKS, n) if u >= BANKS else (u - BANKS + USES, n - 1)
                    if u < BANKS and first:
                        return
                    if before < 2:
                        pe.wait_ge(kv_lo_ready, m * 2 + before + 1)
                    elif before < 2 + HH * KT:
                        pe.wait_ge((m_by_act, m_by_dve)[before % 2], m * 4 + (before - 2) // 2 + 1)
                    else:
                        pe.wait_ge((vw_by_act, vw_by_dve)[before % 2], m * 4 + (before - 2 - HH * KT) // 2 + 1)

                for kv, kind in enumerate("kv"):
                    drained(kv)
                    for t in range(CT):
                        last = product(nc, bank[kv][:, :], [wslice(w, par, kind)[:, t, :] for w in (w_hi, w_lo)],
                                       [c[:, t, :] for c in (c_hi, c_lo)], t == 0, t == CT - 1)
                    last.then_inc(bank_full, 1)
                pe.wait_ge(kv_lo_ready, n * 2 + 1)
                for u in range(2, 2 + HH * KT):
                    h, t = divmod(u - 2, KT)
                    drained(u)
                    product(nc, bank[u % BANKS][:, :], [wslice(w, par, "q")[:, h, t * P:(t + 1) * P] for w in (w_hi, w_lo)],
                            [k[:, par, 0, :] for k in (kv_hi, kv_lo)], True, True).then_inc(bank_full, 1)
                pe.wait_ge(kv_lo_ready, n * 2 + 2)
                for u in range(2 + HH * KT, USES):
                    bp, h = divmod(u - 2 - HH * KT, HH)
                    drained(u)
                    product(nc, bank[u % BANKS][:, :], [v[:, par, 1, bp * P:(bp + 1) * P] for v in (kv_hi, kv_lo)],
                            [wslice(w, par, "o")[:, h, :] for w in (w_hi, w_lo)], True, True).then_inc(bank_full, 1)

            group(0, 0, True)
            group(1, 1, False)
            with pe.Fori(1, XG // 2) as i:
                group(i * 2, 0, False)
                group(i * 2 + 1, 1, False)


def units_of_batch():
    out = []
    for q in range(QUADS):
        for i in range(TT):
            step = max(1, TT // (i + 1)) if i < 2 else 1
            step = min(step, HQ)
            for j in range(0, HQ, step):
                out.append((q, i, list(range(j, j + step))))
    return out


def self_attention(nc, x, w_self, bias_self, bo, x1_dram):
    UNITS = units_of_batch()
    NU = len(UNITS)
    PQ = NU // QUADS
    GROUPS = QUADS * TT
    V3 = 3 * HD
    QSCALE = HD ** -0.5
    WQ, WK, WV, WO = (n * D for n in range(4))
    ENDS = [q * TT + i if heads[-1] == HQ - 1 else None for q, i, heads in UNITS]

    with ExitStack() as ctx:
        def sb(name, shape, dt):
            return ctx.enter_context(nc.sbuf_tensor("a_" + name, shape, dt))

        def pb(name):
            return ctx.enter_context(nc.psum_tensor("a_" + name, [P, 512], F32))

        def sem(name):
            return ctx.enter_context(nc.semaphore("a_" + name))

        w_raw = sb("w_raw", [P, KT, 4 * D], F32)
        w_hi, w_lo = (sb(f"w_{n}", [P, KT, 4 * D], F32R) for n in ("hi", "lo"))
        bias = sb("bias", [P, 3, QUADS], F32)
        bias_q = sb("bias_q", [P, QUADS], F32)
        bo_all = sb("bo_all", [P, D], F32)
        ident = sb("ident", [P, P], F32)
        ident_bf = sb("ident_bf", [P, P], BF16)
        causal = sb("causal", [P, P], F32)
        causal_bf = sb("causal_bf", [P, P], BF16)
        minus_half = sb("minus_half", [P, TT], F32)
        x_in = sb("x_in", [P, TT, D], F32)
        x_res = sb("x_res", [P, TT, D], F32)
        stats = sb("stats", [P, TT, 6], F32)
        moments = sb("moments", [P, TT, 2], F32)
        beat = sb("beat", [P, TT], F32)
        var_eps = sb("var_eps", [P, TT], F32)
        rstd = sb("rstd", [P, TT], F32)
        xn = sb("xn", [P, TT, D], F32)
        xt_hi, xt_lo = (sb(f"xt_{n}", [P, KT, T], F32R) for n in ("hi", "lo"))
        qk = sb("qk", [P, 4, T], F32R)
        Q_LO, Q_HI, K_HI, K_LO = range(4)
        stack = [sb(f"stack{n}", [3 * HD, 2, HQ, T], F32R) for n in range(2)]
        v_rest = sb("v_rest", [P, 2, D], F32)
        v = sb("v", [P, TT, H, 3, HD], BF16)
        neg_max = sb("neg_max", [P, GROUPS * HQ], F32)
        sums = sb("sums", [P, GROUPS * HQ], F32)
        probs = sb("probs", [P, 2, T], F32)
        pt_hi, pt_lo = (sb(f"pt_{n}", [P, 2, T], F16) for n in ("hi", "lo"))
        y_sum = sb("y_sum", [P, 2, P], F32)
        y_rec = sb("y_rec", [P, 2, HQ], F32)
        y = sb("y", [P, TT, D], F32)
        gemm = [pb(f"gemm{n}") for n in range(2)]
        score = [pb(f"score{n}") for n in range(2)]
        turned = [pb(f"turned{n}") for n in range(2)]
        out_y = [pb(f"out_y{n}") for n in range(2)]

        w_loaded = [sem(f"w{t}_loaded") for t in range(KT)]
        w_hi_ready, w_lo_ready = sem("w_hi_ready"), sem("w_lo_ready")
        small_loaded, consts_pool, consts_ready = sem("small_loaded"), sem("consts_pool"), sem("consts_ready")
        x_loaded, x_res_ready = sem("x_loaded"), sem("x_res_ready")
        var_ready, rstd_ready, xn_ready = sem("var_ready"), sem("rstd_ready"), sem("xn_ready")
        gemm_full, gemm_drained = sem("gemm_full"), sem("gemm_drained")
        xt_hi_ready = sem("xt_hi_ready")
        qk_hi_ready = sem("qk_hi_ready")
        stacked = [sem(f"stacked{n}") for n in range(2)]
        v1_ready, v2_ready, v_ready = sem("v1_ready"), sem("v2_ready"), sem("v_ready")
        score_full, max_ready, probs_ready = sem("score_full"), sem("max_ready"), sem("probs_ready")
        turned_full, pt_hi_ready, pt_ready = sem("turned_full"), sem("pt_hi_ready"), sem("pt_ready")
        y_full, y_summed, y_ready = sem("y_full"), sem("y_summed"), sem("y_ready")
        yt_hi_ready = sem("yt_hi_ready")
        x1_stored = sem("x1_stored")
        stats_ready, moments_ready = sem("stats_ready"), sem("moments_ready")

        block = ctx.enter_context(nc.Block())

        G_XT = 0
        G_QK = [KT, KT + 2 + TT, KT + 4 + TT, KT + 6 + TT]
        G_V = KT + 2
        G_YT = KT + 8 + TT
        G_O = G_YT + QUADS
        G_ALL = G_O + TT
        assert G_ALL % 2 == 0

        def drained(b, use):
            return b * G_ALL + use + 3

        STACK_DMAS = 16 * 3 * HQ
        QK_AT = (4, 8)
        YT_AT = (4, 6, 8)

        @block.sync
        def _(sp):
            def load_x(b):
                sp.dma_start(x_in[:, :, :], x[bass.ds(b, 1)].rearrange("b (t p) c -> p (b t) c", p=P)).then_inc(x_loaded, 16)

            def batch(b, more):
                for q in range(QUADS):
                    waits = [(gemm_drained, drained(b, G_QK[q] + 1))]
                    if q >= 2:
                        waits.append((score_full, (b * QUADS + (q - 1)) * PQ))
                    wait_all(sp, *waits)
                    st = stack[q % 2]
                    for j in range(HQ):
                        rows = slice(j * HD, (j + 1) * HD)
                        for r, (of_q, of_k) in enumerate([(Q_HI, K_HI), (Q_HI, K_LO), (Q_LO, K_HI)]):
                            sp.dma_start(raw(st[r * HD:(r + 1) * HD, :, j, :]),
                                         raw(qk[rows, of_q:of_k + 1:of_k - of_q, :])).then_inc(stacked[q % 2], 16)
                    if q == 1 and more:
                        wait_all(sp, (xn_ready, (b + 1) * TT), (x_res_ready, b + 1))
                        load_x(b + 1)
                for t in range(TT):
                    sp.wait_ge(gemm_drained, drained(b, G_O + t))
                    sp.dma_start(x1_dram[bass.ds(b, 1), t * P:(t + 1) * P, :].rearrange("b p c -> p (b c)"),
                                 x_res[:, t, :]).then_inc(x1_stored, 16)

            load_x(0)
            for t in range(KT):
                sp.dma_start(w_raw[:, t, :], w_self[:, t, :]).then_inc(w_loaded[t], 16)
            sp.dma_start(bias[:, :, :], bias_self).then_inc(small_loaded, 16)
            sp.dma_start(bo_all[:, :], bo.to_broadcast([P, D])).then_inc(small_loaded, 16)
            sp.sem_inc(x1_stored, 16)
            with sp.Fori(0, B - 1) as b:
                batch(b, True)
            batch(B - 1, False)
            sp.wait_ge(x1_stored, B * TT * 16 + 16)

        @block.gpsimd
        def _(pool):
            nc.gpsimd.memset(ident[:, :], 0.0).then_inc(consts_pool, 1)
            nc.gpsimd.memset(causal[:, :], 0.0).then_inc(consts_pool, 1)
            nc.gpsimd.memset(minus_half[:, :], -0.5).then_inc(consts_pool, 1)
            pool.wait_ge(consts_pool, 3)
            nc.gpsimd.affine_select(out=ident[:, :], in_=ident[:, :], compare_op=ALU.not_equal, fill=1.0,
                                    base=0, pattern=[[-1, P]], channel_multiplier=1).then_inc(consts_pool, 1)
            nc.gpsimd.affine_select(out=causal[:, :], in_=causal[:, :], compare_op=ALU.is_ge, fill=MASKED,
                                    base=0, pattern=[[-1, P]], channel_multiplier=1).then_inc(consts_pool, 1)
            pool.wait_ge(small_loaded, 32)

            def reciprocal_deviation(b):
                pool.wait_ge(var_ready, b + 1)
                nc.gpsimd.tensor_tensor(rstd[:, :], var_eps[:, :], minus_half[:, :], ALU.pow).then_inc(rstd_ready, 1)

            def batch(b, more):
                pool.wait_ge(x1_stored, b * TT * 16 + 16)
                pool.wait_ge(x_loaded, b * 16 + 16)
                nc.gpsimd.tensor_tensor(x_res[:, :, :], x_in[:, :, :], bo_all[:, :].unsqueeze(1).to_broadcast([P, TT, D]),
                                        ALU.add).then_inc(x_res_ready, 1)
                for t in range(TT):
                    pool.wait_ge(v2_ready, b * TT + t + 1)
                    nc.gpsimd.tensor_tensor(v[:, t, :, 2, :], v_rest[:, t % 2, :].rearrange("p (h d) -> p h d", h=H),
                                            v[:, t, :, 1, :], ALU.subtract).then_inc(v_ready, 1)
                for g in range(GROUPS):
                    q, i = divmod(g, TT)
                    pool.wait_ge(y_summed, b * GROUPS + g + 1)
                    nc.gpsimd.tensor_tensor(y[:, i, q * P:(q + 1) * P].rearrange("p (h d) -> p h d", h=HQ),
                                            y_sum[:, g % 2, :].rearrange("p (h d) -> p h d", h=HQ),
                                            y_rec[:, g % 2, :].unsqueeze(2).to_broadcast([P, HQ, HD]),
                                            ALU.mult).then_inc(y_ready, 1)
                    if g == 3 * TT - 2 and more:
                        reciprocal_deviation(b + 1)

            reciprocal_deviation(0)
            with pool.Fori(0, B - 1) as b:
                batch(b, True)
            batch(B - 1, False)

        @block.scalar
        def _(act):
            for t in range(KT):
                act.wait_ge(w_loaded[t], 16)
                nc.scalar.activation(w_hi[:, t, 0:D], w_raw[:, t, 0:D], ACT.Copy, scale=QSCALE).then_inc(w_hi_ready, 1)
                nc.scalar.activation(w_hi[:, t, D:], w_raw[:, t, D:], ACT.Copy).then_inc(w_hi_ready, 1)
            act.wait_ge(consts_ready, 3)
            with act.Fori(0, B) as b:
                def high_part(use, dst, ready, bias_ap=None):
                    act.wait_ge(gemm_full, b * G_ALL + use + 1)
                    if bias_ap is None:
                        nc.scalar.activation(dst, gemm[use % 2][:, :], ACT.Copy).then_inc(ready, 1)
                    else:
                        nc.scalar.activation(dst, gemm[use % 2][:, :], ACT.Identity, bias=bias_ap).then_inc(ready, 1)

                def qk_hi(q, part):
                    if part == 0 and q:
                        act.wait_ge(stacked[(q - 1) % 2], (b * 2 + (q - 1) // 2 + 1) * STACK_DMAS)
                    high_part(G_QK[q] + part, qk[:, (Q_HI, K_HI)[part], :], qk_hi_ready,
                              bias_q[:, q:q + 1] if part == 0 else bias[:, 1, q:q + 1])

                def values_first(t):
                    act.wait_ge(gemm_full, b * G_ALL + G_V + t + 1)
                    nc.scalar.activation(v[:, t, :, 0, :], gemm[(G_V + t) % 2][:, :].rearrange("p (h d) -> p h d", h=H),
                                         ACT.Copy).then_inc(v1_ready, 1)

                def values_second(t):
                    act.wait_ge(gemm_drained, drained(b, G_V + t))
                    nc.scalar.activation(v[:, t, :, 1, :], v_rest[:, t % 2, :].rearrange("p (h d) -> p h d", h=H),
                                         ACT.Copy).then_inc(v2_ready, 1)

                def exps(n):
                    q, i, heads = UNITS[n]
                    width = (i + 1) * P
                    act.wait_ge(max_ready, b * NU + n + 1)
                    for k, j in enumerate(heads):
                        c = (q * TT + i) * HQ + j
                        ins = nc.scalar.activation(probs[:, n % 2, k * width:(k + 1) * width],
                                                   score[n % 2][:, k * width:(k + 1) * width], ACT.Exp,
                                                   bias=neg_max[:, c:c + 1], accum_out=sums[:, c:c + 1])
                    ins.then_inc(probs_ready, 1)

                def probs_hi(n):
                    q, i, heads = UNITS[n]
                    width = (i + 1) * P * len(heads)
                    act.wait_ge(turned_full, b * NU + n + 1)
                    nc.scalar.activation(pt_hi[:, n % 2, 0:width], turned[n % 2][:, 0:width], ACT.Copy).then_inc(pt_hi_ready, 1)

                for t in range(KT):
                    high_part(G_XT + t, xt_hi[:, t, :], xt_hi_ready)
                qk_hi(0, 0)
                qk_hi(0, 1)
                for t in range(TT):
                    values_first(t)
                    if t:
                        values_second(t - 1)
                values_second(TT - 1)
                qk_hi(1, 0)
                qk_hi(1, 1)
                for n in range(NU):
                    q, m = divmod(n, PQ)
                    exps(n)
                    if n:
                        probs_hi(n - 1)
                    if q < QUADS - 2 and m in QK_AT:
                        qk_hi(q + 2, QK_AT.index(m))
                    if q == QUADS - 1 and m in YT_AT:
                        t = YT_AT.index(m)
                        high_part(G_YT + t, xt_hi[:, t, :], yt_hi_ready, bias[:, 2, t:t + 1])
                probs_hi(NU - 1)
                high_part(G_YT + QUADS - 1, xt_hi[:, QUADS - 1, :], yt_hi_ready, bias[:, 2, QUADS - 1:QUADS])

        @block.vector
        def _(dve):
            dve.sem_inc(gemm_drained, 2)
            dve.wait_ge(consts_pool, 5)
            nc.vector.tensor_copy(ident_bf[:, :], ident[:, :]).then_inc(consts_ready, 1)
            nc.vector.tensor_copy(causal_bf[:, :], causal[:, :]).then_inc(consts_ready, 1)
            dve.wait_ge(small_loaded, 32)
            nc.vector.tensor_scalar(bias_q[:, :], bias[:, 0, :], QSCALE, None, ALU.mult).then_inc(consts_ready, 1)
            dve.wait_ge(consts_ready, 3)

            def ln_stats(b, t):
                dve.wait_ge(x_loaded, b * 16 + 16)
                nc.vector.bn_stats(stats[:, t, :], x_in[:, t, :]).then_inc(stats_ready, 1)

            def ln_moments(b, t):
                dve.wait_ge(stats_ready, b * TT + t + 1)
                nc.vector.memset(beat[:, t:t + 1], 0.0).then_inc(moments_ready, 1)
                nc.vector.bn_aggr(moments[:, t, :], stats[:, t, :]).then_inc(moments_ready, 1)

            def ln_variance(b):
                dve.wait_ge(moments_ready, 2 * (b * TT + TT))
                nc.vector.tensor_scalar(var_eps[:, :], moments[:, :, 1], EPS, None, ALU.add).then_inc(var_ready, 1)

            def ln_normalise(b, t):
                dve.wait_ge(rstd_ready, b + 1)
                nc.vector.tensor_scalar(xn[:, t, :], x_in[:, t, :], moments[:, t, 0:1], rstd[:, t:t + 1],
                                        ALU.subtract, ALU.mult).then_inc(xn_ready, 1)

            def batch(b, more):
                def low_part(use, ready_hi, count, hi, lo, bias_ap=None):
                    dve.wait_ge(ready_hi, count)
                    if bias_ap is None:
                        ins = nc.vector.tensor_tensor(lo, gemm[use % 2][:, :], raw(hi), ALU.subtract)
                    else:
                        ins = nc.vector.scalar_tensor_tensor(lo, gemm[use % 2][:, :], bias_ap, raw(hi), ALU.add, ALU.subtract)
                    ins.then_inc(gemm_drained, 1)

                def qk_lo(q, part):
                    low_part(G_QK[q] + part, qk_hi_ready, (b * QUADS + q) * 2 + part + 1,
                             qk[:, (Q_HI, K_HI)[part], :], qk[:, (Q_LO, K_LO)[part], :],
                             bias_q[:, q:q + 1] if part == 0 else bias[:, 1, q:q + 1])

                def values_rest(t):
                    dve.wait_ge(v1_ready, b * TT + t + 1)
                    if t >= 2:
                        dve.wait_ge(v_ready, b * TT + t - 1)
                    nc.vector.tensor_tensor(v_rest[:, t % 2, :].rearrange("p (h d) -> p h d", h=H),
                                            gemm[(G_V + t) % 2][:, :].rearrange("p (h d) -> p h d", h=H),
                                            v[:, t, :, 0, :], ALU.subtract).then_inc(gemm_drained, 1)

                def row_max(n):
                    q, i, heads = UNITS[n]
                    width, k = (i + 1) * P, len(heads)
                    c = (q * TT + i) * HQ + heads[0]
                    dve.wait_ge(score_full, b * NU + n + 1)
                    nc.vector.tensor_reduce(neg_max[:, c:c + k], score[n % 2][:, 0:k * width].rearrange("p (h s) -> p h s", h=k),
                                            AX, ALU.max, negate=True).then_inc(max_ready, 1)

                def probs_lo(n):
                    q, i, heads = UNITS[n]
                    width = (i + 1) * P * len(heads)
                    dve.wait_ge(pt_hi_ready, b * NU + n + 1)
                    nc.vector.tensor_tensor(pt_lo[:, n % 2, 0:width], turned[n % 2][:, 0:width], pt_hi[:, n % 2, 0:width],
                                            ALU.subtract).then_inc(pt_ready, 1)

                def outputs(g):
                    dve.wait_ge(y_full, b * GROUPS + g + 1)
                    if g >= 2:
                        dve.wait_ge(y_ready, b * GROUPS + g - 1)
                    nc.vector.reciprocal(y_rec[:, g % 2, :], sums[:, g * HQ:(g + 1) * HQ])
                    nc.vector.tensor_reduce(y_sum[:, g % 2, :].rearrange("p (h d) -> p h d", h=HQ),
                                            out_y[g % 2][:, 0:HQ * V3].rearrange("p (h k d) -> p h d k", h=HQ, k=3),
                                            AX, ALU.add).then_inc(y_summed, 1)

                def yt_lo(t):
                    low_part(G_YT + t, yt_hi_ready, b * QUADS + t + 1, xt_hi[:, t, :], xt_lo[:, t, :],
                             bias[:, 2, t:t + 1])

                for t in range(KT):
                    low_part(G_XT + t, xt_hi_ready, b * KT + t + 1, xt_hi[:, t, :], xt_lo[:, t, :])
                qk_lo(0, 0)
                qk_lo(0, 1)
                for t in range(TT):
                    values_rest(t)
                qk_lo(1, 0)
                qk_lo(1, 1)
                row_max(0)
                row_max(1)
                for n in range(NU):
                    q, m = divmod(n, PQ)
                    if n + 2 < NU:
                        row_max(n + 2)
                    if n >= 2 and ENDS[n - 2] is not None:
                        outputs(ENDS[n - 2])
                    probs_lo(n)
                    if q < QUADS - 2 and m in QK_AT:
                        qk_lo(q + 2, QK_AT.index(m))
                    if q == QUADS - 1 and m in YT_AT:
                        yt_lo(YT_AT.index(m))
                    if more and q == 2:
                        if m < TT:
                            ln_stats(b + 1, m)
                        elif m < 2 * TT:
                            ln_moments(b + 1, m - TT)
                        elif m == 2 * TT:
                            ln_variance(b + 1)
                    if more and q == 3 and m < TT:
                        ln_normalise(b + 1, m)
                for n in (NU - 2, NU - 1):
                    if ENDS[n] is not None:
                        outputs(ENDS[n])
                yt_lo(QUADS - 1)
                dve.wait_ge(x_res_ready, b + 1)
                for t in range(TT):
                    dve.wait_ge(gemm_full, b * G_ALL + G_O + t + 1)
                    nc.vector.tensor_tensor(x_res[:, t, :], gemm[(G_O + t) % 2][:, :], x_res[:, t, :], ALU.add)\
                        .then_inc(gemm_drained, 1)

            for t in range(TT):
                ln_stats(0, t)
            for t in range(TT):
                ln_moments(0, t)
            ln_variance(0)
            for t in range(KT):
                dve.wait_ge(w_hi_ready, 2 * t + 2)
                nc.vector.scalar_tensor_tensor(w_lo[:, t, 0:D], w_raw[:, t, 0:D], QSCALE, raw(w_hi[:, t, 0:D]),
                                               ALU.mult, ALU.subtract).then_inc(w_lo_ready, 1)
                nc.vector.tensor_tensor(w_lo[:, t, D:], w_raw[:, t, D:], raw(w_hi[:, t, D:]), ALU.subtract).then_inc(w_lo_ready, 1)
            for t in range(TT):
                ln_normalise(0, t)
            with dve.Fori(0, B - 1) as b:
                batch(b, True)
            batch(B - 1, False)

        @block.tensor
        def _(pe):
            pe.wait_ge(consts_ready, 3)
            pe.wait_ge(w_lo_ready, 2 * KT)
            with pe.Fori(0, B) as b:
                def gemm_bank(use):
                    pe.wait_ge(gemm_drained, drained(b, use - 2))
                    return gemm[use % 2]

                def transpose_tiles(use, src, k):
                    out = gemm_bank(use)
                    for t in range(TT):
                        last = nc.tensor.transpose(out[:, t * P:(t + 1) * P], src[:, t, k * P:(k + 1) * P], ident[:, :])
                    last.then_inc(gemm_full, 1)

                def qk_product(q, part, k0, k1):
                    use, col = G_QK[q] + part, (WQ, WK)[part] + q * P
                    out = gemm_bank(use) if k0 == 0 else gemm[use % 2]
                    for k in range(k0, k1):
                        last = product(nc, out[:, :], [w[:, k, col:col + P] for w in (w_hi, w_lo)],
                                       [xt[:, k, :] for xt in (xt_hi, xt_lo)], k == 0, k == KT - 1)
                    if k1 == KT:
                        last.then_inc(gemm_full, 1)

                def token_product(use, t, col):
                    out = gemm_bank(use)
                    for k in range(KT):
                        last = product(nc, out[:, :], [xt[:, k, t * P:(t + 1) * P] for xt in (xt_hi, xt_lo)],
                                       [w[:, k, col:col + D] for w in (w_hi, w_lo)], k == 0, k == KT - 1)
                    last.then_inc(gemm_full, 1)

                def scores(n):
                    q, i, heads = UNITS[n]
                    if n % PQ == 0:
                        pe.wait_ge(stacked[q % 2], (b * 2 + q // 2 + 1) * STACK_DMAS)
                    width = (i + 1) * P
                    st = stack[q % 2]
                    for k, j in enumerate(heads):
                        at = k * width
                        nc.tensor.matmul(score[n % 2][:, at:at + width], st[:, 0, j, i * P:(i + 1) * P], st[:, 1, j, 0:width],
                                         start=True, stop=False)
                        last = nc.tensor.matmul(score[n % 2][:, at + i * P:at + width], ident_bf[:, :], causal_bf[:, :],
                                                start=False, stop=True)
                    last.then_inc(score_full, 1)

                def turn(n):
                    q, i, heads = UNITS[n]
                    pe.wait_ge(probs_ready, b * NU + n + 1)
                    for c in range((i + 1) * len(heads)):
                        last = nc.tensor.transpose(turned[n % 2][:, c * P:(c + 1) * P], probs[:, n % 2, c * P:(c + 1) * P],
                                                   ident[:, :])
                    last.then_inc(turned_full, 1)

                def weigh(n):
                    q, i, heads = UNITS[n]
                    g = q * TT + i
                    pe.wait_ge(pt_ready, b * NU + n + 1)
                    if heads[0] == 0:
                        if g >= 2:
                            pe.wait_ge(y_summed, b * GROUPS + g - 1)
                        if q == 0:
                            pe.wait_ge(v_ready, b * TT + i + 1)
                    for k, j in enumerate(heads):
                        at = j * V3
                        for s in range(i + 1):
                            c = (k * (i + 1) + s) * P
                            val = v[:, s, q * HQ + j, :, :].rearrange("p k d -> p (k d)")
                            nc.tensor.matmul(out_y[g % 2][:, at:at + V3], pt_hi[:, n % 2, c:c + P], val,
                                             start=s == 0, stop=False)
                            last = nc.tensor.matmul(out_y[g % 2][:, at:at + 2 * HD], pt_lo[:, n % 2, c:c + P], val[:, 0:2 * HD],
                                                    start=False, stop=s == i)
                    if ENDS[n] is not None:
                        last.then_inc(y_full, 1)

                pe.wait_ge(xn_ready, b * TT + TT)
                for k in range(KT):
                    transpose_tiles(G_XT + k, xn, k)
                pe.wait_ge(gemm_drained, drained(b, G_XT + KT - 1))
                qk_product(0, 0, 0, KT)
                qk_product(0, 1, 0, KT)
                for t in range(TT):
                    token_product(G_V + t, t, WV)
                qk_product(1, 0, 0, KT)
                qk_product(1, 1, 0, KT)
                scores(0)
                scores(1)
                for n in range(NU):
                    q, m = divmod(n, PQ)
                    turn(n)
                    if n + 2 < NU:
                        scores(n + 2)
                    if q < QUADS - 2 and m < 2 * KT:
                        qk_product(q + 2, m // KT, m % KT, m % KT + 1)
                    if q == QUADS - 1 and m + 1 in YT_AT:
                        k = YT_AT.index(m + 1)
                        pe.wait_ge(y_ready, b * GROUPS + (k + 1) * TT)
                        transpose_tiles(G_YT + k, y, k)
                    if n:
                        weigh(n - 1)
                weigh(NU - 1)
                pe.wait_ge(y_ready, b * GROUPS + GROUPS)
                transpose_tiles(G_YT + QUADS - 1, y, QUADS - 1)
                pe.wait_ge(gemm_drained, drained(b, G_YT + QUADS - 1))
                for t in range(TT):
                    token_product(G_O + t, t, WO)


def cross_attention_and_experts(nc, x1_dram, m_dram, vw_dram, mask, w_experts, w_gate, out):
    HS = XH * S
    HALF = XG // 2
    PAIRS = HS // P
    MW = XG * KT * 2 * S
    assert MW == XG * D

    def neighbour(b, t, d):
        bb, tt = b + (t + d) // TT, (t + d) % TT
        if isinstance(b, int) and not 0 <= bb < B:
            return None
        return bb, tt, bb * TT + tt

    with ExitStack() as ctx:
        def sb(name, shape, dt):
            return ctx.enter_context(nc.sbuf_tensor("b_" + name, shape, dt))

        def pb(name, shape=(P, 512)):
            return ctx.enter_context(nc.psum_tensor("b_" + name, list(shape), F32))

        def sem(name):
            return ctx.enter_context(nc.semaphore("b_" + name))

        m_raw = sb("m_raw", [P, MW], F32)
        vw_raw = sb("vw_raw", [P, MW], F32)
        m_hi, m_lo = (sb(f"m_{n}", [P, MW], F32R) for n in ("hi", "lo"))
        vw_hi, vw_lo = (sb(f"vw_{n}", [P, MW], F32R) for n in ("hi", "lo"))
        we_hi, we_lo = (sb(f"we_{n}", [P, KT, 2 * D], F32R) for n in ("hi", "lo"))
        wg_raw = sb("wg_raw", [P, KT, E], F32)
        wg_hi, wg_lo = (sb(f"wg_{n}", [P, KT, E], F32R) for n in ("hi", "lo"))
        ident = sb("ident", [P, P], F32)
        minus_half = sb("minus_half", [P, 1], F32)
        order = sb("order", [P, E], F32)
        row0 = sb("row0", [P, P], BF16)
        mask_u8 = sb("mask_u8", [P, B * S], U8)
        mask_f = sb("mask_f", [P, B * S], F32)
        mask_add = sb("mask_add", [P, B, S], BF16)
        any_key = sb("any_key", [P, B], F32)
        x1 = sb("x1", [P, TT, D], F32)
        x2 = sb("x2", [P, TT, D], F32)
        beat = sb("beat", [P, 1], F32)
        ln = {k: (sb(f"stats{k}", [P, 6], F32), sb(f"moments{k}", [P, 2], F32), sb(f"var{k}", [P, 1], F32),
                  sb(f"rstd{k}", [P, 1], F32), sb(f"xn{k}", [P, D], F32)) for k in (2, 3)}
        xt2_hi, xt2_lo = (sb(f"xt2_{n}", [P, KT, P], F32R) for n in ("hi", "lo"))
        xt3_hi, xt3_lo = (sb(f"xt3_{n}", [P, KT, P], F32R) for n in ("hi", "lo"))
        row_max = sb("row_max", [P, XH], F32)
        row_sum = sb("row_sum", [P, XH], F32)
        row_inv = sb("row_inv", [P, XH], F32)
        row_scale = sb("row_scale", [P, XH], F32)
        probs = sb("probs", [P, XH, S], F32)
        pt_hi, pt_lo = (sb(f"pt_{n}", [P, PAIRS, P], F32R) for n in ("hi", "lo"))
        gate_negmax = sb("gate_negmax", [P, 1], F32)
        gate_exp = sb("gate_exp", [P, E], F32)
        gate_sum = sb("gate_sum", [P, 1], F32)
        gate_top = sb("gate_top", [P, 1], F32)
        gate_rank = sb("gate_rank", [P, E], F32)
        gate_best = sb("gate_best", [P, 1], F32)
        gate_one = sb("gate_one", [P, E], F32)
        gate_inv = sb("gate_inv", [P, 1], F32)
        gate_scale = sb("gate_scale", [P, TT], F32)
        hidden = sb("hidden", [P, D], F32)
        ht_hi, ht_lo = (sb(f"ht_{n}", [P, KT, P], F32R) for n in ("hi", "lo"))
        turn = [pb(f"turn{n}") for n in range(2)]
        score = pb("score", (P, 2, 512))
        attended, hid, made, gate = pb("attended"), pb("hid"), pb("made"), pb("gate")

        we_loaded = [sem(f"we{n}_loaded") for n in range(2)]
        we_hi_ready, we_lo_ready = sem("we_hi_ready"), sem("we_lo_ready")
        small_loaded, consts_pool, consts_ready = sem("small_loaded"), sem("consts_pool"), sem("consts_ready")
        m_loaded, m_hi_ready = sem("m_loaded"), sem("m_hi_ready")
        M_CHUNKS = 4
        MC = MW // M_CHUNKS
        m_lo_by_pool, m_lo_by_dve = sem("m_lo_by_pool"), sem("m_lo_by_dve")
        vw_loaded, vw_hi_ready, vw_ready = sem("vw_loaded"), sem("vw_hi_ready"), sem("vw_ready")
        x1_loaded, out_stored = ([sem(f"{n}{t}") for t in range(TT)] for n in ("x1_loaded", "out_stored"))
        stats_ready = {k: sem(f"stats{k}_ready") for k in (2, 3)}
        moments_ready = {k: sem(f"moments{k}_ready") for k in (2, 3)}
        var_ready = {k: sem(f"var{k}_ready") for k in (2, 3)}
        rstd_ready = {k: sem(f"rstd{k}_ready") for k in (2, 3)}
        xn_ready = {k: sem(f"xn{k}_ready") for k in (2, 3)}
        xt2_full, xt2_hi_ready, xt2_ready = sem("xt2_full"), sem("xt2_hi_ready"), sem("xt2_ready")
        xt3_full, xt3_hi_ready, xt3_ready = sem("xt3_full"), sem("xt3_hi_ready"), sem("xt3_ready")
        ht_full, ht_hi_ready, ht_ready = sem("ht_full"), sem("ht_hi_ready"), sem("ht_ready")
        pt_full, pt_hi_ready, pt_ready = sem("pt_full"), sem("pt_hi_ready"), sem("pt_ready")
        score_full, max_ready, shifted, exp_ready = sem("score_full"), sem("max_ready"), sem("shifted"), sem("exp_ready")
        sum_ready, inv_ready, scale_ready, probs_ready = sem("sum_ready"), sem("inv_ready"), sem("scale_ready"), sem("probs_ready")
        attended_full, x2_ready = sem("attended_full"), sem("x2_ready")
        hid_full, hidden_ready = sem("hid_full"), sem("hidden_ready")
        gate_max_ready, gate_exp_ready, gate_step = sem("gate_max_ready"), sem("gate_exp_ready"), sem("gate_step")
        GATE_STEPS = 5
        made_full, out_ready = sem("made_full"), sem("out_ready")

        block = ctx.enter_context(nc.Block())

        def run(engine, step, before=None):
            for t in range(TT):
                step(0, t)
            with engine.Fori(1, B - 1) as b:
                for t in range(TT):
                    step(b, t)
            for t in range(TT):
                step(B - 1, t)
            for t in range(3):
                step(B, t)

        def is_tile(b):
            return not (isinstance(b, int) and b >= B)

        @block.sync
        def _(sp):
            def load_x1(tile):
                b, t, _ = tile
                sp.dma_start(x1[:, t, :], x1_dram[bass.ds(b, 1), t * P:(t + 1) * P, :].rearrange("b p c -> p (b c)")).then_inc(x1_loaded[t], 16)

            def load_m(b):
                sp.dma_start(m_raw[:, :], m_dram[bass.ds(b, 1)].rearrange("b p g m -> p (b g m)")).then_inc(m_loaded, 16)

            def load_vw(b):
                sp.dma_start(vw_raw[:, :], vw_dram[bass.ds(b, 1)].rearrange("b p g m -> p (b g m)")).then_inc(vw_loaded, 16)

            def step(b, t):
                done, ahead, made_tile = neighbour(b, t, -1), neighbour(b, t, 3), neighbour(b, t, -3)
                if ahead and done:
                    sp.wait_ge(x2_ready, done[2] + 1)
                    load_x1(ahead)
                if t == 0 and is_tile(b) and is_tile(b + 1):
                    wait_all(sp, (m_lo_by_pool, (b + 1) * 2), (m_lo_by_dve, (b + 1) * 2))
                    load_m(b + 1)
                if t == 1 and is_tile(b) and is_tile(b + 1):
                    sp.wait_ge(vw_ready, b + 1)
                    load_vw(b + 1)
                if made_tile:
                    _, mt, n = made_tile
                    sp.wait_ge(out_ready, n + 1)
                    sp.dma_start(out.rearrange("b (t p) c -> (b t) p c", p=P)[bass.ds(n, 1)].rearrange("n p c -> p (n c)"),
                                 x2[:, mt, :]).then_inc(out_stored[mt], 16)

            for k in range(KT):
                load_x1((0, k, k))
            half = KT // 2
            sp.dma_start(m_raw[:, :].rearrange("p (k w) -> p k w", w=2 * D)[:, 0:half, :], w_experts[:, 0:half, :]).then_inc(we_loaded[0], 16)
            sp.dma_start(vw_raw[:, :].rearrange("p (k w) -> p k w", w=2 * D)[:, 0:half, :], w_experts[:, half:, :]).then_inc(we_loaded[1], 16)
            sp.dma_start(wg_raw[:, :, :], w_gate).then_inc(small_loaded, 16)
            sp.dma_start(mask_u8[:, :], mask.to_broadcast([P, B * S])).then_inc(small_loaded, 16)
            sp.wait_ge(we_lo_ready, 3)
            load_m(0)
            load_vw(0)
            run(sp, step)
            for t in range(TT):
                sp.wait_ge(out_stored[t], B * 16)

        @block.gpsimd
        def _(pool):
            def deviation(k, n):
                pool.wait_ge(var_ready[k], n + 1)
                nc.gpsimd.tensor_tensor(ln[k][3][:, :], ln[k][2][:, :], minus_half[:, :], ALU.pow).then_inc(rstd_ready[k], 1)

            def m_low(b, c):
                part = slice(c * MC, (c + 1) * MC)
                pool.wait_ge(m_hi_ready, b * M_CHUNKS + c + 1)
                nc.gpsimd.tensor_tensor(m_lo[:, part], m_raw[:, part], raw(m_hi[:, part]), ALU.subtract).then_inc(m_lo_by_pool, 1)

            def vw_low(b):
                pool.wait_ge(vw_hi_ready, b + 1)
                nc.gpsimd.tensor_tensor(vw_lo[:, :], vw_raw[:, :], raw(vw_hi[:, :]), ALU.subtract).then_inc(vw_ready, 1)

            def step(b, t):
                done, ahead = neighbour(b, t, -1), neighbour(b, t, 2)
                last_scored = t == TT - 1 and is_tile(b) and is_tile(b + 1)
                if last_scored:
                    m_low(b + 1, 0)
                if is_tile(b):
                    n = b * TT + t
                    pool.wait_ge(scale_ready, n + 1)
                    nc.gpsimd.tensor_tensor(probs[:, :, :], probs[:, :, :], row_scale[:, :].unsqueeze(2).to_broadcast([P, XH, S]),
                                            ALU.mult).then_inc(probs_ready, 1)
                if last_scored:
                    m_low(b + 1, 2)
                if done:
                    deviation(3, done[2])
                if ahead:
                    deviation(2, ahead[2])
                if t == 0 and is_tile(b) and not (isinstance(b, int) and b == 0):
                    vw_low(b)

            nc.gpsimd.memset(ident[:, :], 0.0).then_inc(consts_pool, 1)
            nc.gpsimd.memset(minus_half[:, :], -0.5).then_inc(consts_pool, 1)
            nc.gpsimd.memset(row0[:, :], 0.0).then_inc(consts_pool, 1)
            for e in range(E):
                nc.gpsimd.memset(order[:, e:e + 1], float(E - e)).then_inc(consts_pool, 1)
            pool.wait_ge(consts_pool, 3 + E)
            nc.gpsimd.affine_select(out=ident[:, :], in_=ident[:, :], compare_op=ALU.not_equal, fill=1.0,
                                    base=0, pattern=[[-1, P]], channel_multiplier=1).then_inc(consts_pool, 1)
            nc.gpsimd.memset(row0[0:1, :], 1.0).then_inc(consts_pool, 1)
            deviation(2, 0)
            deviation(2, 1)
            m_low(0, 0)
            m_low(0, 2)
            vw_low(0)
            run(pool, step)

        @block.scalar
        def _(act):
            def copy_hi(dst, src, full, count, ready):
                act.wait_ge(full, count)
                nc.scalar.activation(dst, src, ACT.Copy).then_inc(ready, 1)

            def split_m(b, chunks):
                for c in chunks:
                    part = slice(c * MC, (c + 1) * MC)
                    if c == 0:
                        act.wait_ge(m_loaded, b * 16 + 16)
                    nc.scalar.activation(m_hi[:, part], m_raw[:, part], ACT.Copy).then_inc(m_hi_ready, 1)

            def split_vw(b):
                act.wait_ge(vw_loaded, b * 16 + 16)
                nc.scalar.activation(vw_hi[:, :], vw_raw[:, :], ACT.Copy).then_inc(vw_hi_ready, 1)

            def flat(ap):
                return ap[:, :, :].rearrange("p k w -> p (k w)")

            def step(b, t):
                done, gated, made_tile, ahead = (neighbour(b, t, d) for d in (-1, -2, -3, 1))
                here = b * TT + t if is_tile(b) else None
                last_scored = t == TT - 1 and is_tile(b) and is_tile(b + 1)
                if done:
                    for half in range(2):
                        w = PAIRS // 2
                        copy_hi(pt_hi[:, half * w:(half + 1) * w, :].rearrange("p k w -> p (k w)"), turn[half][:, :],
                                pt_full, done[2] * 2 + half + 1, pt_hi_ready)
                if made_tile:
                    act.wait_ge(gate_max_ready, made_tile[2] + 1)
                    nc.scalar.activation(gate_exp[:, :], gate[:, 0:E], ACT.Exp, bias=gate_negmax[:, :],
                                         accum_out=gate_sum[:, :]).then_inc(gate_exp_ready, 1)
                if last_scored:
                    act.wait_ge(score_full, here + 1)
                    split_m(b + 1, (0, 1))
                if gated:
                    copy_hi(flat(xt3_hi), turn[0][:, :], xt3_full, gated[2] + 1, xt3_hi_ready)
                if made_tile:
                    copy_hi(flat(ht_hi), turn[1][:, :], ht_full, made_tile[2] + 1, ht_hi_ready)
                if here is not None:
                    act.wait_ge(shifted, here + 1)
                    nc.scalar.activation(probs[:, :, :], probs[:, :, :], ACT.Exp).then_inc(exp_ready, 1)
                if last_scored:
                    split_m(b + 1, (2, 3))
                if ahead:
                    copy_hi(flat(xt2_hi), turn[0][:, :], xt2_full, ahead[2] + 1, xt2_hi_ready)
                if t == 0 and here is not None and not (isinstance(b, int) and b == 0):
                    act.wait_ge(attended_full, here)
                    split_vw(b)

            for h, src in enumerate((m_raw, vw_raw)):
                act.wait_ge(we_loaded[h], 16)
                nc.scalar.activation(we_hi[:, h * KT // 2:(h + 1) * KT // 2, :],
                                     src[:, :].rearrange("p (k w) -> p k w", w=2 * D)[:, 0:KT // 2, :], ACT.Copy).then_inc(we_hi_ready, 1)
            act.wait_ge(small_loaded, 32)
            nc.scalar.activation(wg_hi[:, :, :], wg_raw[:, :, :], ACT.Copy).then_inc(we_hi_ready, 1)
            copy_hi(flat(xt2_hi), turn[0][:, :], xt2_full, 1, xt2_hi_ready)
            split_m(0, range(M_CHUNKS))
            split_vw(0)
            run(act, step)

        @block.vector
        def _(dve):
            def low(dst, psum, hi, hi_ready, count, ready):
                dve.wait_ge(hi_ready, count)
                nc.vector.tensor_tensor(dst, psum, raw(hi), ALU.subtract).then_inc(ready, 1)

            def flat(ap):
                return ap[:, :, :].rearrange("p k w -> p (k w)")

            def layernorm_moments(k, src, n):
                stats, moments, var, _, _ = ln[k]
                nc.vector.bn_stats(stats[:, :], src).then_inc(stats_ready[k], 1)
                dve.wait_ge(stats_ready[k], n + 1)
                nc.vector.memset(beat[:, :], 0.0).then_inc(moments_ready[k], 1)
                nc.vector.bn_aggr(moments[:, :], stats[:, :]).then_inc(moments_ready[k], 1)
                dve.wait_ge(moments_ready[k], 2 * (n + 1))
                nc.vector.tensor_scalar(var[:, :], moments[:, 1:2], EPS, None, ALU.add).then_inc(var_ready[k], 1)

            def normalise(k, src, n):
                _, moments, _, rstd, xn = ln[k]
                dve.wait_ge(rstd_ready[k], n + 1)
                nc.vector.tensor_scalar(xn[:, :], src, moments[:, 0:1], rstd[:, :], ALU.subtract, ALU.mult).then_inc(xn_ready[k], 1)

            def layernorm2_moments(tile):
                b, t, n = tile
                dve.wait_ge(x1_loaded[t], b * 16 + 16)
                layernorm_moments(2, x1[:, t, :], n)

            def choose_expert(n, t):
                s = n * GATE_STEPS
                dve.wait_ge(gate_exp_ready, n + 1)
                nc.vector.tensor_reduce(gate_top[:, :], gate_exp[:, :], AX, ALU.max).then_inc(gate_step, 1)
                nc.vector.reciprocal(gate_inv[:, :], gate_sum[:, :]).then_inc(gate_step, 1)
                dve.wait_ge(gate_step, s + 2)
                nc.vector.scalar_tensor_tensor(gate_rank[:, :], gate_exp[:, :], gate_top[:, :], order[:, :],
                                               ALU.is_ge, ALU.mult).then_inc(gate_step, 1)
                nc.vector.tensor_scalar(gate_scale[:, t:t + 1], gate_inv[:, :], gate_top[:, :], SCALING, ALU.mult, ALU.mult)
                dve.wait_ge(gate_step, s + 3)
                nc.vector.tensor_reduce(gate_best[:, :], gate_rank[:, :], AX, ALU.max).then_inc(gate_step, 1)
                dve.wait_ge(gate_step, s + 4)
                nc.vector.tensor_scalar(gate_one[:, :], gate_rank[:, :], gate_best[:, :], None, ALU.is_equal).then_inc(gate_step, 1)
                dve.wait_ge(gate_step, s + 5)

            def m_low(b, c):
                part = slice(c * MC, (c + 1) * MC)
                dve.wait_ge(m_hi_ready, b * M_CHUNKS + c + 1)
                nc.vector.tensor_tensor(m_lo[:, part], m_raw[:, part], raw(m_hi[:, part]), ALU.subtract).then_inc(m_lo_by_dve, 1)

            def step(b, t):
                done, gated, made_tile, ahead, far = (neighbour(b, t, d) for d in (-1, -2, -3, 1, 2))
                here = b * TT + t if is_tile(b) else None
                last_scored = t == TT - 1 and is_tile(b) and is_tile(b + 1)
                if done:
                    for half in range(2):
                        w = PAIRS // 2
                        part = slice(half * w, (half + 1) * w)
                        low(pt_lo[:, part, :].rearrange("p k w -> p (k w)"), turn[half][:, :],
                            pt_hi[:, part, :].rearrange("p k w -> p (k w)"), pt_hi_ready, done[2] * 2 + half + 1, pt_ready)
                if made_tile:
                    _, mt, n = made_tile
                    dve.wait_ge(hid_full, n + 1)
                    nc.vector.tensor_reduce(gate_negmax[:, :], gate[:, 0:E], AX, ALU.max, negate=True).then_inc(gate_max_ready, 1)
                    choose_expert(n, mt)
                    nc.vector.tensor_tensor(hidden[:, :].rearrange("p (e r) -> p e r", e=E),
                                            hid[:, :].rearrange("p (e r) -> p e r", e=E),
                                            gate_one[:, :].unsqueeze(2).to_broadcast([P, E, R]), ALU.mult).then_inc(hidden_ready, 1)
                if here is not None:
                    dve.wait_ge(score_full, here + 1)
                    s = score[:, :, :].rearrange("p a (h s) -> p (a h) s", s=S)
                    nc.vector.tensor_reduce(row_max[:, :], s, AX, ALU.max).then_inc(max_ready, 1)
                    dve.wait_ge(max_ready, here + 1)
                    nc.vector.tensor_tensor(probs[:, :, :], s, row_max[:, :].unsqueeze(2).to_broadcast([P, XH, S]),
                                            ALU.subtract).then_inc(shifted, 1)
                if gated:
                    low(flat(xt3_lo), turn[0][:, :], flat(xt3_hi), xt3_hi_ready, gated[2] + 1, xt3_ready)
                if made_tile:
                    low(flat(ht_lo), turn[1][:, :], flat(ht_hi), ht_hi_ready, made_tile[2] + 1, ht_ready)
                if last_scored:
                    m_low(b + 1, 1)
                if here is not None:
                    dve.wait_ge(exp_ready, here + 1)
                    nc.vector.tensor_reduce(row_sum[:, :], probs[:, :, :], AX, ALU.add).then_inc(sum_ready, 1)
                    dve.wait_ge(sum_ready, here + 1)
                    nc.vector.reciprocal(row_inv[:, :], row_sum[:, :]).then_inc(inv_ready, 1)
                    dve.wait_ge(inv_ready, here + 1)
                    nc.vector.tensor_scalar(row_scale[:, :], row_inv[:, :], any_key[:, bass.ds(b, 1)], None,
                                            ALU.mult).then_inc(scale_ready, 1)
                if done:
                    db, dt_, n = done
                    dve.wait_ge(attended_full, n + 1)
                    if not (isinstance(n, int) and n < TT):
                        dve.wait_ge(out_stored[dt_], db * 16)
                    nc.vector.tensor_tensor(x2[:, dt_, :], attended[:, :], x1[:, dt_, :], ALU.add).then_inc(x2_ready, 1)
                    dve.wait_ge(x2_ready, n + 1)
                    layernorm_moments(3, x2[:, dt_, :], n)
                if ahead:
                    low(flat(xt2_lo), turn[0][:, :], flat(xt2_hi), xt2_hi_ready, ahead[2] + 1, xt2_ready)
                if last_scored:
                    m_low(b + 1, 3)
                if far:
                    layernorm2_moments(far)
                if done:
                    normalise(3, x2[:, done[1], :], done[2])
                if far:
                    normalise(2, x1[:, far[1], :], far[2])
                if made_tile:
                    _, mt, n = made_tile
                    dve.wait_ge(made_full, n + 1)
                    nc.vector.scalar_tensor_tensor(x2[:, mt, :], made[:, :], gate_scale[:, mt:mt + 1], x2[:, mt, :],
                                                   ALU.mult, ALU.add).then_inc(out_ready, 1)

            dve.wait_ge(small_loaded, 32)
            nc.vector.tensor_copy(mask_f[:, :], mask_u8[:, :]).then_inc(consts_ready, 1)
            dve.wait_ge(consts_ready, 1)
            nc.vector.tensor_scalar(mask_add[:, :, :], mask_f[:, :].rearrange("p (b s) -> p b s", b=B), 1.0, -MASKED,
                                    ALU.subtract, ALU.mult).then_inc(consts_ready, 1)
            nc.vector.tensor_reduce(any_key[:, :], mask_f[:, :].rearrange("p (b s) -> p b s", b=B), AX, ALU.max).then_inc(consts_ready, 1)
            dve.wait_ge(consts_ready, 3)
            for n in range(2):
                layernorm2_moments((0, n, n))
                normalise(2, x1[:, n, :], n)
                if n == 0:
                    low(flat(xt2_lo), turn[0][:, :], flat(xt2_hi), xt2_hi_ready, 1, xt2_ready)
            for h, src in enumerate((m_raw, vw_raw)):
                dve.wait_ge(we_hi_ready, h + 1)
                part = slice(h * KT // 2, (h + 1) * KT // 2)
                nc.vector.tensor_tensor(we_lo[:, part, :], src[:, :].rearrange("p (k w) -> p k w", w=2 * D)[:, 0:KT // 2, :],
                                        raw(we_hi[:, part, :]), ALU.subtract).then_inc(we_lo_ready, 1)
            dve.wait_ge(we_hi_ready, 3)
            nc.vector.tensor_tensor(wg_lo[:, :, :], wg_raw[:, :, :], raw(wg_hi[:, :, :]), ALU.subtract).then_inc(we_lo_ready, 1)
            m_low(0, 1)
            m_low(0, 3)
            run(dve, step)

        @block.tensor
        def _(pe):
            def transpose_tile(bank, src, width, ready, count, full):
                pe.wait_ge(ready, count)
                for k in range(width):
                    last = nc.tensor.transpose(bank[:, k * P:(k + 1) * P], src(k), ident[:, :])
                last.then_inc(full, 1)

            def view_m(m, half, k):
                return m[:, :].rearrange("p (g k w) -> p g k w", g=XG, k=KT)[:, half * HALF:(half + 1) * HALF, k, :]

            def turn_ahead(tile):
                n = tile[2]
                transpose_tile(turn[0], lambda k: ln[2][4][:, k * P:(k + 1) * P], KT, xn_ready[2], n + 1, xt2_full)

            def step(b, t):
                done, gated, made_tile, ahead = (neighbour(b, t, d) for d in (-1, -2, -3, 1))
                here = b * TT + t if is_tile(b) else None
                if done:
                    n = done[2]
                    for half in range(2):
                        if half == 0:
                            pe.wait_ge(xt2_ready, n + 2) if here is not None else None
                        elif made_tile is not None and neighbour(b, t, -4) is not None:
                            pe.wait_ge(ht_ready, n - 2)
                        transpose_tile(turn[half], lambda k: probs[:, :, :].rearrange("p h s -> p (h s)")[:, (half * 4 + k) * P:(half * 4 + k + 1) * P],
                                       4, probs_ready, n + 1, pt_full)
                if here is not None:
                    n = here
                    if t == 0:
                        pe.wait_ge(m_lo_by_pool, (b + 1) * 2)
                        pe.wait_ge(m_lo_by_dve, (b + 1) * 2)
                    pe.wait_ge(xt2_ready, n + 1)
                    if not (isinstance(n, int) and n == 0):
                        pe.wait_ge(shifted, n)
                    for half in range(2):
                        o = score[:, half, :]
                        nc.tensor.matmul(o, row0[:, :], mask_add[:, bass.ds(b, 1), :].to_broadcast([P, XH // 2, S]), start=True, stop=False)
                        for k in range(KT):
                            last = product(nc, o, [x[:, k, :] for x in (xt2_hi, xt2_lo)], [view_m(m, half, k) for m in (m_hi, m_lo)],
                                           False, k == KT - 1)
                    last.then_inc(score_full, 1)
                if gated:
                    if done:
                        pe.wait_ge(pt_ready, done[2] * 2 + 1)
                    transpose_tile(turn[0], lambda k: ln[3][4][:, k * P:(k + 1) * P], KT, xn_ready[3], gated[2] + 1, xt3_full)
                if made_tile:
                    if done:
                        pe.wait_ge(pt_ready, done[2] * 2 + 2)
                    transpose_tile(turn[1], lambda k: hidden[:, k * P:(k + 1) * P], KT, hidden_ready, made_tile[2] + 1, ht_full)
                if done:
                    db, dt_, n = done
                    if dt_ == 0:
                        pe.wait_ge(vw_ready, db + 1)
                    pe.wait_ge(pt_ready, n * 2 + 2)
                    if not (isinstance(n, int) and n == 0):
                        pe.wait_ge(x2_ready, n)
                    for g in range(PAIRS):
                        last = product(nc, attended[:, :], [p[:, g, :] for p in (pt_hi, pt_lo)],
                                       [w[:, g * D:(g + 1) * D] for w in (vw_hi, vw_lo)], g == 0, g == PAIRS - 1)
                    last.then_inc(attended_full, 1)
                if ahead:
                    if gated:
                        pe.wait_ge(xt3_ready, gated[2] + 1)
                    elif done:
                        pe.wait_ge(pt_ready, done[2] * 2 + 1)
                    turn_ahead(ahead)
                if made_tile:
                    n = made_tile[2]
                    pe.wait_ge(ht_ready, n + 1)
                    if not (isinstance(n, int) and n == 0):
                        pe.wait_ge(out_ready, n)
                    for k in range(KT):
                        last = product(nc, made[:, :], [h[:, k, :] for h in (ht_hi, ht_lo)],
                                       [w[:, k, D:2 * D] for w in (we_hi, we_lo)], k == 0, k == KT - 1)
                    last.then_inc(made_full, 1)
                if gated:
                    n = gated[2]
                    pe.wait_ge(xt3_ready, n + 1)
                    if not (isinstance(n, int) and n == 0):
                        pe.wait_ge(hidden_ready, n)
                    for k in range(KT):
                        product(nc, gate[:, 0:E], [x[:, k, :] for x in (xt3_hi, xt3_lo)],
                                [w[:, k, :] for w in (wg_hi, wg_lo)], k == 0, k == KT - 1)
                    for k in range(KT):
                        last = product(nc, hid[:, :], [x[:, k, :] for x in (xt3_hi, xt3_lo)],
                                       [w[:, k, 0:D] for w in (we_hi, we_lo)], k == 0, k == KT - 1)
                    last.then_inc(hid_full, 1)

            pe.wait_ge(consts_pool, 3 + E + 2)
            pe.wait_ge(consts_ready, 3)
            turn_ahead((0, 0, 0))
            pe.wait_ge(we_lo_ready, 3)
            run(pe, step)


def build(nc, x, mask, w_group, ctx_t, w_self, bias_self, bo, w_experts, w_gate, out):
    m_dram = nc.dram_tensor("m_dram", [B, P, XG, KT * 2 * S], F32, kind="Internal").ap()
    vw_dram = nc.dram_tensor("vw_dram", [B, P, XG, D], F32, kind="Internal").ap()
    x1_dram = nc.dram_tensor("x1_dram", [B, T, D], F32, kind="Internal").ap()
    cross_products(nc, w_group, ctx_t, m_dram, vw_dram)
    self_attention(nc, x, w_self, bias_self, bo, x1_dram)
    cross_attention_and_experts(nc, x1_dram, m_dram, vw_dram, mask, w_experts, w_gate, out)


def kernel(x, ctx_1024, mask_BxS2_bf1, L0_attn_Wq, L0_attn_bq, L0_attn_Wk, L0_attn_bk, L0_attn_Wv, L0_attn_bv, L0_attn_Wo,
           L0_attn_bo, L0_xattn_Wq, L0_xattn_Wk, L0_xattn_Wv, L0_xattn_Wo, L0_ffn_A, L0_ffn_Bw, L0_ffn_Wg):
    import numpy as np
    import concourse.bacc as bacc
    from concourse.bass_utils import run_bass_kernel_spmd

    def rows(a):
        return a.reshape(-1, P, a.shape[-1]).transpose(1, 0, 2)

    heads = [np.asarray(w).transpose(1, 0, 2).reshape(D, H * HD) for w in (L0_attn_Wq, L0_attn_Wk, L0_attn_Wv)]
    w_self = rows(np.concatenate(heads + [np.asarray(L0_attn_Wo)], axis=1))
    bias_self = np.stack([np.asarray(v).reshape(QUADS, P).T for v in (L0_attn_bq, L0_attn_bk, L0_attn_bv)], axis=1)
    wk, wv = (np.asarray(w).reshape(CT, P, XG, XD).transpose(2, 1, 0, 3).reshape(XG, P, CT * XD) for w in (L0_xattn_Wk, L0_xattn_Wv))
    wq = np.asarray(L0_xattn_Wq).reshape(D, XG, XH // XG, XD).transpose(1, 3, 2, 0).reshape(XG, P, -1)
    wo = np.asarray(L0_xattn_Wo).reshape(XG, XH // XG, XD, D).transpose(0, 2, 1, 3).reshape(XG, P, -1)
    w_group = np.concatenate([wk, wv, wq, wo], axis=2)
    ctx_t = rows(np.asarray(ctx_1024).reshape(B * S, DC).T)
    w_experts = rows(np.concatenate([np.asarray(L0_ffn_A).reshape(E * R, D).T,
                                     np.asarray(L0_ffn_Bw).transpose(0, 2, 1).reshape(E * R, D)], axis=1))
    w_gate = rows(np.asarray(L0_ffn_Wg).T)
    arrays = {"x": x, "mask": np.asarray(mask_BxS2_bf1).view(np.uint8).reshape(1, B * S), "w_group": w_group, "ctx_t": ctx_t,
              "w_self": w_self, "bias_self": bias_self, "bo": np.asarray(L0_attn_bo).reshape(1, D), "w_experts": w_experts,
              "w_gate": w_gate}
    arrays = {k: np.ascontiguousarray(a) for k, a in arrays.items()}
    nc = bacc.Bacc("TRN2", target_bir_lowering=False, num_devices=1, dynamic_dma_scratch_size=1024)
    aps = {k: nc.dram_tensor(k + "_dram", a.shape, mybir.dt.from_np(a.dtype), kind="ExternalInput").ap() for k, a in arrays.items()}
    out = nc.dram_tensor("out_dram", [B, T, D], F32, kind="ExternalOutput").ap()
    build(nc, out=out, **aps)
    got = run_bass_kernel_spmd(nc, [{k + "_dram": a for k, a in arrays.items()}], core_ids=[0])
    return got.results[0]["out_dram"]
```

```python
import concourse.bass as bass
from concourse import mybir
from concourse.alu_op_type import AluOpType as ALU
from contextlib import ExitStack

F32 = mybir.dt.float32
F32R = mybir.dt.float32r
F16 = mybir.dt.float16
BF16 = mybir.dt.bfloat16
U8 = mybir.dt.uint8
ACT = mybir.ActivationFunctionType
AX = mybir.AxisListType.X

P = 128
B, T, D = 8, 512, 512
TT = T // P
KT = D // P
H, HD = 16, D // 16
QUADS = H * HD // P
HQ = H // QUADS
XH, XG, XD = 16, 8, 128
S = 64
DC = 256
CT = DC // P
E, R = 8, 64
SCALING = 4.0
EPS = 1e-5
MASKED = -1e30



def raw(ap):
    return ap.bitcast(F32)


def product(nc, out, lhs, rhs, start, stop):
    pairs = [(lhs[0], rhs[0]), (lhs[0], rhs[1]), (lhs[1], rhs[0])]
    for n, (a, b) in enumerate(pairs):
        last = nc.tensor.matmul(out, a, b, start=start and n == 0, stop=stop and n == 2)
    return last


def wait_all(engine, *waits):
    values = [v if isinstance(v, int) else engine.snap(v) for _, v in waits]
    for (sem, _), v in zip(waits, values):
        engine.wait_ge(sem, v)


def cross_products(nc, w_group, ctx_t, m_dram, vw_dram, w_self, self_split):
    HH = XH // XG
    BP = B // 2
    KV = 2 * CT * XD
    COLS = KV + 2 * HH * D
    USES, BANKS = 2 + HH * KT + BP * HH, 6
    assert USES % BANKS == 0
    BS = B * S

    with ExitStack() as ctx:
        def sb(name, shape, dt):
            return ctx.enter_context(nc.sbuf_tensor("c_" + name, shape, dt))

        def sem(name):
            return ctx.enter_context(nc.semaphore("c_" + name))

        c_raw = sb("c_raw", [P, CT, BS], F32)
        c_hi, c_lo = (sb(f"c_{n}", [P, CT, BS], F32R) for n in ("hi", "lo"))
        w_raw = sb("w_raw", [P, 2, COLS], F32)
        w_hi, w_lo = (sb(f"w_{n}", [P, 2, COLS], F32R) for n in ("hi", "lo"))
        kv_hi, kv_lo = (sb(f"kv_{n}", [P, 2, 2, BS], F32R) for n in ("hi", "lo"))
        ws_raw = sb("ws_raw", [P, KT, 4 * D], F32)
        ws_hi, ws_lo = self_split
        m_out = sb("m_out", [P, B, KT, HH, S], F32)
        vw_out = sb("vw_out", [P, BP, HH, D], F32)
        bank = [ctx.enter_context(nc.psum_tensor(f"c_bank{n}", [P, 512], F32)) for n in range(BANKS)]

        ctx_loaded, ctx_hi_ready, ctx_lo_ready = sem("ctx_loaded"), sem("ctx_hi"), sem("ctx_lo")
        w_loaded = [sem(f"w{n}_loaded") for n in range(2)]
        w_hi_ready, w_lo_ready = sem("w_hi_ready"), sem("w_lo_ready")
        bank_full = sem("bank_full")
        kv_hi_ready, kv_lo_ready = sem("kv_hi_ready"), sem("kv_lo_ready")
        m_by_act, m_by_dve = sem("m_by_act"), sem("m_by_dve")
        vw_by_act, vw_by_dve = sem("vw_by_act"), sem("vw_by_dve")
        m_stored, vw_stored = sem("m_stored"), sem("vw_stored")
        ws_loaded, ws_hi_ready, ws_lo_ready = sem("ws_loaded"), sem("ws_hi_ready"), sem("ws_lo_ready")

        block = ctx.enter_context(nc.Block())

        def wslice(w, par, kind):
            if kind in "kv":
                at = 0 if kind == "k" else KV // 2
                return w[:, par, at:at + KV // 2].rearrange("p (t d) -> p t d", t=CT)
            at = KV + (HH * D if kind == "o" else 0)
            return w[:, par, at:at + HH * D].rearrange("p (h c) -> p h c", h=HH)

        @block.sync
        def _(sp):
            sp.dma_start(c_raw[:, :, :], ctx_t).then_inc(ctx_loaded, 16)
            sp.dma_start(w_raw[:, 0, :], w_group[0]).then_inc(w_loaded[0], 16)
            sp.dma_start(w_raw[:, 1, :], w_group[1]).then_inc(w_loaded[1], 16)
            sp.dma_start(ws_raw[:, :, :], w_self).then_inc(ws_loaded, 16)

            def store(n, par):
                wait_all(sp, (m_by_act, n * 4 + 4), (m_by_dve, n * 4 + 4))
                sp.dma_start(m_dram[:, :, bass.ds(n, 1), :].rearrange("b p g m -> p b (g m)"),
                             m_out[:, :, :, :, :].rearrange("p b t h s -> p b (t h s)")).then_inc(m_stored, 16)
                wait_all(sp, (vw_by_act, n * 4 + 4), (vw_by_dve, n * 4 + 4))
                rows = vw_dram[:, :, bass.ds(n, 1), :].rearrange("(bp b2) (h s) g e -> b2 h s bp (g e)", b2=2, h=HH)
                for b2 in range(2):
                    for h in range(HH):
                        sp.dma_start(rows[b2, h], vw_out[b2 * S:(b2 + 1) * S, :, h, :]).then_inc(vw_stored, 16)

            sp.sem_inc(m_stored, 16)
            sp.sem_inc(vw_stored, 64)
            with sp.Fori(0, XG // 2 - 1) as i:
                for par in range(2):
                    n = i * 2 + par
                    wait_all(sp, (w_hi_ready, n + 1), (w_lo_ready, n + 1))
                    sp.dma_start(w_raw[:, par, :], w_group[bass.ds(n + 2, 1)].rearrange("g p w -> p (g w)")).then_inc(w_loaded[par], 16)
                    store(n, par)
            for par in range(2):
                store(XG - 2 + par, par)
            sp.wait_ge(m_stored, XG * 16 + 16)
            sp.wait_ge(vw_stored, XG * 64 + 64)

        @block.gpsimd
        def _(pool):
            with pool.Fori(0, XG // 2) as i:
                for par in range(2):
                    pool.wait_ge(w_hi_ready, i * 2 + par + 1)
                    nc.gpsimd.tensor_tensor(w_lo[:, par, :], w_raw[:, par, :], raw(w_hi[:, par, :]),
                                            ALU.subtract).then_inc(w_lo_ready, 1)

        @block.scalar
        def _(act):
            def split_hi(pair, par):
                act.wait_ge(w_loaded[par], pair * 16 + 16)
                nc.scalar.activation(w_hi[:, par, :], w_raw[:, par, :], ACT.Copy).then_inc(w_hi_ready, 1)

            def group(pair, par, more):
                n = pair * 2 + par
                for kv in range(2):
                    act.wait_ge(bank_full, n * USES + kv + 1)
                    nc.scalar.activation(kv_hi[:, par, kv, :], bank[kv][:, :], ACT.Copy,
                                         scale=XD ** -0.5 if kv == 0 else 1.0).then_inc(kv_hi_ready, 1)
                if more:
                    split_hi(pair + par, 1 - par)
                act.wait_ge(m_stored, n * 16 + 16)
                for u in range(2, 2 + HH * KT, 2):
                    h, t = divmod(u - 2, KT)
                    act.wait_ge(bank_full, n * USES + u + 1)
                    nc.scalar.activation(m_out[:, :, t, h, :], bank[u % BANKS][:, :].rearrange("p (b s) -> p b s", b=B),
                                         ACT.Copy).then_inc(m_by_act, 1)
                act.wait_ge(vw_stored, n * 64 + 64)
                for u in range(2 + HH * KT, USES, 2):
                    bp, h = divmod(u - 2 - HH * KT, HH)
                    act.wait_ge(bank_full, n * USES + u + 1)
                    nc.scalar.activation(vw_out[:, bp, h, :], bank[u % BANKS][:, :], ACT.Copy).then_inc(vw_by_act, 1)

            act.wait_ge(ctx_loaded, 16)
            nc.scalar.activation(c_hi[:, :, :], c_raw[:, :, :], ACT.Copy).then_inc(ctx_hi_ready, 1)
            split_hi(0, 0)
            with act.Fori(0, XG // 2 - 1) as i:
                group(i, 0, True)
                group(i, 1, True)

            def split_self(k):
                nc.scalar.activation(ws_hi[:, k, 0:D], ws_raw[:, k, 0:D], ACT.Copy, scale=HD ** -0.5).then_inc(ws_hi_ready, 1)
                nc.scalar.activation(ws_hi[:, k, D:], ws_raw[:, k, D:], ACT.Copy).then_inc(ws_hi_ready, 1)

            act.wait_ge(ws_loaded, 16)
            split_self(0)
            group(XG // 2 - 1, 0, True)
            split_self(1)
            group(XG // 2 - 1, 1, False)
            split_self(2)
            split_self(3)

        @block.vector
        def _(dve):
            dve.wait_ge(ctx_hi_ready, 1)
            nc.vector.tensor_tensor(c_lo[:, :, :], c_raw[:, :, :], raw(c_hi[:, :, :]), ALU.subtract).then_inc(ctx_lo_ready, 1)

            def group(n, par):
                for kv in range(2):
                    dve.wait_ge(kv_hi_ready, n * 2 + kv + 1)
                    nc.vector.scalar_tensor_tensor(kv_lo[:, par, kv, :], bank[kv][:, :], XD ** -0.5 if kv == 0 else 1.0,
                                                   raw(kv_hi[:, par, kv, :]), ALU.mult, ALU.subtract)\
                        .then_inc(kv_lo_ready, 1)
                dve.wait_ge(m_stored, n * 16 + 16)
                for u in range(3, 2 + HH * KT, 2):
                    h, t = divmod(u - 2, KT)
                    dve.wait_ge(bank_full, n * USES + u + 1)
                    nc.vector.tensor_copy(m_out[:, :, t, h, :], bank[u % BANKS][:, :].rearrange("p (b s) -> p b s", b=B))\
                        .then_inc(m_by_dve, 1)
                dve.wait_ge(vw_stored, n * 64 + 64)
                for u in range(3 + HH * KT, USES, 2):
                    bp, h = divmod(u - 2 - HH * KT, HH)
                    dve.wait_ge(bank_full, n * USES + u + 1)
                    nc.vector.tensor_copy(vw_out[:, bp, h, :], bank[u % BANKS][:, :]).then_inc(vw_by_dve, 1)

            def split_self(k):
                dve.wait_ge(ws_hi_ready, 2 * k + 2)
                nc.vector.scalar_tensor_tensor(ws_lo[:, k, 0:D], ws_raw[:, k, 0:D], HD ** -0.5, raw(ws_hi[:, k, 0:D]),
                                               ALU.mult, ALU.subtract).then_inc(ws_lo_ready, 1)
                nc.vector.tensor_tensor(ws_lo[:, k, D:], ws_raw[:, k, D:], raw(ws_hi[:, k, D:]), ALU.subtract).then_inc(ws_lo_ready, 1)

            with dve.Fori(0, XG // 2 - 1) as i:
                for par in range(2):
                    group(i * 2 + par, par)
            split_self(0)
            group(XG - 2, 0)
            split_self(1)
            group(XG - 1, 1)
            split_self(2)
            split_self(3)

        @block.tensor
        def _(pe):
            pe.wait_ge(ctx_lo_ready, 1)

            def group(n, par, first):
                pe.wait_ge(w_lo_ready, n + 1)

                def drained(u):
                    before, m = (u - BANKS, n) if u >= BANKS else (u - BANKS + USES, n - 1)
                    if u < BANKS and first:
                        return
                    if before < 2:
                        pe.wait_ge(kv_lo_ready, m * 2 + before + 1)
                    elif before < 2 + HH * KT:
                        pe.wait_ge((m_by_act, m_by_dve)[before % 2], m * 4 + (before - 2) // 2 + 1)
                    else:
                        pe.wait_ge((vw_by_act, vw_by_dve)[before % 2], m * 4 + (before - 2 - HH * KT) // 2 + 1)

                for kv, kind in enumerate("kv"):
                    drained(kv)
                    for t in range(CT):
                        last = product(nc, bank[kv][:, :], [wslice(w, par, kind)[:, t, :] for w in (w_hi, w_lo)],
                                       [c[:, t, :] for c in (c_hi, c_lo)], t == 0, t == CT - 1)
                    last.then_inc(bank_full, 1)
                pe.wait_ge(kv_lo_ready, n * 2 + 1)
                for u in range(2, 2 + HH * KT):
                    h, t = divmod(u - 2, KT)
                    drained(u)
                    product(nc, bank[u % BANKS][:, :], [wslice(w, par, "q")[:, h, t * P:(t + 1) * P] for w in (w_hi, w_lo)],
                            [k[:, par, 0, :] for k in (kv_hi, kv_lo)], True, True).then_inc(bank_full, 1)
                pe.wait_ge(kv_lo_ready, n * 2 + 2)
                for u in range(2 + HH * KT, USES):
                    bp, h = divmod(u - 2 - HH * KT, HH)
                    drained(u)
                    product(nc, bank[u % BANKS][:, :], [v[:, par, 1, bp * P:(bp + 1) * P] for v in (kv_hi, kv_lo)],
                            [wslice(w, par, "o")[:, h, :] for w in (w_hi, w_lo)], True, True).then_inc(bank_full, 1)

            group(0, 0, True)
            group(1, 1, False)
            with pe.Fori(1, XG // 2) as i:
                group(i * 2, 0, False)
                group(i * 2 + 1, 1, False)


def units_of_batch():
    out = []
    for q in range(QUADS):
        for i in range(TT):
            step = max(1, TT // (i + 1)) if i < 2 else 1
            step = min(step, HQ)
            for j in range(0, HQ, step):
                out.append((q, i, list(range(j, j + step))))
    return out


STEPS = {"xt": 1, "yt": 1, "qk": KT, "v": 2 * KT, "o": KT}


def beside_units(uses):
    units = len(units_of_batch()) // 2
    passes = {"xt": 4, "yt": 4, "qk": 3, "v": 1.5, "o": 3}
    steps = [(kind, n, k) for kind, n in uses for k in range(STEPS[kind])]
    out, done, total = [[] for _ in range(units)], 0, sum(passes[kind] for kind, _, _ in steps)
    unit, completed = 0, -1
    for kind, n, k in steps:
        unit = max(unit, int(done / total * (units - 1)))
        if k == STEPS[kind] - 1:
            unit = max(unit, completed + 1)
            completed = unit
        out[unit].append((kind, n, k))
        done += passes[kind]
    assert not out[-1]
    return out


def self_attention(nc, x, self_split, bias_self, bo, x1_dram):
    UNITS = units_of_batch()
    NU = len(UNITS)
    PQ = NU // QUADS
    HU = NU // 2
    GROUPS = QUADS * TT
    V3 = 3 * HD
    WQ, WK, WV, WO = (n * D for n in range(4))
    ENDS = [q * TT + i if heads[-1] == HQ - 1 else None for q, i, heads in UNITS]

    with ExitStack() as ctx:
        def sb(name, shape, dt):
            return ctx.enter_context(nc.sbuf_tensor("a_" + name, shape, dt))

        def pb(name):
            return ctx.enter_context(nc.psum_tensor("a_" + name, [P, 512], F32))

        def sem(name):
            return ctx.enter_context(nc.semaphore("a_" + name))

        w_hi, w_lo = self_split
        bias = sb("bias", [P, 3, QUADS], F32)
        bias_q = sb("bias_q", [P, QUADS], F32)
        bo_all = sb("bo_all", [P, D], F32)
        ident = sb("ident", [P, P], F32)
        ident_bf = sb("ident_bf", [P, P], BF16)
        causal = sb("causal", [P, P], F32)
        causal_bf = sb("causal_bf", [P, P], BF16)
        minus_half = sb("minus_half", [P, TT], F32)
        x_in = sb("x_in", [P, TT, D], F32)
        x_res = sb("x_res", [P, TT, D], F32)
        stats = sb("stats", [P, TT, 6], F32)
        moments = sb("moments", [P, TT, 2], F32)
        beat = sb("beat", [P, TT], F32)
        var_eps = sb("var_eps", [P, TT], F32)
        rstd = sb("rstd", [P, TT], F32)
        xn = sb("xn", [P, TT, D], F32)
        xt_hi, xt_lo = (sb(f"xt_{n}", [P, KT, T], F32R) for n in ("hi", "lo"))
        yt_hi, yt_lo = (sb(f"yt_{n}", [P, QUADS, T], F32R) for n in ("hi", "lo"))
        qk = [sb(f"qk{n}", [P, 4, T], F32R) for n in range(2)]
        Q_LO, Q_HI, K_HI, K_LO = range(4)
        stack = [sb(f"stack{n}", [3 * HD, 2, HQ, T], F32R) for n in range(2)]
        v_rest = sb("v_rest", [P, 2, D], F32)
        v = sb("v", [P, TT, H, 3, HD], BF16)
        neg_max = sb("neg_max", [P, GROUPS * HQ], F32)
        sums = sb("sums", [P, GROUPS * HQ], F32)
        probs = sb("probs", [P, 2, T], F32)
        pt_hi, pt_lo = (sb(f"pt_{n}", [P, 2, T], F16) for n in ("hi", "lo"))
        y_sum = sb("y_sum", [P, 2, P], F32)
        y_rec = sb("y_rec", [P, 2, HQ], F32)
        y = sb("y", [P, TT, D], F32)
        gemm = [pb(f"gemm{n}") for n in range(2)]
        score = [pb(f"score{n}") for n in range(2)]
        turned = [pb(f"turned{n}") for n in range(2)]
        out_y = [pb(f"out_y{n}") for n in range(2)]

        small_loaded, consts_pool, consts_ready = sem("small_loaded"), sem("consts_pool"), sem("consts_ready")
        x_loaded, x_res_loaded, x_res_ready = sem("x_loaded"), sem("x_res_loaded"), sem("x_res_ready")
        var_ready, rstd_ready, xn_ready = sem("var_ready"), sem("rstd_ready"), sem("xn_ready")
        gemm_full, gemm_drained = sem("gemm_full"), sem("gemm_drained")
        xt_hi_ready = sem("xt_hi_ready")
        qk_hi_ready = sem("qk_hi_ready")
        stacked = [sem(f"stacked{n}") for n in range(2)]
        v1_ready, v2_ready, v_ready = sem("v1_ready"), sem("v2_ready"), sem("v_ready")
        score_full, max_ready, probs_ready = sem("score_full"), sem("max_ready"), sem("probs_ready")
        turned_full, pt_hi_ready, pt_ready = sem("turned_full"), sem("pt_hi_ready"), sem("pt_ready")
        y_full, y_summed, y_ready = sem("y_full"), sem("y_summed"), sem("y_ready")
        yt_hi_ready = sem("yt_hi_ready")
        x1_stored = sem("x1_stored")
        stats_ready, moments_ready = sem("stats_ready"), sem("moments_ready")

        block = ctx.enter_context(nc.Block())

        LATE = ([("xt", k) for k in range(KT)] + [("yt", 0), ("yt", 1), ("qk", 0), ("qk", 1), ("v", 0), ("v", 1),
                                                  ("yt", 2), ("qk", 2), ("qk", 3)])
        EARLY = [("v", 2), ("v", 3), ("yt", 3), ("qk", 4), ("qk", 5)] + [("o", t) for t in range(TT)] + [("qk", 6), ("qk", 7)]
        AHEAD = [("xt", k) for k in range(KT)] + [("qk", 0), ("qk", 1), ("v", 0), ("v", 1), ("qk", 2), ("qk", 3)]
        late, early = beside_units(LATE), beside_units(EARLY)

        def only(steps, wanted):
            return [[step for step in unit if wanted(step[0])] for unit in steps]

        BESIDE = {"first": only(early, lambda kind: kind not in ("yt", "o")), "late": late, "early": early,
                  "last": only(late, lambda kind: kind == "yt")}

        def completed(steps):
            return [(kind, n) for unit in steps for kind, n, k in unit if k == STEPS[kind] - 1]

        USES = {"first": AHEAD + completed(BESIDE["first"]), "loop": completed(late) + completed(early),
                "last": completed(BESIDE["last"]) + [("yt", 3)] + [("o", t) for t in range(TT)]}
        FIRST, G_ALL = len(USES["first"]), len(USES["loop"])
        assert G_ALL % 2 == 0 and FIRST % 2 == 0
        for steps in (late, early):
            ends = [m for m, unit in enumerate(steps) for kind, n, k in unit if kind == "qk" and n % 2 and k == KT - 1]
            assert all(m + 1 + 2 >= (j + 1) * PQ - 1 for j, m in enumerate(ends))

        def use_of(it, kind, n):
            table = "first" if it is None else "last" if isinstance(it, int) and it == B - 1 else "loop"
            u = USES[table].index((kind, n))
            return (u if it is None else it * G_ALL + FIRST + u), gemm[u % 2]

        def drained(use):
            return use + 3

        def values(u, part):
            half, pair = divmod(u, 2)
            return v[:, pair * 2:pair * 2 + 2, half * H // 2:(half + 1) * H // 2, part, :]

        def rest(u):
            return v_rest[:, u % 2, :].rearrange("p (t h d) -> p t h d", t=2, d=HD)

        def next_batch(it):
            return 0 if it is None else it + 1

        def unit_at(b, n):
            d = -1 if n < 0 else n // NU
            if isinstance(b, int) and not 0 <= b + d < B:
                return None
            return b + d, n - d * NU

        def halves(engine, half):
            half(0, 0, None, BESIDE["first"], True)
            with engine.Fori(0, B - 2) as b:
                half(b, HU, b, BESIDE["late"], True)
                half(b + 1, 0, b, BESIDE["early"], True)
            half(B - 2, HU, B - 2, BESIDE["late"], False)
            half(B - 1, 0, B - 2, BESIDE["early"], False)
            half(B - 1, HU, B - 1, BESIDE["last"], False)

        STACK_DMAS = 16 * 3 * HQ
        @block.sync
        def _(sp):
            def load_x(b):
                sp.dma_start(x_in[:, :, :], x[bass.ds(b, 1)].rearrange("b (t p) c -> p (b t) c", p=P)).then_inc(x_loaded, 16)

            def stack_quad(b, q, it):
                sp.wait_ge(gemm_drained, drained(use_of(it, "qk", 2 * q + 1)[0]))
                st = stack[q % 2]
                for j in range(HQ):
                    rows = slice(j * HD, (j + 1) * HD)
                    for r, (of_q, of_k) in enumerate([(Q_HI, K_HI), (Q_HI, K_LO), (Q_LO, K_HI)]):
                        sp.dma_start(raw(st[r * HD:(r + 1) * HD, :, j, :]),
                                     raw(qk[q % 2][rows, of_q:of_k + 1:of_k - of_q, :])).then_inc(stacked[q % 2], 16)

            def store_x1(it):
                for t in range(TT):
                    sp.wait_ge(gemm_drained, drained(use_of(it, "o", t)[0]))
                    sp.dma_start(x1_dram[bass.ds(it, 1), t * P:(t + 1) * P, :].rearrange("b p c -> p (b c)"),
                                 x_res[:, t, :]).then_inc(x1_stored, 16)

            def half(b, n0, it, beside, more):
                if n0:
                    if more:
                        sp.wait_ge(xn_ready, (b + 2) * TT)
                        load_x(b + 2)
                    sp.wait_ge(x1_stored, b * TT * 16 + 16)
                    sp.dma_start(x_res[:, :, :], x[bass.ds(b, 1)].rearrange("b (t p) c -> p (b t) c", p=P)).then_inc(x_res_loaded, 16)
                    if not (isinstance(b, int) and b == B - 1):
                        stack_quad(b + 1, 0, it)
                        stack_quad(b + 1, 1, it)
                else:
                    stack_quad(b, 2, it)
                    if it is not None:
                        store_x1(it)
                    stack_quad(b, 3, it)

            load_x(0)
            sp.dma_start(bias[:, :, :], bias_self).then_inc(small_loaded, 16)
            sp.dma_start(bo_all[:, :], bo.to_broadcast([P, D])).then_inc(small_loaded, 16)
            sp.sem_inc(x1_stored, 16)
            sp.wait_ge(xn_ready, TT)
            load_x(1)
            stack_quad(0, 0, None)
            stack_quad(0, 1, None)
            halves(sp, half)
            store_x1(B - 1)
            sp.wait_ge(x1_stored, B * TT * 16 + 16)

        @block.gpsimd
        def _(pool):
            nc.gpsimd.memset(ident[:, :], 0.0).then_inc(consts_pool, 1)
            nc.gpsimd.memset(causal[:, :], 0.0).then_inc(consts_pool, 1)
            nc.gpsimd.memset(minus_half[:, :], -0.5).then_inc(consts_pool, 1)
            pool.wait_ge(consts_pool, 3)
            nc.gpsimd.affine_select(out=ident[:, :], in_=ident[:, :], compare_op=ALU.not_equal, fill=1.0,
                                    base=0, pattern=[[-1, P]], channel_multiplier=1).then_inc(consts_pool, 1)
            nc.gpsimd.affine_select(out=causal[:, :], in_=causal[:, :], compare_op=ALU.is_ge, fill=MASKED,
                                    base=0, pattern=[[-1, P]], channel_multiplier=1).then_inc(consts_pool, 1)
            pool.wait_ge(small_loaded, 32)

            def reciprocal_deviation(b):
                pool.wait_ge(var_ready, b + 1)
                nc.gpsimd.tensor_tensor(rstd[:, :], var_eps[:, :], minus_half[:, :], ALU.pow).then_inc(rstd_ready, 1)

            def values_third(b, u):
                pool.wait_ge(v2_ready, b * 4 + u + 1)
                nc.gpsimd.tensor_tensor(values(u, 2), rest(u), values(u, 1), ALU.subtract).then_inc(v_ready, 1)

            def half(b, n0, it, beside, more):
                g0 = GROUPS // 2 if n0 else 0
                for g in range(g0, g0 + GROUPS // 2):
                    q, i = divmod(g, TT)
                    pool.wait_ge(y_summed, b * GROUPS + g + 1)
                    nc.gpsimd.tensor_tensor(y[:, i, q * P:(q + 1) * P].rearrange("p (h d) -> p h d", h=HQ),
                                            y_sum[:, g % 2, :].rearrange("p (h d) -> p h d", h=HQ),
                                            y_rec[:, g % 2, :].unsqueeze(2).to_broadcast([P, HQ, HD]),
                                            ALU.mult).then_inc(y_ready, 1)
                    if g == 1:
                        values_third(b, 2)
                        values_third(b, 3)
                    if g == 2 and more:
                        reciprocal_deviation(b + 1)
                    if g == 2 * TT + 2:
                        pool.wait_ge(x_res_loaded, b * 16 + 16)
                        nc.gpsimd.tensor_tensor(x_res[:, :, :], x_res[:, :, :], bo_all[:, :].unsqueeze(1).to_broadcast([P, TT, D]),
                                                ALU.add).then_inc(x_res_ready, 1)
                    if g in (3 * TT + 1, 3 * TT + 2) and not (isinstance(b, int) and b == B - 1):
                        values_third(b + 1, g - 3 * TT - 1)

            reciprocal_deviation(0)
            values_third(0, 0)
            values_third(0, 1)
            halves(pool, half)

        @block.scalar
        def _(act):
            act.wait_ge(consts_ready, 3)

            def high_part(it, kind, n):
                use, bank = use_of(it, kind, n)
                act.wait_ge(gemm_full, use + 1)
                if kind == "xt":
                    nc.scalar.activation(xt_hi[:, n, :], bank[:, :], ACT.Copy).then_inc(xt_hi_ready, 1)
                elif kind == "yt":
                    nc.scalar.activation(yt_hi[:, n, :], bank[:, :], ACT.Identity, bias=bias[:, 2, n:n + 1]).then_inc(yt_hi_ready, 1)
                elif kind == "qk":
                    q, part = divmod(n, 2)
                    b = next_batch(it)
                    if part == 0 and not (it is None and q < 2):
                        act.wait_ge(stacked[q % 2], (b * 2 + q // 2) * STACK_DMAS)
                    nc.scalar.activation(qk[q % 2][:, (Q_HI, K_HI)[part], :], bank[:, :], ACT.Identity,
                                         bias=bias_q[:, q:q + 1] if part == 0 else bias[:, 1, q:q + 1]).then_inc(qk_hi_ready, 1)
                elif kind == "v":
                    nc.scalar.activation(values(n, 0), bank[:, :].rearrange("p (t h d) -> p t h d", t=2, d=HD),
                                         ACT.Copy).then_inc(v1_ready, 1)

            def values_second(it, n):
                act.wait_ge(gemm_drained, drained(use_of(it, "v", n)[0]))
                nc.scalar.activation(values(n, 1), rest(n), ACT.Copy).then_inc(v2_ready, 1)

            def exps(b, n):
                q, i, heads = UNITS[n]
                width = (i + 1) * P
                act.wait_ge(max_ready, b * NU + n + 1)
                for k, j in enumerate(heads):
                    c = (q * TT + i) * HQ + j
                    ins = nc.scalar.activation(probs[:, n % 2, k * width:(k + 1) * width],
                                               score[n % 2][:, k * width:(k + 1) * width], ACT.Exp,
                                               bias=neg_max[:, c:c + 1], accum_out=sums[:, c:c + 1])
                ins.then_inc(probs_ready, 1)

            def probs_hi(b, n):
                q, i, heads = UNITS[n]
                width = (i + 1) * P * len(heads)
                act.wait_ge(turned_full, b * NU + n + 1)
                nc.scalar.activation(pt_hi[:, n % 2, 0:width], turned[n % 2][:, 0:width], ACT.Copy).then_inc(pt_hi_ready, 1)

            def half(b, n0, it, beside, more):
                for m in range(HU):
                    exps(b, n0 + m)
                    if unit_at(b, n0 + m - 1):
                        probs_hi(*unit_at(b, n0 + m - 1))
                    for kind, n in completed(beside[max(0, m - 1):m]):
                        high_part(it, kind, n)
                    for kind, n in completed(beside[max(0, m - 2):max(0, m - 1)]):
                        if kind == "v":
                            values_second(it, n)

            for kind, n in AHEAD:
                high_part(None, kind, n)
                if kind == "v":
                    values_second(None, n)
            halves(act, half)
            probs_hi(B - 1, NU - 1)
            high_part(B - 1, "yt", 3)

        @block.vector
        def _(dve):
            dve.sem_inc(gemm_drained, 2)
            dve.wait_ge(consts_pool, 5)
            nc.vector.tensor_copy(ident_bf[:, :], ident[:, :]).then_inc(consts_ready, 1)
            nc.vector.tensor_copy(causal_bf[:, :], causal[:, :]).then_inc(consts_ready, 1)
            dve.wait_ge(small_loaded, 32)
            nc.vector.tensor_scalar(bias_q[:, :], bias[:, 0, :], HD ** -0.5, None, ALU.mult).then_inc(consts_ready, 1)
            dve.wait_ge(consts_ready, 3)

            def ln_stats(b, t):
                dve.wait_ge(x_loaded, b * 16 + 16)
                nc.vector.bn_stats(stats[:, t, :], x_in[:, t, :]).then_inc(stats_ready, 1)

            def ln_moments(b, t):
                dve.wait_ge(stats_ready, b * TT + t + 1)
                nc.vector.memset(beat[:, t:t + 1], 0.0).then_inc(moments_ready, 1)
                nc.vector.bn_aggr(moments[:, t, :], stats[:, t, :]).then_inc(moments_ready, 1)

            def ln_variance(b):
                dve.wait_ge(moments_ready, 2 * (b * TT + TT))
                nc.vector.tensor_scalar(var_eps[:, :], moments[:, :, 1], EPS, None, ALU.add).then_inc(var_ready, 1)

            def ln_normalise(b, t):
                dve.wait_ge(rstd_ready, b + 1)
                nc.vector.tensor_scalar(xn[:, t, :], x_in[:, t, :], moments[:, t, 0:1], rstd[:, t:t + 1],
                                        ALU.subtract, ALU.mult).then_inc(xn_ready, 1)

            def low_part(it, kind, n):
                use, bank = use_of(it, kind, n)
                b = next_batch(it)
                if kind == "xt":
                    dve.wait_ge(xt_hi_ready, b * KT + n + 1)
                    ins = nc.vector.tensor_tensor(xt_lo[:, n, :], bank[:, :], raw(xt_hi[:, n, :]), ALU.subtract)
                elif kind == "yt":
                    dve.wait_ge(yt_hi_ready, it * QUADS + n + 1)
                    ins = nc.vector.scalar_tensor_tensor(yt_lo[:, n, :], bank[:, :], bias[:, 2, n:n + 1], raw(yt_hi[:, n, :]),
                                                         ALU.add, ALU.subtract)
                elif kind == "qk":
                    q, part = divmod(n, 2)
                    dve.wait_ge(qk_hi_ready, (b * QUADS + q) * 2 + part + 1)
                    ins = nc.vector.scalar_tensor_tensor(qk[q % 2][:, (Q_LO, K_LO)[part], :], bank[:, :],
                                                         bias_q[:, q:q + 1] if part == 0 else bias[:, 1, q:q + 1],
                                                         raw(qk[q % 2][:, (Q_HI, K_HI)[part], :]), ALU.add, ALU.subtract)
                elif kind == "v":
                    dve.wait_ge(v1_ready, b * 4 + n + 1)
                    if not (it is None and n < 2):
                        dve.wait_ge(v_ready, b * 4 + n - 1)
                    ins = nc.vector.tensor_tensor(rest(n), bank[:, :].rearrange("p (t h d) -> p t h d", t=2, d=HD),
                                                  values(n, 0), ALU.subtract)
                else:
                    if n == 0:
                        dve.wait_ge(x_res_ready, it + 1)
                    dve.wait_ge(gemm_full, use + 1)
                    ins = nc.vector.tensor_tensor(x_res[:, n, :], bank[:, :], x_res[:, n, :], ALU.add)
                ins.then_inc(gemm_drained, 1)

            def row_max(b, n):
                q, i, heads = UNITS[n]
                width, k = (i + 1) * P, len(heads)
                c = (q * TT + i) * HQ + heads[0]
                dve.wait_ge(score_full, b * NU + n + 1)
                nc.vector.tensor_reduce(neg_max[:, c:c + k], score[n % 2][:, 0:k * width].rearrange("p (h s) -> p h s", h=k),
                                        AX, ALU.max, negate=True).then_inc(max_ready, 1)

            def probs_lo(b, n):
                q, i, heads = UNITS[n]
                width = (i + 1) * P * len(heads)
                dve.wait_ge(pt_hi_ready, b * NU + n + 1)
                nc.vector.tensor_tensor(pt_lo[:, n % 2, 0:width], turned[n % 2][:, 0:width], pt_hi[:, n % 2, 0:width],
                                        ALU.subtract).then_inc(pt_ready, 1)

            def outputs(b, n):
                g = ENDS[n]
                if g is None:
                    return
                dve.wait_ge(y_full, b * GROUPS + g + 1)
                if not (isinstance(b, int) and b == 0 and g < 2):
                    dve.wait_ge(y_ready, b * GROUPS + g - 1)
                nc.vector.reciprocal(y_rec[:, g % 2, :], sums[:, g * HQ:(g + 1) * HQ])
                nc.vector.tensor_reduce(y_sum[:, g % 2, :].rearrange("p (h d) -> p h d", h=HQ),
                                        out_y[g % 2][:, 0:HQ * V3].rearrange("p (h k d) -> p h d k", h=HQ, k=3),
                                        AX, ALU.add).then_inc(y_summed, 1)

            def half(b, n0, it, beside, more):
                for m in range(HU):
                    if unit_at(b, n0 + m + 2):
                        row_max(*unit_at(b, n0 + m + 2))
                    if unit_at(b, n0 + m - 2):
                        outputs(*unit_at(b, n0 + m - 2))
                    for kind, n in completed(beside[max(0, m - 1):m]):
                        low_part(it, kind, n)
                    probs_lo(b, n0 + m)
                    if n0 == 0 and more:
                        if TT <= m < 2 * TT:
                            ln_stats(b + 1, m - TT)
                        if TT < m <= 2 * TT:
                            ln_moments(b + 1, m - 1 - TT)
                        if m == 2 * TT + 1:
                            ln_variance(b + 1)
                        if m >= HU - TT:
                            ln_normalise(b + 1, m - (HU - TT))

            for t in range(TT):
                ln_stats(0, t)
            for t in range(TT):
                ln_moments(0, t)
            ln_variance(0)
            for t in range(TT):
                ln_normalise(0, t)
            for use in AHEAD:
                low_part(None, *use)
            row_max(0, 0)
            row_max(0, 1)
            halves(dve, half)
            for n in (NU - 2, NU - 1):
                outputs(B - 1, n)
            low_part(B - 1, "yt", 3)
            for t in range(TT):
                low_part(B - 1, "o", t)

        @block.tensor
        def _(pe):
            pe.wait_ge(consts_ready, 3)

            def step_of_product(it, kind, n, k):
                use, out = use_of(it, kind, n)
                if k == 0:
                    if kind == "xt":
                        pe.wait_ge(xn_ready, (next_batch(it) + 1) * TT)
                    if kind == "yt":
                        pe.wait_ge(y_ready, it * GROUPS + (n + 1) * TT)
                    if (kind, n) == ("o", 0):
                        pe.wait_ge(gemm_drained, drained(use_of(it, "yt", QUADS - 1)[0]))
                    pe.wait_ge(gemm_drained, drained(use - 2))
                if kind in ("xt", "yt"):
                    for t in range(TT):
                        last = nc.tensor.transpose(out[:, t * P:(t + 1) * P], (xn if kind == "xt" else y)[:, t, n * P:(n + 1) * P],
                                                   ident[:, :])
                elif kind == "qk":
                    if n == 0:
                        pe.wait_ge(gemm_drained, drained(use_of(it, "xt", k)[0]))
                    col = (WQ, WK)[n % 2] + n // 2 * P
                    last = product(nc, out[:, :], [w[:, k, col:col + P] for w in (w_hi, w_lo)],
                                   [xt[:, k, :] for xt in (xt_hi, xt_lo)], k == 0, k == KT - 1)
                elif kind == "v":
                    half, pair = divmod(n, 2)
                    t, k4 = divmod(k, KT)
                    col, tok = WV + half * D // 2, (pair * 2 + t) * P
                    last = product(nc, out[:, t * D // 2:(t + 1) * D // 2], [xt[:, k4, tok:tok + P] for xt in (xt_hi, xt_lo)],
                                   [w[:, k4, col:col + D // 2] for w in (w_hi, w_lo)], k4 == 0, k4 == KT - 1)
                else:
                    last = product(nc, out[:, :], [yt[:, k, n * P:(n + 1) * P] for yt in (yt_hi, yt_lo)],
                                   [w[:, k, WO:WO + D] for w in (w_hi, w_lo)], k == 0, k == KT - 1)
                if k == STEPS[kind] - 1:
                    last.then_inc(gemm_full, 1)

            def whole_product(it, kind, n):
                for k in range(STEPS[kind]):
                    step_of_product(it, kind, n, k)

            def scores(b, n):
                q, i, heads = UNITS[n]
                if n % PQ == 0:
                    pe.wait_ge(stacked[q % 2], (b * 2 + q // 2 + 1) * STACK_DMAS)
                width = (i + 1) * P
                st = stack[q % 2]
                for k, j in enumerate(heads):
                    at = k * width
                    nc.tensor.matmul(score[n % 2][:, at:at + width], st[:, 0, j, i * P:(i + 1) * P], st[:, 1, j, 0:width],
                                     start=True, stop=False)
                    last = nc.tensor.matmul(score[n % 2][:, at + i * P:at + width], ident_bf[:, :], causal_bf[:, :],
                                            start=False, stop=True)
                last.then_inc(score_full, 1)

            def turn(b, n):
                q, i, heads = UNITS[n]
                pe.wait_ge(probs_ready, b * NU + n + 1)
                for c in range((i + 1) * len(heads)):
                    last = nc.tensor.transpose(turned[n % 2][:, c * P:(c + 1) * P], probs[:, n % 2, c * P:(c + 1) * P],
                                               ident[:, :])
                last.then_inc(turned_full, 1)

            def weigh(b, n):
                q, i, heads = UNITS[n]
                g = q * TT + i
                pe.wait_ge(pt_ready, b * NU + n + 1)
                if heads[0] == 0:
                    if not (isinstance(b, int) and b == 0 and g < 2):
                        pe.wait_ge(y_summed, b * GROUPS + g - 1)
                    if q % 2 == 0 and i % 2 == 0:
                        pe.wait_ge(v_ready, b * 4 + q + i // 2 + 1)
                for k, j in enumerate(heads):
                    at = j * V3
                    for s in range(i + 1):
                        c = (k * (i + 1) + s) * P
                        val = v[:, s, q * HQ + j, :, :].rearrange("p k d -> p (k d)")
                        nc.tensor.matmul(out_y[g % 2][:, at:at + V3], pt_hi[:, n % 2, c:c + P], val,
                                         start=s == 0, stop=False)
                        last = nc.tensor.matmul(out_y[g % 2][:, at:at + 2 * HD], pt_lo[:, n % 2, c:c + P], val[:, 0:2 * HD],
                                                start=False, stop=s == i)
                if ENDS[n] is not None:
                    last.then_inc(y_full, 1)

            def half(b, n0, it, beside, more):
                for m in range(HU):
                    turn(b, n0 + m)
                    if unit_at(b, n0 + m + 2):
                        scores(*unit_at(b, n0 + m + 2))
                    for step in beside[m]:
                        step_of_product(it, *step)
                    if unit_at(b, n0 + m - 1):
                        weigh(*unit_at(b, n0 + m - 1))

            for use in AHEAD:
                whole_product(None, *use)
            scores(0, 0)
            scores(0, 1)
            halves(pe, half)
            weigh(B - 1, NU - 1)
            whole_product(B - 1, "yt", 3)
            for t in range(TT):
                whole_product(B - 1, "o", t)


def cross_attention_and_experts(nc, x1_dram, m_dram, vw_dram, mask, w_experts, w_gate, out):
    HS = XH * S
    HALF = XG // 2
    PAIRS = HS // P
    MW = XG * KT * 2 * S
    assert MW == XG * D

    def neighbour(b, t, d):
        bb, tt = b + (t + d) // TT, (t + d) % TT
        if isinstance(b, int) and not 0 <= bb < B:
            return None
        return bb, tt, bb * TT + tt

    with ExitStack() as ctx:
        def sb(name, shape, dt):
            return ctx.enter_context(nc.sbuf_tensor("b_" + name, shape, dt))

        def pb(name, shape=(P, 512)):
            return ctx.enter_context(nc.psum_tensor("b_" + name, list(shape), F32))

        def sem(name):
            return ctx.enter_context(nc.semaphore("b_" + name))

        m_raw = sb("m_raw", [P, MW], F32)
        vw_raw = sb("vw_raw", [P, MW], F32)
        m_hi, m_lo = (sb(f"m_{n}", [P, MW], F32R) for n in ("hi", "lo"))
        vw_hi, vw_lo = (sb(f"vw_{n}", [P, MW], F32R) for n in ("hi", "lo"))
        we_hi, we_lo = (sb(f"we_{n}", [P, KT, 2 * D], F32R) for n in ("hi", "lo"))
        wg_raw = sb("wg_raw", [P, KT, E], F32)
        wg_hi, wg_lo = (sb(f"wg_{n}", [P, KT, E], F32R) for n in ("hi", "lo"))
        ident = sb("ident", [P, P], F32)
        minus_half = sb("minus_half", [P, 1], F32)
        order = sb("order", [P, E], F32)
        row0 = sb("row0", [P, P], BF16)
        mask_u8 = sb("mask_u8", [P, B * S], U8)
        mask_f = sb("mask_f", [P, B * S], F32)
        mask_add = sb("mask_add", [P, B, S], BF16)
        any_key = sb("any_key", [P, B], F32)
        x1 = sb("x1", [P, TT, D], F32)
        x2 = sb("x2", [P, TT, D], F32)
        beat = sb("beat", [P, 1], F32)
        ln = {k: (sb(f"stats{k}", [P, 6], F32), sb(f"moments{k}", [P, 2], F32), sb(f"var{k}", [P, 1], F32),
                  sb(f"rstd{k}", [P, 1], F32), sb(f"xn{k}", [P, D], F32)) for k in (2, 3)}
        xt2_hi, xt2_lo = (sb(f"xt2_{n}", [P, KT, P], F32R) for n in ("hi", "lo"))
        xt3_hi, xt3_lo = (sb(f"xt3_{n}", [P, KT, P], F32R) for n in ("hi", "lo"))
        row_max = sb("row_max", [P, XH], F32)
        row_sum = sb("row_sum", [P, XH], F32)
        row_inv = sb("row_inv", [P, XH], F32)
        row_scale = sb("row_scale", [P, XH], F32)
        probs = sb("probs", [P, XH, S], F32)
        pt_hi, pt_lo = (sb(f"pt_{n}", [P, PAIRS, P], F32R) for n in ("hi", "lo"))
        gate_negmax = sb("gate_negmax", [P, 1], F32)
        gate_exp = sb("gate_exp", [P, E], F32)
        gate_sum = sb("gate_sum", [P, 1], F32)
        gate_top = sb("gate_top", [P, 1], F32)
        gate_rank = sb("gate_rank", [P, E], F32)
        gate_best = sb("gate_best", [P, 1], F32)
        gate_one = sb("gate_one", [P, E], F32)
        gate_inv = sb("gate_inv", [P, 1], F32)
        gate_scale = sb("gate_scale", [P, TT], F32)
        hidden = sb("hidden", [P, D], F32)
        ht_hi, ht_lo = (sb(f"ht_{n}", [P, KT, P], F32R) for n in ("hi", "lo"))
        turn = [pb(f"turn{n}") for n in range(2)]
        score = pb("score", (P, 2, 512))
        attended, hid, made, gate = pb("attended"), pb("hid"), pb("made"), pb("gate")

        we_loaded = [sem(f"we{n}_loaded") for n in range(2)]
        we_hi_ready, we_lo_ready = sem("we_hi_ready"), sem("we_lo_ready")
        small_loaded, consts_pool, consts_ready = sem("small_loaded"), sem("consts_pool"), sem("consts_ready")
        m_loaded, m_hi_ready = sem("m_loaded"), sem("m_hi_ready")
        M_CHUNKS = 4
        MC = MW // M_CHUNKS
        m_lo_by_pool, m_lo_by_dve = sem("m_lo_by_pool"), sem("m_lo_by_dve")
        vw_loaded, vw_hi_ready, vw_ready = sem("vw_loaded"), sem("vw_hi_ready"), sem("vw_ready")
        x1_loaded, out_stored = ([sem(f"{n}{t}") for t in range(TT)] for n in ("x1_loaded", "out_stored"))
        stats_ready = {k: sem(f"stats{k}_ready") for k in (2, 3)}
        moments_ready = {k: sem(f"moments{k}_ready") for k in (2, 3)}
        var_ready = {k: sem(f"var{k}_ready") for k in (2, 3)}
        rstd_ready = {k: sem(f"rstd{k}_ready") for k in (2, 3)}
        xn_ready = {k: sem(f"xn{k}_ready") for k in (2, 3)}
        xt2_full, xt2_hi_ready, xt2_ready = sem("xt2_full"), sem("xt2_hi_ready"), sem("xt2_ready")
        xt3_full, xt3_hi_ready, xt3_ready = sem("xt3_full"), sem("xt3_hi_ready"), sem("xt3_ready")
        ht_full, ht_hi_ready, ht_ready = sem("ht_full"), sem("ht_hi_ready"), sem("ht_ready")
        pt_full, pt_hi_ready, pt_ready = sem("pt_full"), sem("pt_hi_ready"), sem("pt_ready")
        score_full, max_ready, shifted, exp_ready = sem("score_full"), sem("max_ready"), sem("shifted"), sem("exp_ready")
        sum_ready, inv_ready, scale_ready, probs_ready = sem("sum_ready"), sem("inv_ready"), sem("scale_ready"), sem("probs_ready")
        attended_full, x2_ready = sem("attended_full"), sem("x2_ready")
        hid_full, hidden_ready = sem("hid_full"), sem("hidden_ready")
        gate_max_ready, gate_exp_ready, gate_step = sem("gate_max_ready"), sem("gate_exp_ready"), sem("gate_step")
        GATE_STEPS = 5
        made_full, out_ready = sem("made_full"), sem("out_ready")

        block = ctx.enter_context(nc.Block())

        def run(engine, step, before=None):
            for t in range(TT):
                step(0, t)
            with engine.Fori(1, B - 1) as b:
                for t in range(TT):
                    step(b, t)
            for t in range(TT):
                step(B - 1, t)
            for t in range(3):
                step(B, t)

        def is_tile(b):
            return not (isinstance(b, int) and b >= B)

        @block.sync
        def _(sp):
            def load_x1(tile):
                b, t, _ = tile
                sp.dma_start(x1[:, t, :], x1_dram[bass.ds(b, 1), t * P:(t + 1) * P, :].rearrange("b p c -> p (b c)")).then_inc(x1_loaded[t], 16)

            def load_m(b):
                sp.dma_start(m_raw[:, :], m_dram[bass.ds(b, 1)].rearrange("b p g m -> p (b g m)")).then_inc(m_loaded, 16)

            def load_vw(b):
                sp.dma_start(vw_raw[:, :], vw_dram[bass.ds(b, 1)].rearrange("b p g m -> p (b g m)")).then_inc(vw_loaded, 16)

            def step(b, t):
                done, ahead, made_tile = neighbour(b, t, -1), neighbour(b, t, 3), neighbour(b, t, -3)
                if ahead and done:
                    sp.wait_ge(x2_ready, done[2] + 1)
                    load_x1(ahead)
                if t == 0 and is_tile(b) and is_tile(b + 1):
                    wait_all(sp, (m_lo_by_pool, (b + 1) * 2), (m_lo_by_dve, (b + 1) * 2))
                    load_m(b + 1)
                if t == 1 and is_tile(b) and is_tile(b + 1):
                    sp.wait_ge(vw_ready, b + 1)
                    load_vw(b + 1)
                if made_tile:
                    _, mt, n = made_tile
                    sp.wait_ge(out_ready, n + 1)
                    sp.dma_start(out.rearrange("b (t p) c -> (b t) p c", p=P)[bass.ds(n, 1)].rearrange("n p c -> p (n c)"),
                                 x2[:, mt, :]).then_inc(out_stored[mt], 16)

            for k in range(KT):
                load_x1((0, k, k))
            half = KT // 2
            sp.dma_start(m_raw[:, :].rearrange("p (k w) -> p k w", w=2 * D)[:, 0:half, :], w_experts[:, 0:half, :]).then_inc(we_loaded[0], 16)
            sp.dma_start(vw_raw[:, :].rearrange("p (k w) -> p k w", w=2 * D)[:, 0:half, :], w_experts[:, half:, :]).then_inc(we_loaded[1], 16)
            sp.dma_start(wg_raw[:, :, :], w_gate).then_inc(small_loaded, 16)
            sp.dma_start(mask_u8[:, :], mask.to_broadcast([P, B * S])).then_inc(small_loaded, 16)
            sp.wait_ge(we_lo_ready, 3)
            load_m(0)
            load_vw(0)
            run(sp, step)
            for t in range(TT):
                sp.wait_ge(out_stored[t], B * 16)

        @block.gpsimd
        def _(pool):
            def deviation(k, n):
                pool.wait_ge(var_ready[k], n + 1)
                nc.gpsimd.tensor_tensor(ln[k][3][:, :], ln[k][2][:, :], minus_half[:, :], ALU.pow).then_inc(rstd_ready[k], 1)

            def m_low(b, c):
                part = slice(c * MC, (c + 1) * MC)
                pool.wait_ge(m_hi_ready, b * M_CHUNKS + c + 1)
                nc.gpsimd.tensor_tensor(m_lo[:, part], m_raw[:, part], raw(m_hi[:, part]), ALU.subtract).then_inc(m_lo_by_pool, 1)

            def vw_low(b):
                pool.wait_ge(vw_hi_ready, b + 1)
                nc.gpsimd.tensor_tensor(vw_lo[:, :], vw_raw[:, :], raw(vw_hi[:, :]), ALU.subtract).then_inc(vw_ready, 1)

            def step(b, t):
                done, ahead = neighbour(b, t, -1), neighbour(b, t, 2)
                last_scored = t == TT - 1 and is_tile(b) and is_tile(b + 1)
                if last_scored:
                    m_low(b + 1, 0)
                if is_tile(b):
                    n = b * TT + t
                    pool.wait_ge(scale_ready, n + 1)
                    nc.gpsimd.tensor_tensor(probs[:, :, :], probs[:, :, :], row_scale[:, :].unsqueeze(2).to_broadcast([P, XH, S]),
                                            ALU.mult).then_inc(probs_ready, 1)
                if last_scored:
                    m_low(b + 1, 2)
                if done:
                    deviation(3, done[2])
                if ahead:
                    deviation(2, ahead[2])
                if t == 0 and is_tile(b) and not (isinstance(b, int) and b == 0):
                    vw_low(b)

            nc.gpsimd.memset(ident[:, :], 0.0).then_inc(consts_pool, 1)
            nc.gpsimd.memset(minus_half[:, :], -0.5).then_inc(consts_pool, 1)
            nc.gpsimd.memset(row0[:, :], 0.0).then_inc(consts_pool, 1)
            for e in range(E):
                nc.gpsimd.memset(order[:, e:e + 1], float(E - e)).then_inc(consts_pool, 1)
            pool.wait_ge(consts_pool, 3 + E)
            nc.gpsimd.affine_select(out=ident[:, :], in_=ident[:, :], compare_op=ALU.not_equal, fill=1.0,
                                    base=0, pattern=[[-1, P]], channel_multiplier=1).then_inc(consts_pool, 1)
            nc.gpsimd.memset(row0[0:1, :], 1.0).then_inc(consts_pool, 1)
            deviation(2, 0)
            deviation(2, 1)
            m_low(0, 0)
            m_low(0, 2)
            vw_low(0)
            run(pool, step)

        @block.scalar
        def _(act):
            def copy_hi(dst, src, full, count, ready):
                act.wait_ge(full, count)
                nc.scalar.activation(dst, src, ACT.Copy).then_inc(ready, 1)

            def split_m(b, chunks):
                for c in chunks:
                    part = slice(c * MC, (c + 1) * MC)
                    if c == 0:
                        act.wait_ge(m_loaded, b * 16 + 16)
                    nc.scalar.activation(m_hi[:, part], m_raw[:, part], ACT.Copy).then_inc(m_hi_ready, 1)

            def split_vw(b):
                act.wait_ge(vw_loaded, b * 16 + 16)
                nc.scalar.activation(vw_hi[:, :], vw_raw[:, :], ACT.Copy).then_inc(vw_hi_ready, 1)

            def flat(ap):
                return ap[:, :, :].rearrange("p k w -> p (k w)")

            def step(b, t):
                done, gated, made_tile, ahead = (neighbour(b, t, d) for d in (-1, -2, -3, 1))
                here = b * TT + t if is_tile(b) else None
                last_scored = t == TT - 1 and is_tile(b) and is_tile(b + 1)
                if done:
                    for half in range(2):
                        w = PAIRS // 2
                        copy_hi(pt_hi[:, half * w:(half + 1) * w, :].rearrange("p k w -> p (k w)"), turn[half][:, :],
                                pt_full, done[2] * 2 + half + 1, pt_hi_ready)
                if made_tile:
                    act.wait_ge(gate_max_ready, made_tile[2] + 1)
                    nc.scalar.activation(gate_exp[:, :], gate[:, 0:E], ACT.Exp, bias=gate_negmax[:, :],
                                         accum_out=gate_sum[:, :]).then_inc(gate_exp_ready, 1)
                if last_scored:
                    act.wait_ge(score_full, here + 1)
                    split_m(b + 1, (0, 1))
                if gated:
                    copy_hi(flat(xt3_hi), turn[0][:, :], xt3_full, gated[2] + 1, xt3_hi_ready)
                if made_tile:
                    copy_hi(flat(ht_hi), turn[1][:, :], ht_full, made_tile[2] + 1, ht_hi_ready)
                if here is not None:
                    act.wait_ge(shifted, here + 1)
                    nc.scalar.activation(probs[:, :, :], probs[:, :, :], ACT.Exp).then_inc(exp_ready, 1)
                if last_scored:
                    split_m(b + 1, (2, 3))
                if ahead:
                    copy_hi(flat(xt2_hi), turn[0][:, :], xt2_full, ahead[2] + 1, xt2_hi_ready)
                if t == 0 and here is not None and not (isinstance(b, int) and b == 0):
                    act.wait_ge(attended_full, here)
                    split_vw(b)

            for h, src in enumerate((m_raw, vw_raw)):
                act.wait_ge(we_loaded[h], 16)
                nc.scalar.activation(we_hi[:, h * KT // 2:(h + 1) * KT // 2, :],
                                     src[:, :].rearrange("p (k w) -> p k w", w=2 * D)[:, 0:KT // 2, :], ACT.Copy).then_inc(we_hi_ready, 1)
            act.wait_ge(small_loaded, 32)
            nc.scalar.activation(wg_hi[:, :, :], wg_raw[:, :, :], ACT.Copy).then_inc(we_hi_ready, 1)
            copy_hi(flat(xt2_hi), turn[0][:, :], xt2_full, 1, xt2_hi_ready)
            split_m(0, range(M_CHUNKS))
            split_vw(0)
            run(act, step)

        @block.vector
        def _(dve):
            def low(dst, psum, hi, hi_ready, count, ready):
                dve.wait_ge(hi_ready, count)
                nc.vector.tensor_tensor(dst, psum, raw(hi), ALU.subtract).then_inc(ready, 1)

            def flat(ap):
                return ap[:, :, :].rearrange("p k w -> p (k w)")

            def layernorm_moments(k, src, n):
                stats, moments, var, _, _ = ln[k]
                nc.vector.bn_stats(stats[:, :], src).then_inc(stats_ready[k], 1)
                dve.wait_ge(stats_ready[k], n + 1)
                nc.vector.memset(beat[:, :], 0.0).then_inc(moments_ready[k], 1)
                nc.vector.bn_aggr(moments[:, :], stats[:, :]).then_inc(moments_ready[k], 1)
                dve.wait_ge(moments_ready[k], 2 * (n + 1))
                nc.vector.tensor_scalar(var[:, :], moments[:, 1:2], EPS, None, ALU.add).then_inc(var_ready[k], 1)

            def normalise(k, src, n):
                _, moments, _, rstd, xn = ln[k]
                dve.wait_ge(rstd_ready[k], n + 1)
                nc.vector.tensor_scalar(xn[:, :], src, moments[:, 0:1], rstd[:, :], ALU.subtract, ALU.mult).then_inc(xn_ready[k], 1)

            def layernorm2_moments(tile):
                b, t, n = tile
                dve.wait_ge(x1_loaded[t], b * 16 + 16)
                layernorm_moments(2, x1[:, t, :], n)

            def choose_expert(n, t):
                s = n * GATE_STEPS
                dve.wait_ge(gate_exp_ready, n + 1)
                nc.vector.tensor_reduce(gate_top[:, :], gate_exp[:, :], AX, ALU.max).then_inc(gate_step, 1)
                nc.vector.reciprocal(gate_inv[:, :], gate_sum[:, :]).then_inc(gate_step, 1)
                dve.wait_ge(gate_step, s + 2)
                nc.vector.scalar_tensor_tensor(gate_rank[:, :], gate_exp[:, :], gate_top[:, :], order[:, :],
                                               ALU.is_ge, ALU.mult).then_inc(gate_step, 1)
                nc.vector.tensor_scalar(gate_scale[:, t:t + 1], gate_inv[:, :], gate_top[:, :], SCALING, ALU.mult, ALU.mult)
                dve.wait_ge(gate_step, s + 3)
                nc.vector.tensor_reduce(gate_best[:, :], gate_rank[:, :], AX, ALU.max).then_inc(gate_step, 1)
                dve.wait_ge(gate_step, s + 4)
                nc.vector.tensor_scalar(gate_one[:, :], gate_rank[:, :], gate_best[:, :], None, ALU.is_equal).then_inc(gate_step, 1)
                dve.wait_ge(gate_step, s + 5)

            def m_low(b, c):
                part = slice(c * MC, (c + 1) * MC)
                dve.wait_ge(m_hi_ready, b * M_CHUNKS + c + 1)
                nc.vector.tensor_tensor(m_lo[:, part], m_raw[:, part], raw(m_hi[:, part]), ALU.subtract).then_inc(m_lo_by_dve, 1)

            def step(b, t):
                done, gated, made_tile, ahead, far = (neighbour(b, t, d) for d in (-1, -2, -3, 1, 2))
                here = b * TT + t if is_tile(b) else None
                last_scored = t == TT - 1 and is_tile(b) and is_tile(b + 1)
                if done:
                    for half in range(2):
                        w = PAIRS // 2
                        part = slice(half * w, (half + 1) * w)
                        low(pt_lo[:, part, :].rearrange("p k w -> p (k w)"), turn[half][:, :],
                            pt_hi[:, part, :].rearrange("p k w -> p (k w)"), pt_hi_ready, done[2] * 2 + half + 1, pt_ready)
                if made_tile:
                    _, mt, n = made_tile
                    dve.wait_ge(hid_full, n + 1)
                    nc.vector.tensor_reduce(gate_negmax[:, :], gate[:, 0:E], AX, ALU.max, negate=True).then_inc(gate_max_ready, 1)
                    choose_expert(n, mt)
                    nc.vector.tensor_tensor(hidden[:, :].rearrange("p (e r) -> p e r", e=E),
                                            hid[:, :].rearrange("p (e r) -> p e r", e=E),
                                            gate_one[:, :].unsqueeze(2).to_broadcast([P, E, R]), ALU.mult).then_inc(hidden_ready, 1)
                if here is not None:
                    dve.wait_ge(score_full, here + 1)
                    s = score[:, :, :].rearrange("p a (h s) -> p (a h) s", s=S)
                    nc.vector.tensor_reduce(row_max[:, :], s, AX, ALU.max).then_inc(max_ready, 1)
                    dve.wait_ge(max_ready, here + 1)
                    nc.vector.tensor_tensor(probs[:, :, :], s, row_max[:, :].unsqueeze(2).to_broadcast([P, XH, S]),
                                            ALU.subtract).then_inc(shifted, 1)
                if gated:
                    low(flat(xt3_lo), turn[0][:, :], flat(xt3_hi), xt3_hi_ready, gated[2] + 1, xt3_ready)
                if made_tile:
                    low(flat(ht_lo), turn[1][:, :], flat(ht_hi), ht_hi_ready, made_tile[2] + 1, ht_ready)
                if last_scored:
                    m_low(b + 1, 1)
                if here is not None:
                    dve.wait_ge(exp_ready, here + 1)
                    nc.vector.tensor_reduce(row_sum[:, :], probs[:, :, :], AX, ALU.add).then_inc(sum_ready, 1)
                    dve.wait_ge(sum_ready, here + 1)
                    nc.vector.reciprocal(row_inv[:, :], row_sum[:, :]).then_inc(inv_ready, 1)
                    dve.wait_ge(inv_ready, here + 1)
                    nc.vector.tensor_scalar(row_scale[:, :], row_inv[:, :], any_key[:, bass.ds(b, 1)], None,
                                            ALU.mult).then_inc(scale_ready, 1)
                if done:
                    db, dt_, n = done
                    dve.wait_ge(attended_full, n + 1)
                    if not (isinstance(n, int) and n < TT):
                        dve.wait_ge(out_stored[dt_], db * 16)
                    nc.vector.tensor_tensor(x2[:, dt_, :], attended[:, :], x1[:, dt_, :], ALU.add).then_inc(x2_ready, 1)
                    dve.wait_ge(x2_ready, n + 1)
                    layernorm_moments(3, x2[:, dt_, :], n)
                if ahead:
                    low(flat(xt2_lo), turn[0][:, :], flat(xt2_hi), xt2_hi_ready, ahead[2] + 1, xt2_ready)
                if last_scored:
                    m_low(b + 1, 3)
                if far:
                    layernorm2_moments(far)
                if done:
                    normalise(3, x2[:, done[1], :], done[2])
                if far:
                    normalise(2, x1[:, far[1], :], far[2])
                if made_tile:
                    _, mt, n = made_tile
                    dve.wait_ge(made_full, n + 1)
                    nc.vector.scalar_tensor_tensor(x2[:, mt, :], made[:, :], gate_scale[:, mt:mt + 1], x2[:, mt, :],
                                                   ALU.mult, ALU.add).then_inc(out_ready, 1)

            dve.wait_ge(small_loaded, 32)
            nc.vector.tensor_copy(mask_f[:, :], mask_u8[:, :]).then_inc(consts_ready, 1)
            dve.wait_ge(consts_ready, 1)
            nc.vector.tensor_scalar(mask_add[:, :, :], mask_f[:, :].rearrange("p (b s) -> p b s", b=B), 1.0, -MASKED,
                                    ALU.subtract, ALU.mult).then_inc(consts_ready, 1)
            nc.vector.tensor_reduce(any_key[:, :], mask_f[:, :].rearrange("p (b s) -> p b s", b=B), AX, ALU.max).then_inc(consts_ready, 1)
            dve.wait_ge(consts_ready, 3)
            for n in range(2):
                layernorm2_moments((0, n, n))
                normalise(2, x1[:, n, :], n)
                if n == 0:
                    low(flat(xt2_lo), turn[0][:, :], flat(xt2_hi), xt2_hi_ready, 1, xt2_ready)
            for h, src in enumerate((m_raw, vw_raw)):
                dve.wait_ge(we_hi_ready, h + 1)
                part = slice(h * KT // 2, (h + 1) * KT // 2)
                nc.vector.tensor_tensor(we_lo[:, part, :], src[:, :].rearrange("p (k w) -> p k w", w=2 * D)[:, 0:KT // 2, :],
                                        raw(we_hi[:, part, :]), ALU.subtract).then_inc(we_lo_ready, 1)
            dve.wait_ge(we_hi_ready, 3)
            nc.vector.tensor_tensor(wg_lo[:, :, :], wg_raw[:, :, :], raw(wg_hi[:, :, :]), ALU.subtract).then_inc(we_lo_ready, 1)
            m_low(0, 1)
            m_low(0, 3)
            run(dve, step)

        @block.tensor
        def _(pe):
            def transpose_tile(bank, src, width, ready, count, full):
                pe.wait_ge(ready, count)
                for k in range(width):
                    last = nc.tensor.transpose(bank[:, k * P:(k + 1) * P], src(k), ident[:, :])
                last.then_inc(full, 1)

            def view_m(m, half, k):
                return m[:, :].rearrange("p (g k w) -> p g k w", g=XG, k=KT)[:, half * HALF:(half + 1) * HALF, k, :]

            def turn_ahead(tile):
                n = tile[2]
                transpose_tile(turn[0], lambda k: ln[2][4][:, k * P:(k + 1) * P], KT, xn_ready[2], n + 1, xt2_full)

            def step(b, t):
                done, gated, made_tile, ahead = (neighbour(b, t, d) for d in (-1, -2, -3, 1))
                here = b * TT + t if is_tile(b) else None
                if done:
                    n = done[2]
                    for half in range(2):
                        if half == 0:
                            pe.wait_ge(xt2_ready, n + 2) if here is not None else None
                        elif made_tile is not None and neighbour(b, t, -4) is not None:
                            pe.wait_ge(ht_ready, n - 2)
                        transpose_tile(turn[half], lambda k: probs[:, :, :].rearrange("p h s -> p (h s)")[:, (half * 4 + k) * P:(half * 4 + k + 1) * P],
                                       4, probs_ready, n + 1, pt_full)
                if here is not None:
                    n = here
                    if t == 0:
                        pe.wait_ge(m_lo_by_pool, (b + 1) * 2)
                        pe.wait_ge(m_lo_by_dve, (b + 1) * 2)
                    pe.wait_ge(xt2_ready, n + 1)
                    if not (isinstance(n, int) and n == 0):
                        pe.wait_ge(shifted, n)
                    for half in range(2):
                        o = score[:, half, :]
                        nc.tensor.matmul(o, row0[:, :], mask_add[:, bass.ds(b, 1), :].to_broadcast([P, XH // 2, S]), start=True, stop=False)
                        for k in range(KT):
                            last = product(nc, o, [x[:, k, :] for x in (xt2_hi, xt2_lo)], [view_m(m, half, k) for m in (m_hi, m_lo)],
                                           False, k == KT - 1)
                    last.then_inc(score_full, 1)
                if gated:
                    if done:
                        pe.wait_ge(pt_ready, done[2] * 2 + 1)
                    transpose_tile(turn[0], lambda k: ln[3][4][:, k * P:(k + 1) * P], KT, xn_ready[3], gated[2] + 1, xt3_full)
                if made_tile:
                    if done:
                        pe.wait_ge(pt_ready, done[2] * 2 + 2)
                    transpose_tile(turn[1], lambda k: hidden[:, k * P:(k + 1) * P], KT, hidden_ready, made_tile[2] + 1, ht_full)
                if done:
                    db, dt_, n = done
                    if dt_ == 0:
                        pe.wait_ge(vw_ready, db + 1)
                    pe.wait_ge(pt_ready, n * 2 + 2)
                    if not (isinstance(n, int) and n == 0):
                        pe.wait_ge(x2_ready, n)
                    for g in range(PAIRS):
                        last = product(nc, attended[:, :], [p[:, g, :] for p in (pt_hi, pt_lo)],
                                       [w[:, g * D:(g + 1) * D] for w in (vw_hi, vw_lo)], g == 0, g == PAIRS - 1)
                    last.then_inc(attended_full, 1)
                if ahead:
                    if gated:
                        pe.wait_ge(xt3_ready, gated[2] + 1)
                    elif done:
                        pe.wait_ge(pt_ready, done[2] * 2 + 1)
                    turn_ahead(ahead)
                if made_tile:
                    n = made_tile[2]
                    pe.wait_ge(ht_ready, n + 1)
                    if not (isinstance(n, int) and n == 0):
                        pe.wait_ge(out_ready, n)
                    for k in range(KT):
                        last = product(nc, made[:, :], [h[:, k, :] for h in (ht_hi, ht_lo)],
                                       [w[:, k, D:2 * D] for w in (we_hi, we_lo)], k == 0, k == KT - 1)
                    last.then_inc(made_full, 1)
                if gated:
                    n = gated[2]
                    pe.wait_ge(xt3_ready, n + 1)
                    if not (isinstance(n, int) and n == 0):
                        pe.wait_ge(hidden_ready, n)
                    for k in range(KT):
                        product(nc, gate[:, 0:E], [x[:, k, :] for x in (xt3_hi, xt3_lo)],
                                [w[:, k, :] for w in (wg_hi, wg_lo)], k == 0, k == KT - 1)
                    for k in range(KT):
                        last = product(nc, hid[:, :], [x[:, k, :] for x in (xt3_hi, xt3_lo)],
                                       [w[:, k, 0:D] for w in (we_hi, we_lo)], k == 0, k == KT - 1)
                    last.then_inc(hid_full, 1)

            pe.wait_ge(consts_pool, 3 + E + 2)
            pe.wait_ge(consts_ready, 3)
            turn_ahead((0, 0, 0))
            pe.wait_ge(we_lo_ready, 3)
            run(pe, step)


def build(nc, x, mask, w_group, ctx_t, w_self, bias_self, bo, w_experts, w_gate, out):
    m_dram = nc.dram_tensor("m_dram", [B, P, XG, KT * 2 * S], F32, kind="Internal").ap()
    vw_dram = nc.dram_tensor("vw_dram", [B, P, XG, D], F32, kind="Internal").ap()
    x1_dram = nc.dram_tensor("x1_dram", [B, T, D], F32, kind="Internal").ap()
    with ExitStack() as ctx:
        self_split = [ctx.enter_context(nc.sbuf_tensor(f"w_self_{n}", [P, KT, 4 * D], F32R)) for n in ("hi", "lo")]
        cross_products(nc, w_group, ctx_t, m_dram, vw_dram, w_self, self_split)
        self_attention(nc, x, self_split, bias_self, bo, x1_dram)
    cross_attention_and_experts(nc, x1_dram, m_dram, vw_dram, mask, w_experts, w_gate, out)


def kernel(x, ctx_1024, mask_BxS2_bf1, L0_attn_Wq, L0_attn_bq, L0_attn_Wk, L0_attn_bk, L0_attn_Wv, L0_attn_bv, L0_attn_Wo,
           L0_attn_bo, L0_xattn_Wq, L0_xattn_Wk, L0_xattn_Wv, L0_xattn_Wo, L0_ffn_A, L0_ffn_Bw, L0_ffn_Wg):
    import numpy as np
    import concourse.bacc as bacc
    from concourse.bass_utils import run_bass_kernel_spmd

    def rows(a):
        return a.reshape(-1, P, a.shape[-1]).transpose(1, 0, 2)

    heads = [np.asarray(w).transpose(1, 0, 2).reshape(D, H * HD) for w in (L0_attn_Wq, L0_attn_Wk, L0_attn_Wv)]
    w_self = rows(np.concatenate(heads + [np.asarray(L0_attn_Wo)], axis=1))
    bias_self = np.stack([np.asarray(v).reshape(QUADS, P).T for v in (L0_attn_bq, L0_attn_bk, L0_attn_bv)], axis=1)
    wk, wv = (np.asarray(w).reshape(CT, P, XG, XD).transpose(2, 1, 0, 3).reshape(XG, P, CT * XD) for w in (L0_xattn_Wk, L0_xattn_Wv))
    wq = np.asarray(L0_xattn_Wq).reshape(D, XG, XH // XG, XD).transpose(1, 3, 2, 0).reshape(XG, P, -1)
    wo = np.asarray(L0_xattn_Wo).reshape(XG, XH // XG, XD, D).transpose(0, 2, 1, 3).reshape(XG, P, -1)
    w_group = np.concatenate([wk, wv, wq, wo], axis=2)
    ctx_t = rows(np.asarray(ctx_1024).reshape(B * S, DC).T)
    w_experts = rows(np.concatenate([np.asarray(L0_ffn_A).reshape(E * R, D).T,
                                     np.asarray(L0_ffn_Bw).transpose(0, 2, 1).reshape(E * R, D)], axis=1))
    w_gate = rows(np.asarray(L0_ffn_Wg).T)
    arrays = {"x": x, "mask": np.asarray(mask_BxS2_bf1).view(np.uint8).reshape(1, B * S), "w_group": w_group, "ctx_t": ctx_t,
              "w_self": w_self, "bias_self": bias_self, "bo": np.asarray(L0_attn_bo).reshape(1, D), "w_experts": w_experts,
              "w_gate": w_gate}
    arrays = {k: np.ascontiguousarray(a) for k, a in arrays.items()}
    nc = bacc.Bacc("TRN2", target_bir_lowering=False, num_devices=1, dynamic_dma_scratch_size=1024)
    aps = {k: nc.dram_tensor(k + "_dram", a.shape, mybir.dt.from_np(a.dtype), kind="ExternalInput").ap() for k, a in arrays.items()}
    out = nc.dram_tensor("out_dram", [B, T, D], F32, kind="ExternalOutput").ap()
    build(nc, out=out, **aps)
    got = run_bass_kernel_spmd(nc, [{k + "_dram": a for k, a in arrays.items()}], core_ids=[0])
    return got.results[0]["out_dram"]
```

```python
import concourse.bass as bass
from concourse import mybir
from concourse.alu_op_type import AluOpType as ALU
from contextlib import ExitStack

F32 = mybir.dt.float32
F32R = mybir.dt.float32r
F16 = mybir.dt.float16
BF16 = mybir.dt.bfloat16
U8 = mybir.dt.uint8
ACT = mybir.ActivationFunctionType
AX = mybir.AxisListType.X

P = 128
B, T, D = 8, 512, 512
TT = T // P
KT = D // P
H, HD = 16, D // 16
QUADS = H * HD // P
HQ = H // QUADS
XH, XG, XD = 16, 8, 128
S = 64
DC = 256
CT = DC // P
E, R = 8, 64
SCALING = 4.0
EPS = 1e-5
MASKED = -1e30



def raw(ap):
    return ap.bitcast(F32)


def product(nc, out, lhs, rhs, start, stop):
    pairs = [(lhs[0], rhs[0]), (lhs[0], rhs[1]), (lhs[1], rhs[0])]
    for n, (a, b) in enumerate(pairs):
        last = nc.tensor.matmul(out, a, b, start=start and n == 0, stop=stop and n == 2)
    return last


def wait_all(engine, *waits):
    values = [v if isinstance(v, int) else engine.snap(v) for _, v in waits]
    for (sem, _), v in zip(waits, values):
        engine.wait_ge(sem, v)


def cross_products(nc, w_group, ctx_t, m_dram, vw_dram, w_self, self_split, x, x_in, xn, ident, vw_out, vw_stored):
    HH = XH // XG
    BP = B // 2
    KV = 2 * CT * XD
    COLS = KV + 2 * HH * D
    USES, BANKS = 2 + HH * KT + BP * HH, 6
    assert USES % BANKS == 0
    BS = B * S

    with ExitStack() as ctx:
        def sb(name, shape, dt):
            return ctx.enter_context(nc.sbuf_tensor("c_" + name, shape, dt))

        def sem(name):
            return ctx.enter_context(nc.semaphore("c_" + name))

        c_raw = sb("c_raw", [P, CT, BS], F32)
        c_hi, c_lo = (sb(f"c_{n}", [P, CT, BS], F32R) for n in ("hi", "lo"))
        w_raw = sb("w_raw", [P, 2, COLS], F32)
        w_hi, w_lo = (sb(f"w_{n}", [P, 2, COLS], F32R) for n in ("hi", "lo"))
        kv_hi, kv_lo = (sb(f"kv_{n}", [P, 2, 2, BS], F32R) for n in ("hi", "lo"))
        ws_raw = sb("ws_raw", [P, 2, 4 * D], F32)
        ws_hi, ws_lo = self_split
        stats = sb("stats", [P, TT, 6], F32)
        moments = sb("moments", [P, TT, 2], F32)
        var_eps, rstd, minus_half = (sb(n, [P, TT], F32) for n in ("var_eps", "rstd", "minus_half"))
        m_out = sb("m_out", [P, B, KT, HH, S], F32)
        bank = [ctx.enter_context(nc.psum_tensor(f"c_bank{n}", [P, 512], F32)) for n in range(BANKS)]

        ctx_loaded, ctx_hi_ready, ctx_lo_ready = sem("ctx_loaded"), sem("ctx_hi"), sem("ctx_lo")
        w_loaded = [sem(f"w{n}_loaded") for n in range(2)]
        w_hi_ready, w_lo_ready = sem("w_hi_ready"), sem("w_lo_ready")
        bank_full = sem("bank_full")
        kv_hi_ready, kv_lo_ready = sem("kv_hi_ready"), sem("kv_lo_ready")
        m_by_act, m_by_dve = sem("m_by_act"), sem("m_by_dve")
        vw_by_act, vw_by_dve = sem("vw_by_act"), sem("vw_by_dve")
        m_stored = sem("m_stored")
        ws_loaded = [sem(f"ws{n}_loaded") for n in range(2)]
        ws_hi_ready, ws_lo_ready = sem("ws_hi_ready"), sem("ws_lo_ready")
        kv0_loaded, kv0_hi_ready, kv0_lo_ready = sem("kv0_loaded"), sem("kv0_hi_ready"), sem("kv0_lo_ready")
        x_loaded, stats_ready, moments_ready, var_ready = sem("x_loaded"), sem("stats_ready"), sem("moments_ready"), sem("var_ready")
        rstd_ready, consts = sem("rstd_ready"), sem("consts")

        block = ctx.enter_context(nc.Block())

        def wslice(w, par, kind):
            if kind in "kv":
                at = 0 if kind == "k" else KV // 2
                return w[:, par, at:at + KV // 2].rearrange("p (t d) -> p t d", t=CT)
            at = KV + (HH * D if kind == "o" else 0)
            return w[:, par, at:at + HH * D].rearrange("p (h c) -> p h c", h=HH)

        @block.sync
        def _(sp):
            sp.dma_start(c_raw[:, :, :], ctx_t).then_inc(ctx_loaded, 16)
            sp.dma_start(w_raw[:, 0, 0:KV], w_group[0, :, 0:KV]).then_inc(kv0_loaded, 16)
            sp.dma_start(w_raw[:, 0, KV:], w_group[0, :, KV:]).then_inc(w_loaded[0], 16)

            def load_self(k):
                sp.dma_start(ws_raw[:, k % 2, :], w_self[:, k, :]).then_inc(ws_loaded[k % 2], 16)

            load_self(0)
            sp.dma_start(w_raw[:, 1, :], w_group[1]).then_inc(w_loaded[1], 16)
            load_self(1)
            sp.dma_start(x_in[:, :, :], x[0].rearrange("(t p) c -> p t c", p=P)).then_inc(x_loaded, 16)
            sp.wait_ge(ws_lo_ready, 2)
            load_self(2)

            def store(n, par):
                wait_all(sp, (m_by_act, n * 4 + 4), (m_by_dve, n * 4 + 4))
                sp.dma_start(m_dram[:, :, bass.ds(n, 1), :].rearrange("b p g m -> p b (g m)"),
                             m_out[:, :, :, :, :].rearrange("p b t h s -> p b (t h s)")).then_inc(m_stored, 16)
                wait_all(sp, (vw_by_act, n * 4 + 4), (vw_by_dve, n * 4 + 4))
                rows = vw_dram[:, :, bass.ds(n, 1), :].rearrange("(bp b2) (h s) g e -> b2 h s bp (g e)", b2=2, h=HH)
                for b2 in range(2):
                    for h in range(HH):
                        sp.dma_start(rows[b2, h], vw_out[b2 * S:(b2 + 1) * S, :, h, :]).then_inc(vw_stored, 16)

            sp.sem_inc(m_stored, 16)
            sp.sem_inc(vw_stored, 64)
            with sp.Fori(0, XG // 2 - 1) as i:
                for par in range(2):
                    n = i * 2 + par
                    wait_all(sp, (w_hi_ready, n + 1), (w_lo_ready, n + 1))
                    sp.dma_start(w_raw[:, par, :], w_group[bass.ds(n + 2, 1)].rearrange("g p w -> p (g w)")).then_inc(w_loaded[par], 16)
                    store(n, par)

            sp.wait_ge(ws_lo_ready, 4)
            load_self(3)
            for par in range(2):
                store(XG - 2 + par, par)
            sp.wait_ge(m_stored, XG * 16 + 16)

        @block.gpsimd
        def _(pool):
            nc.gpsimd.memset(ident[:, :], 0.0).then_inc(consts, 1)
            nc.gpsimd.memset(minus_half[:, :], -0.5).then_inc(consts, 1)
            pool.wait_ge(consts, 2)
            nc.gpsimd.affine_select(out=ident[:, :], in_=ident[:, :], compare_op=ALU.not_equal, fill=1.0,
                                    base=0, pattern=[[-1, P]], channel_multiplier=1).then_inc(consts, 1)

            def low(n, par):
                pool.wait_ge(w_hi_ready, n + 1)
                nc.gpsimd.tensor_tensor(w_lo[:, par, :], w_raw[:, par, :], raw(w_hi[:, par, :]),
                                        ALU.subtract).then_inc(w_lo_ready, 1)

            pool.wait_ge(w_lo_ready, 1)
            low(1, 1)
            with pool.Fori(1, XG // 2) as i:
                low(i * 2, 0)
                low(i * 2 + 1, 1)
            pool.wait_ge(var_ready, 1)
            nc.gpsimd.tensor_tensor(rstd[:, :], var_eps[:, :], minus_half[:, :], ALU.pow).then_inc(rstd_ready, 1)

        @block.scalar
        def _(act):
            def split_hi(pair, par):
                act.wait_ge(w_loaded[par], pair * 16 + 16)
                nc.scalar.activation(w_hi[:, par, :], w_raw[:, par, :], ACT.Copy).then_inc(w_hi_ready, 1)

            def group(pair, par, more, self_tile=None):
                n = pair * 2 + par
                for kv in range(2):
                    act.wait_ge(bank_full, n * USES + kv + 1)
                    nc.scalar.activation(kv_hi[:, par, kv, :], bank[kv][:, :], ACT.Copy,
                                         scale=XD ** -0.5 if kv == 0 else 1.0).then_inc(kv_hi_ready, 1)
                if more:
                    split_hi(pair + par, 1 - par)
                act.wait_ge(m_stored, n * 16 + 16)
                for u in range(2, 2 + HH * KT, 2):
                    h, t = divmod(u - 2, KT)
                    act.wait_ge(bank_full, n * USES + u + 1)
                    nc.scalar.activation(m_out[:, :, t, h, :], bank[u % BANKS][:, :].rearrange("p (b s) -> p b s", b=B),
                                         ACT.Copy).then_inc(m_by_act, 1)
                if self_tile is not None:
                    split_self(self_tile)
                act.wait_ge(vw_stored, n * 64 + 64)
                for u in range(2 + HH * KT, USES, 2):
                    bp, h = divmod(u - 2 - HH * KT, HH)
                    act.wait_ge(bank_full, n * USES + u + 1)
                    nc.scalar.activation(vw_out[:, bp, h, :], bank[u % BANKS][:, :], ACT.Copy).then_inc(vw_by_act, 1)

            act.wait_ge(ctx_loaded, 16)
            nc.scalar.activation(c_hi[:, :, :], c_raw[:, :, :], ACT.Copy).then_inc(ctx_hi_ready, 1)
            def split_self(k):
                act.wait_ge(ws_loaded[k % 2], k // 2 * 16 + 16)
                nc.scalar.activation(ws_hi[:, k, 0:D], ws_raw[:, k % 2, 0:D], ACT.Copy, scale=HD ** -0.5).then_inc(ws_hi_ready, 1)
                nc.scalar.activation(ws_hi[:, k, D:], ws_raw[:, k % 2, D:], ACT.Copy).then_inc(ws_hi_ready, 1)

            act.wait_ge(kv0_loaded, 16)
            nc.scalar.activation(w_hi[:, 0, 0:KV], w_raw[:, 0, 0:KV], ACT.Copy).then_inc(kv0_hi_ready, 1)
            act.wait_ge(w_loaded[0], 16)
            nc.scalar.activation(w_hi[:, 0, KV:], w_raw[:, 0, KV:], ACT.Copy).then_inc(w_hi_ready, 1)
            split_self(0)
            with act.Fori(0, XG // 2 - 1) as i:
                group(i, 0, True)
                group(i, 1, True)

            group(XG // 2 - 1, 0, True, 1)
            group(XG // 2 - 1, 1, False, 2)
            split_self(3)

        @block.vector
        def _(dve):
            dve.wait_ge(ctx_hi_ready, 1)
            nc.vector.tensor_tensor(c_lo[:, :, :], c_raw[:, :, :], raw(c_hi[:, :, :]), ALU.subtract).then_inc(ctx_lo_ready, 1)
            def split_self(k):
                dve.wait_ge(ws_hi_ready, 2 * k + 2)
                nc.vector.scalar_tensor_tensor(ws_lo[:, k, 0:D], ws_raw[:, k % 2, 0:D], HD ** -0.5, raw(ws_hi[:, k, 0:D]),
                                               ALU.mult, ALU.subtract).then_inc(ws_lo_ready, 1)
                nc.vector.tensor_tensor(ws_lo[:, k, D:], ws_raw[:, k % 2, D:], raw(ws_hi[:, k, D:]), ALU.subtract).then_inc(ws_lo_ready, 1)

            dve.wait_ge(kv0_hi_ready, 1)
            nc.vector.tensor_tensor(w_lo[:, 0, 0:KV], w_raw[:, 0, 0:KV], raw(w_hi[:, 0, 0:KV]), ALU.subtract).then_inc(kv0_lo_ready, 1)
            dve.wait_ge(w_hi_ready, 1)
            nc.vector.tensor_tensor(w_lo[:, 0, KV:], w_raw[:, 0, KV:], raw(w_hi[:, 0, KV:]), ALU.subtract).then_inc(w_lo_ready, 1)
            split_self(0)

            def group(n, par, self_tile=None):
                for kv in range(2):
                    dve.wait_ge(kv_hi_ready, n * 2 + kv + 1)
                    nc.vector.scalar_tensor_tensor(kv_lo[:, par, kv, :], bank[kv][:, :], XD ** -0.5 if kv == 0 else 1.0,
                                                   raw(kv_hi[:, par, kv, :]), ALU.mult, ALU.subtract)\
                        .then_inc(kv_lo_ready, 1)
                dve.wait_ge(m_stored, n * 16 + 16)
                for u in range(3, 2 + HH * KT, 2):
                    h, t = divmod(u - 2, KT)
                    dve.wait_ge(bank_full, n * USES + u + 1)
                    nc.vector.tensor_copy(m_out[:, :, t, h, :], bank[u % BANKS][:, :].rearrange("p (b s) -> p b s", b=B))\
                        .then_inc(m_by_dve, 1)
                if self_tile is not None:
                    split_self(self_tile)
                dve.wait_ge(vw_stored, n * 64 + 64)
                for u in range(3 + HH * KT, USES, 2):
                    bp, h = divmod(u - 2 - HH * KT, HH)
                    dve.wait_ge(bank_full, n * USES + u + 1)
                    nc.vector.tensor_copy(vw_out[:, bp, h, :], bank[u % BANKS][:, :]).then_inc(vw_by_dve, 1)

            with dve.Fori(0, XG // 2 - 1) as i:
                for par in range(2):
                    group(i * 2 + par, par)
            dve.wait_ge(x_loaded, 16)
            for t in range(TT):
                nc.vector.bn_stats(stats[:, t, :], x_in[:, t, :]).then_inc(stats_ready, 1)
            dve.wait_ge(stats_ready, TT)
            for t in range(TT):
                nc.vector.bn_aggr(moments[:, t, :], stats[:, t, :]).then_inc(moments_ready, 1)
            dve.wait_ge(moments_ready, TT)
            nc.vector.tensor_scalar(var_eps[:, :], moments[:, :, 1], EPS, None, ALU.add).then_inc(var_ready, 1)
            group(XG - 2, 0, 1)
            dve.wait_ge(rstd_ready, 1)
            for t in range(TT):
                nc.vector.tensor_scalar(xn[:, t, :], x_in[:, t, :], moments[:, t, 0:1], rstd[:, t:t + 1], ALU.subtract, ALU.mult)
            group(XG - 1, 1, 2)
            split_self(3)

        @block.tensor
        def _(pe):
            pe.wait_ge(ctx_lo_ready, 1)

            def group(n, par, first):
                if first:
                    pe.wait_ge(kv0_lo_ready, 1)
                else:
                    pe.wait_ge(w_lo_ready, n + 1)

                def drained(u):
                    before, m = (u - BANKS, n) if u >= BANKS else (u - BANKS + USES, n - 1)
                    if u < BANKS and first:
                        return
                    if before < 2:
                        pe.wait_ge(kv_lo_ready, m * 2 + before + 1)
                    elif before < 2 + HH * KT:
                        pe.wait_ge((m_by_act, m_by_dve)[before % 2], m * 4 + (before - 2) // 2 + 1)
                    else:
                        pe.wait_ge((vw_by_act, vw_by_dve)[before % 2], m * 4 + (before - 2 - HH * KT) // 2 + 1)

                for kv, kind in enumerate("kv"):
                    drained(kv)
                    for t in range(CT):
                        last = product(nc, bank[kv][:, :], [wslice(w, par, kind)[:, t, :] for w in (w_hi, w_lo)],
                                       [c[:, t, :] for c in (c_hi, c_lo)], t == 0, t == CT - 1)
                    last.then_inc(bank_full, 1)
                pe.wait_ge(kv_lo_ready, n * 2 + 1)
                if first:
                    pe.wait_ge(w_lo_ready, 1)
                for u in range(2, 2 + HH * KT):
                    h, t = divmod(u - 2, KT)
                    drained(u)
                    product(nc, bank[u % BANKS][:, :], [wslice(w, par, "q")[:, h, t * P:(t + 1) * P] for w in (w_hi, w_lo)],
                            [k[:, par, 0, :] for k in (kv_hi, kv_lo)], True, True).then_inc(bank_full, 1)
                pe.wait_ge(kv_lo_ready, n * 2 + 2)
                for u in range(2 + HH * KT, USES):
                    bp, h = divmod(u - 2 - HH * KT, HH)
                    drained(u)
                    product(nc, bank[u % BANKS][:, :], [v[:, par, 1, bp * P:(bp + 1) * P] for v in (kv_hi, kv_lo)],
                            [wslice(w, par, "o")[:, h, :] for w in (w_hi, w_lo)], True, True).then_inc(bank_full, 1)

            group(0, 0, True)
            group(1, 1, False)
            with pe.Fori(1, XG // 2) as i:
                group(i * 2, 0, False)
                group(i * 2 + 1, 1, False)


def units_of_batch():
    out = []
    for q in range(QUADS):
        for i in range(TT):
            step = max(1, TT // (i + 1)) if i < 2 else 1
            step = min(step, HQ)
            for j in range(0, HQ, step):
                out.append((q, i, list(range(j, j + step))))
    return out


STEPS = {"xt": 1, "yt": 1, "qk": KT, "v": 2 * KT, "o": KT}


def beside_units(uses):
    units = len(units_of_batch()) // 2
    passes = {"xt": 8, "yt": 8, "qk": 3, "v": 1.5, "o": 3}
    steps = [(kind, n, k) for kind, n in uses for k in range(STEPS[kind])]
    out, done, total = [[] for _ in range(units)], 0, sum(passes[kind] for kind, _, _ in steps)
    unit, completed = 0, -1
    for kind, n, k in steps:
        unit = max(unit, int(done / total * (units - 1)))
        if k == STEPS[kind] - 1:
            unit = max(unit, completed + 1)
            completed = unit
        out[unit].append((kind, n, k))
        done += passes[kind]
    assert not out[-1]
    return out


def self_attention(nc, x, self_split, bias_self, bo, x1_dram, x_in, xn, ident, vw_stored, m_dram, m_raw):
    UNITS = units_of_batch()
    NU = len(UNITS)
    PQ = NU // QUADS
    HU = NU // 2
    GROUPS = QUADS * TT
    V3 = 3 * HD
    WQ, WK, WV, WO = (n * D for n in range(4))
    ENDS = [q * TT + i if heads[-1] == HQ - 1 else None for q, i, heads in UNITS]

    with ExitStack() as ctx:
        def sb(name, shape, dt):
            return ctx.enter_context(nc.sbuf_tensor("a_" + name, shape, dt))

        def pb(name):
            return ctx.enter_context(nc.psum_tensor("a_" + name, [P, 512], F32))

        def sem(name):
            return ctx.enter_context(nc.semaphore("a_" + name))

        w_hi, w_lo = self_split
        bias = sb("bias", [P, 3, QUADS], F32)
        bias_q = sb("bias_q", [P, QUADS], F32)
        bo_all = sb("bo_all", [P, D], F32)
        ident_bf = sb("ident_bf", [P, P], BF16)
        causal = sb("causal", [P, P], F32)
        causal_bf = sb("causal_bf", [P, P], BF16)
        minus_half = sb("minus_half", [P, TT], F32)
        x_res = sb("x_res", [P, TT, D], F32)
        stats = sb("stats", [P, TT, 6], F32)
        moments = sb("moments", [P, TT, 2], F32)
        beat = sb("beat", [P, TT], F32)
        var_eps = sb("var_eps", [P, TT], F32)
        rstd = sb("rstd", [P, TT], F32)
        xt_hi, xt_lo = (sb(f"xt_{n}", [P, KT, T], F32R) for n in ("hi", "lo"))
        yt_hi, yt_lo = (sb(f"yt_{n}", [P, QUADS, T], F32R) for n in ("hi", "lo"))
        qk = [sb(f"qk{n}", [P, 4, T], F32R) for n in range(2)]
        Q_LO, Q_HI, K_HI, K_LO = range(4)
        stack = [sb(f"stack{n}", [3 * HD, 2, HQ, T], F32R) for n in range(2)]
        v_rest = sb("v_rest", [P, 2, D], F32)
        v = sb("v", [P, TT, H, 3, HD], BF16)
        neg_max = sb("neg_max", [P, GROUPS * HQ], F32)
        sums = sb("sums", [P, GROUPS * HQ], F32)
        probs = sb("probs", [P, 2, T], F32)
        pt_hi, pt_lo = (sb(f"pt_{n}", [P, 2, T], F16) for n in ("hi", "lo"))
        y_sum = sb("y_sum", [P, 2, P], F32)
        y_rec = sb("y_rec", [P, 2, HQ], F32)
        y = sb("y", [P, TT, D], F32)
        gemm = [pb(f"gemm{n}") for n in range(2)]
        score = [pb(f"score{n}") for n in range(2)]
        turned = [pb(f"turned{n}") for n in range(2)]
        out_y = [pb(f"out_y{n}") for n in range(2)]

        small_loaded, consts_pool, consts_ready = sem("small_loaded"), sem("consts_pool"), sem("consts_ready")
        x_loaded, x_res_loaded, x_res_ready = sem("x_loaded"), sem("x_res_loaded"), sem("x_res_ready")
        var_ready, rstd_ready, xn_ready = sem("var_ready"), sem("rstd_ready"), sem("xn_ready")
        gemm_full, gemm_drained = sem("gemm_full"), sem("gemm_drained")
        xt_hi_ready = sem("xt_hi_ready")
        qk_hi_ready = sem("qk_hi_ready")
        stacked = [sem(f"stacked{n}") for n in range(2)]
        v1_ready, v2_ready, v_ready = sem("v1_ready"), sem("v2_ready"), sem("v_ready")
        score_full, max_ready, probs_ready = sem("score_full"), sem("max_ready"), sem("probs_ready")
        turned_full, pt_hi_ready, pt_ready = sem("turned_full"), sem("pt_hi_ready"), sem("pt_ready")
        y_full, y_summed, y_ready = sem("y_full"), sem("y_summed"), sem("y_ready")
        yt_hi_ready = sem("yt_hi_ready")
        x1_stored = sem("x1_stored")
        stats_ready, moments_ready = sem("stats_ready"), sem("moments_ready")
        m_loaded = sem("m_loaded")

        block = ctx.enter_context(nc.Block())

        LATE = ([("xt", k) for k in range(KT)] + [("yt", 0), ("yt", 1), ("qk", 0), ("qk", 1), ("v", 0), ("v", 1),
                                                  ("yt", 2), ("qk", 2), ("qk", 3)])
        EARLY = [("v", 2), ("v", 3), ("yt", 3), ("qk", 4), ("qk", 5)] + [("o", t) for t in range(TT)] + [("qk", 6), ("qk", 7)]
        AHEAD = [("xt", k) for k in range(KT)] + [("qk", 0), ("qk", 1), ("v", 0), ("v", 1), ("qk", 2), ("qk", 3)]
        late, early = beside_units(LATE), beside_units(EARLY)

        def only(steps, wanted):
            return [[step for step in unit if wanted(step[0])] for unit in steps]

        BESIDE = {"first": only(early, lambda kind: kind not in ("yt", "o")), "late": late, "early": early,
                  "last": only(late, lambda kind: kind == "yt")}

        def completed(steps):
            return [(kind, n) for unit in steps for kind, n, k in unit if k == STEPS[kind] - 1]

        USES = {"first": AHEAD + completed(BESIDE["first"]), "loop": completed(late) + completed(early),
                "last": completed(BESIDE["last"]) + [("yt", 3)] + [("o", t) for t in range(TT)]}
        FIRST, G_ALL = len(USES["first"]), len(USES["loop"])
        assert G_ALL % 2 == 0 and FIRST % 2 == 0
        for steps in (late, early):
            ends = [m for m, unit in enumerate(steps) for kind, n, k in unit if kind == "qk" and n % 2 and k == KT - 1]
            assert all(m + 1 + 1 >= (j + 1) * PQ - 1 for j, m in enumerate(ends))

        def use_of(it, kind, n):
            table = "first" if it is None else "last" if isinstance(it, int) and it == B - 1 else "loop"
            u = USES[table].index((kind, n))
            return (u if it is None else it * G_ALL + FIRST + u), gemm[u % 2]

        def drained(use):
            return use + 3

        def values(u, part):
            half, pair = divmod(u, 2)
            return v[:, pair * 2:pair * 2 + 2, half * H // 2:(half + 1) * H // 2, part, :]

        def rest(u):
            return v_rest[:, u % 2, :].rearrange("p (t h d) -> p t h d", t=2, d=HD)

        def next_batch(it):
            return 0 if it is None else it + 1

        def unit_at(b, n):
            d = -1 if n < 0 else n // NU
            if isinstance(b, int) and not 0 <= b + d < B:
                return None
            return b + d, n - d * NU

        def halves(engine, half):
            half(0, 0, None, BESIDE["first"], True)
            with engine.Fori(0, B - 2) as b:
                half(b, HU, b, BESIDE["late"], True)
                half(b + 1, 0, b, BESIDE["early"], True)
            half(B - 2, HU, B - 2, BESIDE["late"], False)
            half(B - 1, 0, B - 2, BESIDE["early"], False)
            half(B - 1, HU, B - 1, BESIDE["last"], False)

        STACK_DMAS = 16 * 3 * HQ
        @block.sync
        def _(sp):
            def load_x(b):
                sp.dma_start(x_in[:, :, :], x[bass.ds(b, 1)].rearrange("b (t p) c -> p (b t) c", p=P)).then_inc(x_loaded, 16)

            def stack_quad(b, q, it):
                sp.wait_ge(gemm_drained, drained(use_of(it, "qk", 2 * q + 1)[0]))
                st = stack[q % 2]
                for j in range(HQ):
                    rows = slice(j * HD, (j + 1) * HD)
                    for r, (of_q, of_k) in enumerate([(Q_HI, K_HI), (Q_HI, K_LO), (Q_LO, K_HI)]):
                        sp.dma_start(raw(st[r * HD:(r + 1) * HD, :, j, :]),
                                     raw(qk[q % 2][rows, of_q:of_k + 1:of_k - of_q, :])).then_inc(stacked[q % 2], 16)

            def store_x1(it):
                for t in range(TT):
                    sp.wait_ge(gemm_drained, drained(use_of(it, "o", t)[0]))
                    sp.dma_start(x1_dram[bass.ds(it, 1), t * P:(t + 1) * P, :].rearrange("b p c -> p (b c)"),
                                 x_res[:, t, :]).then_inc(x1_stored, 16)

            def half(b, n0, it, beside, more):
                if n0:
                    if more:
                        sp.wait_ge(xn_ready, (b + 1) * TT)
                        load_x(b + 2)
                    sp.wait_ge(x1_stored, b * TT * 16 + 16)
                    sp.dma_start(x_res[:, :, :], x[bass.ds(b, 1)].rearrange("b (t p) c -> p (b t) c", p=P)).then_inc(x_res_loaded, 16)
                    if not (isinstance(b, int) and b == B - 1):
                        stack_quad(b + 1, 0, it)
                        stack_quad(b + 1, 1, it)
                else:
                    stack_quad(b, 2, it)
                    if it is not None:
                        store_x1(it)
                    stack_quad(b, 3, it)

            sp.dma_start(bias[:, :, :], bias_self).then_inc(small_loaded, 16)
            sp.dma_start(bo_all[:, :], bo.to_broadcast([P, D])).then_inc(small_loaded, 16)
            sp.sem_inc(x1_stored, 16)
            load_x(1)
            stack_quad(0, 0, None)
            stack_quad(0, 1, None)
            halves(sp, half)
            sp.wait_ge(vw_stored, XG * 64 + 64)
            sp.dma_start(m_raw, m_dram[0].rearrange("p g m -> p (g m)")).then_inc(m_loaded, 16)
            store_x1(B - 1)
            sp.wait_ge(m_loaded, 16)
            sp.wait_ge(x1_stored, B * TT * 16 + 16)

        @block.gpsimd
        def _(pool):
            nc.gpsimd.memset(causal[:, :], 0.0).then_inc(consts_pool, 1)
            nc.gpsimd.memset(minus_half[:, :], -0.5).then_inc(consts_pool, 1)
            pool.wait_ge(consts_pool, 2)
            nc.gpsimd.affine_select(out=causal[:, :], in_=causal[:, :], compare_op=ALU.is_ge, fill=MASKED,
                                    base=0, pattern=[[-1, P]], channel_multiplier=1).then_inc(consts_pool, 1)
            pool.wait_ge(small_loaded, 32)

            def reciprocal_deviation(b):
                pool.wait_ge(var_ready, b)
                nc.gpsimd.tensor_tensor(rstd[:, :], var_eps[:, :], minus_half[:, :], ALU.pow).then_inc(rstd_ready, 1)

            def values_third(b, u):
                pool.wait_ge(v2_ready, b * 4 + u + 1)
                nc.gpsimd.tensor_tensor(values(u, 2), rest(u), values(u, 1), ALU.subtract).then_inc(v_ready, 1)

            def half(b, n0, it, beside, more):
                g0 = GROUPS // 2 if n0 else 0
                for g in range(g0, g0 + GROUPS // 2):
                    q, i = divmod(g, TT)
                    pool.wait_ge(y_summed, b * GROUPS + g + 1)
                    nc.gpsimd.tensor_tensor(y[:, i, q * P:(q + 1) * P].rearrange("p (h d) -> p h d", h=HQ),
                                            y_sum[:, g % 2, :].rearrange("p (h d) -> p h d", h=HQ),
                                            y_rec[:, g % 2, :].unsqueeze(2).to_broadcast([P, HQ, HD]),
                                            ALU.mult).then_inc(y_ready, 1)
                    if g == 1:
                        values_third(b, 2)
                        values_third(b, 3)
                    if g == 2 and more:
                        reciprocal_deviation(b + 1)
                    if g == 2 * TT + 2:
                        pool.wait_ge(x_res_loaded, b * 16 + 16)
                        nc.gpsimd.tensor_tensor(x_res[:, :, :], x_res[:, :, :], bo_all[:, :].unsqueeze(1).to_broadcast([P, TT, D]),
                                                ALU.add).then_inc(x_res_ready, 1)
                    if g in (3 * TT + 1, 3 * TT + 2) and not (isinstance(b, int) and b == B - 1):
                        values_third(b + 1, g - 3 * TT - 1)

            values_third(0, 0)
            values_third(0, 1)
            halves(pool, half)

        @block.scalar
        def _(act):
            def high_part(it, kind, n):
                use, bank = use_of(it, kind, n)
                act.wait_ge(gemm_full, use + 1)
                if kind == "xt":
                    nc.scalar.activation(xt_hi[:, n, :], bank[:, :], ACT.Copy).then_inc(xt_hi_ready, 1)
                elif kind == "yt":
                    nc.scalar.activation(yt_hi[:, n, :], bank[:, :], ACT.Identity, bias=bias[:, 2, n:n + 1]).then_inc(yt_hi_ready, 1)
                elif kind == "qk":
                    q, part = divmod(n, 2)
                    b = next_batch(it)
                    if part == 0 and not (it is None and q < 2):
                        act.wait_ge(stacked[q % 2], (b * 2 + q // 2) * STACK_DMAS)
                    nc.scalar.activation(qk[q % 2][:, (Q_HI, K_HI)[part], :], bank[:, :], ACT.Identity,
                                         bias=bias_q[:, q:q + 1] if part == 0 else bias[:, 1, q:q + 1]).then_inc(qk_hi_ready, 1)
                elif kind == "v":
                    nc.scalar.activation(values(n, 0), bank[:, :].rearrange("p (t h d) -> p t h d", t=2, d=HD),
                                         ACT.Copy).then_inc(v1_ready, 1)

            def values_second(it, n):
                act.wait_ge(gemm_drained, drained(use_of(it, "v", n)[0]))
                nc.scalar.activation(values(n, 1), rest(n), ACT.Copy).then_inc(v2_ready, 1)

            def exps(b, n):
                q, i, heads = UNITS[n]
                width = (i + 1) * P
                act.wait_ge(max_ready, b * NU + n + 1)
                for k, j in enumerate(heads):
                    c = (q * TT + i) * HQ + j
                    ins = nc.scalar.activation(probs[:, n % 2, k * width:(k + 1) * width],
                                               score[n % 2][:, k * width:(k + 1) * width], ACT.Exp,
                                               bias=neg_max[:, c:c + 1], accum_out=sums[:, c:c + 1])
                ins.then_inc(probs_ready, 1)

            def probs_hi(b, n):
                q, i, heads = UNITS[n]
                width = (i + 1) * P * len(heads)
                act.wait_ge(turned_full, b * NU + n + 1)
                nc.scalar.activation(pt_hi[:, n % 2, 0:width], turned[n % 2][:, 0:width], ACT.Copy).then_inc(pt_hi_ready, 1)

            def half(b, n0, it, beside, more):
                for m in range(HU):
                    exps(b, n0 + m)
                    if unit_at(b, n0 + m - 1):
                        probs_hi(*unit_at(b, n0 + m - 1))
                    for kind, n in completed(beside[max(0, m - 1):m]):
                        high_part(it, kind, n)
                    for kind, n in completed(beside[max(0, m - 2):max(0, m - 1)]):
                        if kind == "v":
                            values_second(it, n)

            for kind, n in AHEAD:
                if (kind, n) == ("qk", 0):
                    act.wait_ge(consts_ready, 3)
                high_part(None, kind, n)
                if kind == "v":
                    values_second(None, n)
            halves(act, half)
            probs_hi(B - 1, NU - 1)
            high_part(B - 1, "yt", 3)

        @block.vector
        def _(dve):
            dve.sem_inc(gemm_drained, 2)
            nc.vector.tensor_copy(ident_bf[:, :], ident[:, :]).then_inc(consts_ready, 1)
            dve.wait_ge(consts_pool, 3)
            nc.vector.tensor_copy(causal_bf[:, :], causal[:, :]).then_inc(consts_ready, 1)

            def ln_stats(b, t):
                dve.wait_ge(x_loaded, b * 16)
                nc.vector.bn_stats(stats[:, t, :], x_in[:, t, :]).then_inc(stats_ready, 1)

            def ln_moments(b, t):
                dve.wait_ge(stats_ready, (b - 1) * TT + t + 1)
                nc.vector.memset(beat[:, t:t + 1], 0.0).then_inc(moments_ready, 1)
                nc.vector.bn_aggr(moments[:, t, :], stats[:, t, :]).then_inc(moments_ready, 1)

            def ln_variance(b):
                dve.wait_ge(moments_ready, 2 * TT * b)
                nc.vector.tensor_scalar(var_eps[:, :], moments[:, :, 1], EPS, None, ALU.add).then_inc(var_ready, 1)

            def ln_normalise(b, t):
                dve.wait_ge(rstd_ready, b)
                nc.vector.tensor_scalar(xn[:, t, :], x_in[:, t, :], moments[:, t, 0:1], rstd[:, t:t + 1],
                                        ALU.subtract, ALU.mult).then_inc(xn_ready, 1)

            def low_part(it, kind, n):
                use, bank = use_of(it, kind, n)
                b = next_batch(it)
                if kind == "xt":
                    dve.wait_ge(xt_hi_ready, b * KT + n + 1)
                    ins = nc.vector.tensor_tensor(xt_lo[:, n, :], bank[:, :], raw(xt_hi[:, n, :]), ALU.subtract)
                elif kind == "yt":
                    dve.wait_ge(yt_hi_ready, it * QUADS + n + 1)
                    ins = nc.vector.scalar_tensor_tensor(yt_lo[:, n, :], bank[:, :], bias[:, 2, n:n + 1], raw(yt_hi[:, n, :]),
                                                         ALU.add, ALU.subtract)
                elif kind == "qk":
                    q, part = divmod(n, 2)
                    dve.wait_ge(qk_hi_ready, (b * QUADS + q) * 2 + part + 1)
                    ins = nc.vector.scalar_tensor_tensor(qk[q % 2][:, (Q_LO, K_LO)[part], :], bank[:, :],
                                                         bias_q[:, q:q + 1] if part == 0 else bias[:, 1, q:q + 1],
                                                         raw(qk[q % 2][:, (Q_HI, K_HI)[part], :]), ALU.add, ALU.subtract)
                elif kind == "v":
                    dve.wait_ge(v1_ready, b * 4 + n + 1)
                    if not (it is None and n < 2):
                        dve.wait_ge(v_ready, b * 4 + n - 1)
                    ins = nc.vector.tensor_tensor(rest(n), bank[:, :].rearrange("p (t h d) -> p t h d", t=2, d=HD),
                                                  values(n, 0), ALU.subtract)
                else:
                    if n == 0:
                        dve.wait_ge(x_res_ready, it + 1)
                    dve.wait_ge(gemm_full, use + 1)
                    ins = nc.vector.tensor_tensor(x_res[:, n, :], bank[:, :], x_res[:, n, :], ALU.add)
                ins.then_inc(gemm_drained, 1)

            def row_max(b, n):
                q, i, heads = UNITS[n]
                width, k = (i + 1) * P, len(heads)
                c = (q * TT + i) * HQ + heads[0]
                dve.wait_ge(score_full, b * NU + n + 1)
                nc.vector.tensor_reduce(neg_max[:, c:c + k], score[n % 2][:, 0:k * width].rearrange("p (h s) -> p h s", h=k),
                                        AX, ALU.max, negate=True).then_inc(max_ready, 1)

            def probs_lo(b, n):
                q, i, heads = UNITS[n]
                width = (i + 1) * P * len(heads)
                dve.wait_ge(pt_hi_ready, b * NU + n + 1)
                nc.vector.tensor_tensor(pt_lo[:, n % 2, 0:width], turned[n % 2][:, 0:width], pt_hi[:, n % 2, 0:width],
                                        ALU.subtract).then_inc(pt_ready, 1)

            def outputs(b, n):
                g = ENDS[n]
                if g is None:
                    return
                dve.wait_ge(y_full, b * GROUPS + g + 1)
                if not (isinstance(b, int) and b == 0 and g < 2):
                    dve.wait_ge(y_ready, b * GROUPS + g - 1)
                nc.vector.reciprocal(y_rec[:, g % 2, :], sums[:, g * HQ:(g + 1) * HQ])
                nc.vector.tensor_reduce(y_sum[:, g % 2, :].rearrange("p (h d) -> p h d", h=HQ),
                                        out_y[g % 2][:, 0:HQ * V3].rearrange("p (h k d) -> p h d k", h=HQ, k=3),
                                        AX, ALU.add).then_inc(y_summed, 1)

            def half(b, n0, it, beside, more):
                for m in range(HU):
                    for kind, n in completed(beside[max(0, m - 1):m]):
                        low_part(it, kind, n)
                    if unit_at(b, n0 + m + 2):
                        row_max(*unit_at(b, n0 + m + 2))
                    if unit_at(b, n0 + m - 2):
                        outputs(*unit_at(b, n0 + m - 2))
                    probs_lo(b, n0 + m)
                    if n0 == 0 and more:
                        if TT <= m < 2 * TT:
                            ln_stats(b + 1, m - TT)
                        if TT < m <= 2 * TT:
                            ln_moments(b + 1, m - 1 - TT)
                        if m == 2 * TT + 1:
                            ln_variance(b + 1)
                        if m >= HU - TT:
                            ln_normalise(b + 1, m - (HU - TT))

            for kind, n in AHEAD:
                if (kind, n) == ("qk", 0):
                    dve.wait_ge(small_loaded, 32)
                    nc.vector.tensor_scalar(bias_q[:, :], bias[:, 0, :], HD ** -0.5, None, ALU.mult).then_inc(consts_ready, 1)
                    dve.wait_ge(consts_ready, 3)
                low_part(None, kind, n)
            row_max(0, 0)
            row_max(0, 1)
            halves(dve, half)
            for n in (NU - 2, NU - 1):
                outputs(B - 1, n)
            low_part(B - 1, "yt", 3)
            for t in range(TT):
                low_part(B - 1, "o", t)

        @block.tensor
        def _(pe):
            def step_of_product(it, kind, n, k):
                use, out = use_of(it, kind, n)
                if k == 0:
                    if kind == "xt" and it is not None:
                        pe.wait_ge(xn_ready, (it + 1) * TT)
                    if kind == "yt":
                        pe.wait_ge(y_ready, it * GROUPS + (n + 1) * TT)
                    if (kind, n) == ("o", 0):
                        pe.wait_ge(gemm_drained, drained(use_of(it, "yt", QUADS - 1)[0]))
                    pe.wait_ge(gemm_drained, drained(use - 2))
                if kind in ("xt", "yt"):
                    for t in range(TT):
                        last = nc.tensor.transpose(out[:, t * P:(t + 1) * P], (xn if kind == "xt" else y)[:, t, n * P:(n + 1) * P],
                                                   ident[:, :])
                elif kind == "qk":
                    if n == 0:
                        pe.wait_ge(gemm_drained, drained(use_of(it, "xt", k)[0]))
                    col = (WQ, WK)[n % 2] + n // 2 * P
                    last = product(nc, out[:, :], [w[:, k, col:col + P] for w in (w_hi, w_lo)],
                                   [xt[:, k, :] for xt in (xt_hi, xt_lo)], k == 0, k == KT - 1)
                elif kind == "v":
                    half, pair = divmod(n, 2)
                    t, k4 = divmod(k, KT)
                    col, tok = WV + half * D // 2, (pair * 2 + t) * P
                    last = product(nc, out[:, t * D // 2:(t + 1) * D // 2], [xt[:, k4, tok:tok + P] for xt in (xt_hi, xt_lo)],
                                   [w[:, k4, col:col + D // 2] for w in (w_hi, w_lo)], k4 == 0, k4 == KT - 1)
                else:
                    last = product(nc, out[:, :], [yt[:, k, n * P:(n + 1) * P] for yt in (yt_hi, yt_lo)],
                                   [w[:, k, WO:WO + D] for w in (w_hi, w_lo)], k == 0, k == KT - 1)
                if k == STEPS[kind] - 1:
                    last.then_inc(gemm_full, 1)

            def whole_product(it, kind, n):
                for k in range(STEPS[kind]):
                    step_of_product(it, kind, n, k)

            def scores(b, n):
                q, i, heads = UNITS[n]
                if n % PQ == 0:
                    pe.wait_ge(stacked[q % 2], (b * 2 + q // 2 + 1) * STACK_DMAS)
                width = (i + 1) * P
                st = stack[q % 2]
                for k, j in enumerate(heads):
                    at = k * width
                    nc.tensor.matmul(score[n % 2][:, at:at + width], st[:, 0, j, i * P:(i + 1) * P], st[:, 1, j, 0:width],
                                     start=True, stop=False)
                    last = nc.tensor.matmul(score[n % 2][:, at + i * P:at + width], ident_bf[:, :], causal_bf[:, :],
                                            start=False, stop=True)
                last.then_inc(score_full, 1)

            def turn(b, n):
                q, i, heads = UNITS[n]
                pe.wait_ge(probs_ready, b * NU + n + 1)
                for c in range((i + 1) * len(heads)):
                    last = nc.tensor.transpose(turned[n % 2][:, c * P:(c + 1) * P], probs[:, n % 2, c * P:(c + 1) * P],
                                               ident[:, :])
                last.then_inc(turned_full, 1)

            def weigh(b, n):
                q, i, heads = UNITS[n]
                g = q * TT + i
                pe.wait_ge(pt_ready, b * NU + n + 1)
                if heads[0] == 0:
                    if not (isinstance(b, int) and b == 0 and g < 2):
                        pe.wait_ge(y_summed, b * GROUPS + g - 1)
                    if q % 2 == 0 and i % 2 == 0:
                        pe.wait_ge(v_ready, b * 4 + q + i // 2 + 1)
                for k, j in enumerate(heads):
                    at = j * V3
                    for s in range(i + 1):
                        c = (k * (i + 1) + s) * P
                        val = v[:, s, q * HQ + j, :, :].rearrange("p k d -> p (k d)")
                        nc.tensor.matmul(out_y[g % 2][:, at:at + V3], pt_hi[:, n % 2, c:c + P], val,
                                         start=s == 0, stop=False)
                        last = nc.tensor.matmul(out_y[g % 2][:, at:at + 2 * HD], pt_lo[:, n % 2, c:c + P], val[:, 0:2 * HD],
                                                start=False, stop=s == i)
                if ENDS[n] is not None:
                    last.then_inc(y_full, 1)

            def half(b, n0, it, beside, more):
                for m in range(HU):
                    turn(b, n0 + m)
                    if unit_at(b, n0 + m + 2):
                        scores(*unit_at(b, n0 + m + 2))
                    for step in beside[m]:
                        step_of_product(it, *step)
                    if unit_at(b, n0 + m - 1):
                        weigh(*unit_at(b, n0 + m - 1))

            for use in AHEAD:
                whole_product(None, *use)
            pe.wait_ge(consts_ready, 3)
            scores(0, 0)
            scores(0, 1)
            halves(pe, half)
            weigh(B - 1, NU - 1)
            whole_product(B - 1, "yt", 3)
            for t in range(TT):
                whole_product(B - 1, "o", t)


def cross_attention_and_experts(nc, x1_dram, m_raw, m_dram, vw_dram, mask, w_experts, w_gate, out):
    HS = XH * S
    HALF = XG // 2
    PAIRS = HS // P
    MW = XG * KT * 2 * S
    assert MW == XG * D

    def neighbour(b, t, d):
        bb, tt = b + (t + d) // TT, (t + d) % TT
        if isinstance(b, int) and not 0 <= bb < B:
            return None
        return bb, tt, bb * TT + tt

    with ExitStack() as ctx:
        def sb(name, shape, dt):
            return ctx.enter_context(nc.sbuf_tensor("b_" + name, shape, dt))

        def pb(name, shape=(P, 512)):
            return ctx.enter_context(nc.psum_tensor("b_" + name, list(shape), F32))

        def sem(name):
            return ctx.enter_context(nc.semaphore("b_" + name))

        vw_raw = sb("vw_raw", [P, MW], F32)
        m_hi, m_lo = (sb(f"m_{n}", [P, MW], F32R) for n in ("hi", "lo"))
        vw_hi, vw_lo = (sb(f"vw_{n}", [P, MW], F32R) for n in ("hi", "lo"))
        we_hi, we_lo = (sb(f"we_{n}", [P, KT, 2 * D], F32R) for n in ("hi", "lo"))
        we_raw, wg_raw = sb("we_raw", [P, KT, 2 * D], F32), sb("wg_raw", [P, KT, E], F32)
        wg = sb("wg", [P, KT, 2, E], F32R)
        ident = sb("ident", [P, P], F32)
        minus_half = sb("minus_half", [P, 1], F32)
        order = sb("order", [P, E], F32)
        mask_u8 = sb("mask_u8", [P, B * S], U8)
        mask_f = sb("mask_f", [P, B * S], F32)
        mask_add = sb("mask_add", [P, B, S], F32)
        any_key = sb("any_key", [P, B], F32)
        x1 = sb("x1", [P, TT, D], F32)
        x2 = sb("x2", [P, TT, D], F32)
        beat = sb("beat", [P, 1], F32)
        ln = {k: (sb(f"stats{k}", [P, 6], F32), sb(f"moments{k}", [P, 2], F32), sb(f"var{k}", [P, 1], F32),
                  sb(f"rstd{k}", [P, 1], F32), sb(f"xn{k}", [P, D], F32)) for k in (2, 3)}
        xt2_hi, xt2_lo = (sb(f"xt2_{n}", [P, KT, P], F32R) for n in ("hi", "lo"))
        xt3_hi, xt3_lo = (sb(f"xt3_{n}", [P, KT, P], F32R) for n in ("hi", "lo"))
        row_max = sb("row_max", [P, XH], F32)
        row_sum = sb("row_sum", [P, XH], F32)
        row_inv = sb("row_inv", [P, XH], F32)
        row_scale = sb("row_scale", [P, XH], F32)
        probs = sb("probs", [P, XH, S], F32)
        pt_hi, pt_lo = (sb(f"pt_{n}", [P, PAIRS, P], F32R) for n in ("hi", "lo"))
        logits = sb("logits", [P, E], F32)
        gate_negmax = sb("gate_negmax", [P, 1], F32)
        gate_exp = sb("gate_exp", [P, E], F32)
        gate_sum = sb("gate_sum", [P, 1], F32)
        gate_top = sb("gate_top", [P, 1], F32)
        gate_rank = sb("gate_rank", [P, E], F32)
        gate_best = sb("gate_best", [P, 1], F32)
        gate_one = sb("gate_one", [P, E], F32)
        gate_inv = sb("gate_inv", [P, 1], F32)
        gate_scale = sb("gate_scale", [P, TT], F32)
        hidden = sb("hidden", [P, D], F32)
        ht_hi, ht_lo = (sb(f"ht_{n}", [P, KT, P], F32R) for n in ("hi", "lo"))
        turn = [pb(f"turn{n}") for n in range(2)]
        score = pb("score", (P, 2, 512))
        attended, hid, made, gate = pb("attended"), pb("hid"), pb("made"), pb("gate")

        we_loaded, we_hi_ready, we_lo_ready = sem("we_loaded"), sem("we_hi_ready"), sem("we_lo_ready")
        small_loaded, consts_pool, consts_ready = sem("small_loaded"), sem("consts_pool"), sem("consts_ready")
        m_loaded, m_hi_ready = sem("m_loaded"), sem("m_hi_ready")
        M_CHUNKS = 4
        MC = MW // M_CHUNKS
        m_lo_by_pool, m_lo_by_dve = sem("m_lo_by_pool"), sem("m_lo_by_dve")
        vw_loaded, vw_hi_ready = sem("vw_loaded"), sem("vw_hi_ready")
        VC = MW // 2
        vw_lo_by_pool, vw_lo_by_dve = sem("vw_lo_by_pool"), sem("vw_lo_by_dve")
        x1_loaded, out_stored = ([sem(f"{n}{t}") for t in range(TT)] for n in ("x1_loaded", "out_stored"))
        stats_ready = {k: sem(f"stats{k}_ready") for k in (2, 3)}
        moments_ready = {k: sem(f"moments{k}_ready") for k in (2, 3)}
        var_ready = {k: sem(f"var{k}_ready") for k in (2, 3)}
        rstd_ready = {k: sem(f"rstd{k}_ready") for k in (2, 3)}
        xn_ready = {k: sem(f"xn{k}_ready") for k in (2, 3)}
        xt2_full, xt2_hi_ready, xt2_ready = sem("xt2_full"), sem("xt2_hi_ready"), sem("xt2_ready")
        xt3_full, xt3_hi_ready, xt3_ready = sem("xt3_full"), sem("xt3_hi_ready"), sem("xt3_ready")
        ht_full, ht_hi_ready, ht_ready = sem("ht_full"), sem("ht_hi_ready"), sem("ht_ready")
        pt_full, pt_hi_ready, pt_ready = sem("pt_full"), sem("pt_hi_ready"), sem("pt_ready")
        score_full, masked, max_ready, shifted, exp_ready = sem("score_full"), sem("masked"), sem("max_ready"), sem("shifted"), sem("exp_ready")
        sum_ready, inv_ready, scale_ready, probs_ready = sem("sum_ready"), sem("inv_ready"), sem("scale_ready"), sem("probs_ready")
        attended_full, x2_ready = sem("attended_full"), sem("x2_ready")
        hid_full, hidden_ready = sem("hid_full"), sem("hidden_ready")
        gate_max_ready, gate_exp_ready, gate_step = sem("gate_max_ready"), sem("gate_exp_ready"), sem("gate_step")
        GATE_STEPS = 6
        made_full, out_ready = sem("made_full"), sem("out_ready")

        block = ctx.enter_context(nc.Block())

        def run(engine, step):
            for t in range(TT):
                step(0, t)
            with engine.Fori(1, B - 1) as b:
                for t in range(TT):
                    step(b, t)
            for t in range(TT):
                step(B - 1, t)
            for t in range(3):
                step(B, t)

        def is_tile(b):
            return not (isinstance(b, int) and b >= B)

        @block.sync
        def _(sp):
            def load_x1(tile):
                b, t, _ = tile
                sp.dma_start(x1[:, t, :], x1_dram[bass.ds(b, 1), t * P:(t + 1) * P, :].rearrange("b p c -> p (b c)")).then_inc(x1_loaded[t], 16)

            def load_m(b):
                sp.dma_start(m_raw[:, :], m_dram[bass.ds(b, 1)].rearrange("b p g m -> p (b g m)")).then_inc(m_loaded, 16)

            def load_vw(b):
                sp.dma_start(vw_raw[:, :], vw_dram[bass.ds(b, 1)].rearrange("b p g m -> p (b g m)")).then_inc(vw_loaded, 16)

            def step(b, t):
                done, ahead, made_tile = neighbour(b, t, -1), neighbour(b, t, 3), neighbour(b, t, -3)
                if ahead and done:
                    sp.wait_ge(x2_ready, done[2] + 1)
                    load_x1(ahead)
                if t == 0 and is_tile(b) and is_tile(b + 1):
                    wait_all(sp, (m_lo_by_pool, (b + 1) * 2), (m_lo_by_dve, (b + 1) * 2))
                    load_m(b + 1)
                if t == 1 and is_tile(b) and is_tile(b + 1):
                    wait_all(sp, (vw_lo_by_pool, b + 1), (vw_lo_by_dve, b + 1))
                    load_vw(b + 1)
                if made_tile:
                    _, mt, n = made_tile
                    sp.wait_ge(out_ready, n + 1)
                    sp.dma_start(out.rearrange("b (t p) c -> (b t) p c", p=P)[bass.ds(n, 1)].rearrange("n p c -> p (n c)"),
                                 x2[:, mt, :]).then_inc(out_stored[mt], 16)

            load_x1((0, 0, 0))
            sp.dma_start(mask_u8[:, :], mask.to_broadcast([P, B * S])).then_inc(small_loaded, 16)
            load_x1((0, 1, 1))
            load_vw(0)
            sp.dma_start(we_raw[:, :, :], w_experts).then_inc(we_loaded, 16)
            sp.dma_start(wg_raw[:, :, :], w_gate).then_inc(we_loaded, 16)
            load_x1((0, 2, 2))
            load_x1((0, 3, 3))
            run(sp, step)
            for t in range(TT):
                sp.wait_ge(out_stored[t], B * 16)

        @block.gpsimd
        def _(pool):
            def deviation(k, n):
                pool.wait_ge(var_ready[k], n + 1)
                nc.gpsimd.tensor_tensor(ln[k][3][:, :], ln[k][2][:, :], minus_half[:, :], ALU.pow).then_inc(rstd_ready[k], 1)

            def m_low(b, c):
                part = slice(c * MC, (c + 1) * MC)
                pool.wait_ge(m_hi_ready, b * M_CHUNKS + c + 1)
                nc.gpsimd.tensor_tensor(m_lo[:, part], m_raw[:, part], raw(m_hi[:, part]), ALU.subtract).then_inc(m_lo_by_pool, 1)

            def vw_low(b):
                pool.wait_ge(vw_hi_ready, b * 2 + 1)
                nc.gpsimd.tensor_tensor(vw_lo[:, 0:VC], vw_raw[:, 0:VC], raw(vw_hi[:, 0:VC]), ALU.subtract).then_inc(vw_lo_by_pool, 1)

            def step(b, t):
                done, ahead = neighbour(b, t, -1), neighbour(b, t, 2)
                last_scored = t == TT - 1 and is_tile(b) and is_tile(b + 1)
                if last_scored:
                    m_low(b + 1, 0)
                if is_tile(b):
                    n = b * TT + t
                    pool.wait_ge(scale_ready, n + 1)
                    nc.gpsimd.tensor_tensor(probs[:, :, :], probs[:, :, :], row_scale[:, :].unsqueeze(2).to_broadcast([P, XH, S]),
                                            ALU.mult).then_inc(probs_ready, 1)
                if last_scored:
                    m_low(b + 1, 2)
                if done:
                    deviation(3, done[2])
                if ahead:
                    deviation(2, ahead[2])
                if t == 0 and is_tile(b) and not (isinstance(b, int) and b == 0):
                    vw_low(b)

            nc.gpsimd.memset(ident[:, :], 0.0).then_inc(consts_pool, 1)
            nc.gpsimd.memset(minus_half[:, :], -0.5).then_inc(consts_pool, 1)
            for e in range(E):
                nc.gpsimd.memset(order[:, e:e + 1], float(E - e)).then_inc(consts_pool, 1)
            pool.wait_ge(consts_pool, 2 + E)
            nc.gpsimd.affine_select(out=ident[:, :], in_=ident[:, :], compare_op=ALU.not_equal, fill=1.0,
                                    base=0, pattern=[[-1, P]], channel_multiplier=1).then_inc(consts_pool, 1)
            m_low(0, 0)
            m_low(0, 2)
            deviation(2, 0)
            deviation(2, 1)
            vw_low(0)
            pool.wait_ge(we_hi_ready, 1)
            nc.gpsimd.tensor_tensor(wg[:, :, 1, :], wg_raw[:, :, :], raw(wg[:, :, 0, :]), ALU.subtract).then_inc(we_lo_ready, 1)
            for k in range(KT):
                pool.wait_ge(we_hi_ready, k + 2)
                nc.gpsimd.tensor_tensor(we_lo[:, k, :], we_raw[:, k, :], raw(we_hi[:, k, :]), ALU.subtract).then_inc(we_lo_ready, 1)
            run(pool, step)

        @block.scalar
        def _(act):
            def copy_hi(dst, src, full, count, ready):
                act.wait_ge(full, count)
                nc.scalar.activation(dst, src, ACT.Copy).then_inc(ready, 1)

            def split_m(b, chunks):
                for c in chunks:
                    part = slice(c * MC, (c + 1) * MC)
                    if c == 0 and not (isinstance(b, int) and b == 0):
                        act.wait_ge(m_loaded, b * 16)
                    nc.scalar.activation(m_hi[:, part], m_raw[:, part], ACT.Copy).then_inc(m_hi_ready, 1)

            def split_vw(b):
                act.wait_ge(vw_loaded, b * 16 + 16)
                for part in (slice(0, VC), slice(VC, MW)):
                    nc.scalar.activation(vw_hi[:, part], vw_raw[:, part], ACT.Copy).then_inc(vw_hi_ready, 1)

            def flat(ap):
                return ap[:, :, :].rearrange("p k w -> p (k w)")

            def step(b, t):
                done, gated, made_tile, ahead = (neighbour(b, t, d) for d in (-1, -2, -3, 1))
                here = b * TT + t if is_tile(b) else None
                last_scored = t == TT - 1 and is_tile(b) and is_tile(b + 1)
                start = isinstance(here, int) and here == 0
                if done:
                    for half in range(2):
                        w = PAIRS // 2
                        copy_hi(pt_hi[:, half * w:(half + 1) * w, :].rearrange("p k w -> p (k w)"), turn[half][:, :],
                                pt_full, done[2] * 2 + half + 1, pt_hi_ready)
                if made_tile:
                    act.wait_ge(gate_max_ready, made_tile[2] + 1)
                    nc.scalar.activation(gate_exp[:, :], logits[:, :], ACT.Exp, bias=gate_negmax[:, :],
                                         accum_out=gate_sum[:, :]).then_inc(gate_exp_ready, 1)
                if last_scored:
                    act.wait_ge(score_full, here + 1)
                    split_m(b + 1, (0, 1))
                if gated:
                    copy_hi(flat(xt3_hi), turn[0][:, :], xt3_full, gated[2] + 1, xt3_hi_ready)
                if made_tile:
                    copy_hi(flat(ht_hi), turn[1][:, :], ht_full, made_tile[2] + 1, ht_hi_ready)
                if ahead and start:
                    copy_hi(flat(xt2_hi), turn[0][:, :], xt2_full, ahead[2] + 1, xt2_hi_ready)
                if here is not None:
                    act.wait_ge(shifted, here + 1)
                    nc.scalar.activation(probs[:, :, :], probs[:, :, :], ACT.Exp).then_inc(exp_ready, 1)
                if last_scored:
                    split_m(b + 1, (2, 3))
                if ahead and not start:
                    copy_hi(flat(xt2_hi), turn[0][:, :], xt2_full, ahead[2] + 1, xt2_hi_ready)
                if t == 0 and here is not None and not (isinstance(b, int) and b == 0):
                    act.wait_ge(attended_full, here)
                    split_vw(b)

            split_m(0, range(M_CHUNKS))
            copy_hi(flat(xt2_hi), turn[0][:, :], xt2_full, 1, xt2_hi_ready)
            split_vw(0)
            act.wait_ge(we_loaded, 32)
            nc.scalar.activation(wg[:, :, 0, :], wg_raw[:, :, :], ACT.Copy).then_inc(we_hi_ready, 1)
            for k in range(KT):
                nc.scalar.activation(we_hi[:, k, :], we_raw[:, k, :], ACT.Copy).then_inc(we_hi_ready, 1)
            run(act, step)

        @block.vector
        def _(dve):
            def low(dst, psum, hi, hi_ready, count, ready):
                dve.wait_ge(hi_ready, count)
                nc.vector.tensor_tensor(dst, psum, raw(hi), ALU.subtract).then_inc(ready, 1)

            def flat(ap):
                return ap[:, :, :].rearrange("p k w -> p (k w)")

            def layernorm_moments(k, src, n):
                stats, moments, var, _, _ = ln[k]
                nc.vector.bn_stats(stats[:, :], src).then_inc(stats_ready[k], 1)
                dve.wait_ge(stats_ready[k], n + 1)
                nc.vector.memset(beat[:, :], 0.0).then_inc(moments_ready[k], 1)
                nc.vector.bn_aggr(moments[:, :], stats[:, :]).then_inc(moments_ready[k], 1)
                dve.wait_ge(moments_ready[k], 2 * (n + 1))
                nc.vector.tensor_scalar(var[:, :], moments[:, 1:2], EPS, None, ALU.add).then_inc(var_ready[k], 1)

            def normalise(k, src, n):
                _, moments, _, rstd, xn = ln[k]
                dve.wait_ge(rstd_ready[k], n + 1)
                nc.vector.tensor_scalar(xn[:, :], src, moments[:, 0:1], rstd[:, :], ALU.subtract, ALU.mult).then_inc(xn_ready[k], 1)

            def layernorm2_moments(tile):
                b, t, n = tile
                dve.wait_ge(x1_loaded[t], b * 16 + 16)
                layernorm_moments(2, x1[:, t, :], n)

            def choose_expert(n, t):
                s = n * GATE_STEPS + 1
                dve.wait_ge(gate_exp_ready, n + 1)
                nc.vector.tensor_reduce(gate_top[:, :], gate_exp[:, :], AX, ALU.max).then_inc(gate_step, 1)
                nc.vector.reciprocal(gate_inv[:, :], gate_sum[:, :]).then_inc(gate_step, 1)
                dve.wait_ge(gate_step, s + 2)
                nc.vector.scalar_tensor_tensor(gate_rank[:, :], gate_exp[:, :], gate_top[:, :], order[:, :],
                                               ALU.is_ge, ALU.mult).then_inc(gate_step, 1)
                nc.vector.tensor_scalar(gate_scale[:, t:t + 1], gate_inv[:, :], gate_top[:, :], SCALING, ALU.mult, ALU.mult)
                dve.wait_ge(gate_step, s + 3)
                nc.vector.tensor_reduce(gate_best[:, :], gate_rank[:, :], AX, ALU.max).then_inc(gate_step, 1)
                dve.wait_ge(gate_step, s + 4)
                nc.vector.tensor_scalar(gate_one[:, :], gate_rank[:, :], gate_best[:, :], None, ALU.is_equal).then_inc(gate_step, 1)
                dve.wait_ge(gate_step, s + 5)

            def m_low(b, c):
                part = slice(c * MC, (c + 1) * MC)
                dve.wait_ge(m_hi_ready, b * M_CHUNKS + c + 1)
                nc.vector.tensor_tensor(m_lo[:, part], m_raw[:, part], raw(m_hi[:, part]), ALU.subtract).then_inc(m_lo_by_dve, 1)

            def vw_low(b):
                dve.wait_ge(vw_hi_ready, b * 2 + 2)
                nc.vector.tensor_tensor(vw_lo[:, VC:], vw_raw[:, VC:], raw(vw_hi[:, VC:]), ALU.subtract).then_inc(vw_lo_by_dve, 1)

            def step(b, t):
                done, gated, made_tile, ahead, far = (neighbour(b, t, d) for d in (-1, -2, -3, 1, 2))
                here = b * TT + t if is_tile(b) else None
                last_scored = t == TT - 1 and is_tile(b) and is_tile(b + 1)
                start = isinstance(here, int) and here == 0
                if done:
                    for half in range(2):
                        w = PAIRS // 2
                        part = slice(half * w, (half + 1) * w)
                        low(pt_lo[:, part, :].rearrange("p k w -> p (k w)"), turn[half][:, :],
                            pt_hi[:, part, :].rearrange("p k w -> p (k w)"), pt_hi_ready, done[2] * 2 + half + 1, pt_ready)
                if made_tile:
                    _, mt, n = made_tile
                    dve.wait_ge(hid_full, n + 1)
                    nc.vector.tensor_reduce(logits[:, :], gate[:, 0:2 * E].rearrange("p (k e) -> p e k", k=2), AX, ALU.add)\
                        .then_inc(gate_step, 1)
                    dve.wait_ge(gate_step, n * GATE_STEPS + 1)
                    nc.vector.tensor_reduce(gate_negmax[:, :], logits[:, :], AX, ALU.max, negate=True).then_inc(gate_max_ready, 1)
                    choose_expert(n, mt)
                    nc.vector.tensor_tensor(hidden[:, :].rearrange("p (e r) -> p e r", e=E),
                                            hid[:, :].rearrange("p (e r) -> p e r", e=E),
                                            gate_one[:, :].unsqueeze(2).to_broadcast([P, E, R]), ALU.mult).then_inc(hidden_ready, 1)
                if here is not None:
                    dve.wait_ge(score_full, here + 1)
                    s = score[:, :, :].rearrange("p a (h s) -> p (a h) s", s=S)
                    nc.vector.tensor_tensor(probs[:, :, :], s, mask_add[:, bass.ds(b, 1), :].to_broadcast([P, XH, S]),
                                            ALU.add).then_inc(masked, 1)
                    if start:
                        low(flat(xt2_lo), turn[0][:, :], flat(xt2_hi), xt2_hi_ready, ahead[2] + 1, xt2_ready)
                    dve.wait_ge(masked, here + 1)
                    nc.vector.tensor_reduce(row_max[:, :], probs[:, :, :], AX, ALU.max).then_inc(max_ready, 1)
                    dve.wait_ge(max_ready, here + 1)
                    nc.vector.tensor_tensor(probs[:, :, :], probs[:, :, :], row_max[:, :].unsqueeze(2).to_broadcast([P, XH, S]),
                                            ALU.subtract).then_inc(shifted, 1)
                if gated:
                    low(flat(xt3_lo), turn[0][:, :], flat(xt3_hi), xt3_hi_ready, gated[2] + 1, xt3_ready)
                if made_tile:
                    low(flat(ht_lo), turn[1][:, :], flat(ht_hi), ht_hi_ready, made_tile[2] + 1, ht_ready)
                if last_scored:
                    m_low(b + 1, 1)
                if here is not None:
                    dve.wait_ge(exp_ready, here + 1)
                    nc.vector.tensor_reduce(row_sum[:, :], probs[:, :, :], AX, ALU.add).then_inc(sum_ready, 1)
                    dve.wait_ge(sum_ready, here + 1)
                    nc.vector.reciprocal(row_inv[:, :], row_sum[:, :]).then_inc(inv_ready, 1)
                    dve.wait_ge(inv_ready, here + 1)
                    nc.vector.tensor_scalar(row_scale[:, :], row_inv[:, :], any_key[:, bass.ds(b, 1)], None,
                                            ALU.mult).then_inc(scale_ready, 1)
                if done:
                    db, dt_, n = done
                    dve.wait_ge(attended_full, n + 1)
                    if not (isinstance(n, int) and n < TT):
                        dve.wait_ge(out_stored[dt_], db * 16)
                    nc.vector.tensor_tensor(x2[:, dt_, :], attended[:, :], x1[:, dt_, :], ALU.add).then_inc(x2_ready, 1)
                    dve.wait_ge(x2_ready, n + 1)
                    layernorm_moments(3, x2[:, dt_, :], n)
                if ahead and not start:
                    low(flat(xt2_lo), turn[0][:, :], flat(xt2_hi), xt2_hi_ready, ahead[2] + 1, xt2_ready)
                if last_scored:
                    m_low(b + 1, 3)
                if far:
                    layernorm2_moments(far)
                if done:
                    normalise(3, x2[:, done[1], :], done[2])
                if far:
                    normalise(2, x1[:, far[1], :], far[2])
                if made_tile:
                    _, mt, n = made_tile
                    dve.wait_ge(made_full, n + 1)
                    nc.vector.scalar_tensor_tensor(x2[:, mt, :], made[:, :], gate_scale[:, mt:mt + 1], x2[:, mt, :],
                                                   ALU.mult, ALU.add).then_inc(out_ready, 1)
                if t == 0 and here is not None and not start:
                    vw_low(b)

            m_low(0, 1)
            m_low(0, 3)
            for n in range(2):
                layernorm2_moments((0, n, n))
                normalise(2, x1[:, n, :], n)
                if n == 0:
                    low(flat(xt2_lo), turn[0][:, :], flat(xt2_hi), xt2_hi_ready, 1, xt2_ready)
            dve.wait_ge(small_loaded, 16)
            nc.vector.tensor_copy(mask_f[:, :], mask_u8[:, :]).then_inc(consts_ready, 1)
            dve.wait_ge(consts_ready, 1)
            nc.vector.tensor_scalar(mask_add[:, :, :], mask_f[:, :].rearrange("p (b s) -> p b s", b=B), 1.0, -MASKED,
                                    ALU.subtract, ALU.mult).then_inc(consts_ready, 1)
            nc.vector.tensor_reduce(any_key[:, :], mask_f[:, :].rearrange("p (b s) -> p b s", b=B), AX, ALU.max).then_inc(consts_ready, 1)
            dve.wait_ge(consts_ready, 3)
            vw_low(0)
            run(dve, step)

        @block.tensor
        def _(pe):
            def transpose_tile(bank, src, width, ready, count, full):
                pe.wait_ge(ready, count)
                for k in range(width):
                    last = nc.tensor.transpose(bank[:, k * P:(k + 1) * P], src(k), ident[:, :])
                last.then_inc(full, 1)

            def view_m(m, half, k):
                return m[:, :].rearrange("p (g k w) -> p g k w", g=XG, k=KT)[:, half * HALF:(half + 1) * HALF, k, :]

            def turn_ahead(tile):
                n = tile[2]
                transpose_tile(turn[0], lambda k: ln[2][4][:, k * P:(k + 1) * P], KT, xn_ready[2], n + 1, xt2_full)

            def make_scores(b, t, n):
                if t == 0:
                    pe.wait_ge(m_lo_by_pool, (b + 1) * 2)
                    pe.wait_ge(m_lo_by_dve, (b + 1) * 2)
                pe.wait_ge(xt2_ready, n + 1)
                if not (isinstance(n, int) and n == 0):
                    pe.wait_ge(masked, n)
                for half in range(2):
                    o = score[:, half, :]
                    for k in range(KT):
                        last = product(nc, o, [x[:, k, :] for x in (xt2_hi, xt2_lo)], [view_m(m, half, k) for m in (m_hi, m_lo)],
                                       k == 0, k == KT - 1)
                last.then_inc(score_full, 1)
            def step(b, t):
                done, gated, made_tile, ahead = (neighbour(b, t, d) for d in (-1, -2, -3, 1))
                here = b * TT + t if is_tile(b) else None
                second = isinstance(here, int) and here == 1
                if second:
                    make_scores(b, t, here)
                if done:
                    n = done[2]
                    for half in range(2):
                        if half == 0:
                            pe.wait_ge(xt2_ready, n + 2) if here is not None else None
                        elif made_tile is not None and neighbour(b, t, -4) is not None:
                            pe.wait_ge(ht_ready, n - 2)
                        transpose_tile(turn[half], lambda k: probs[:, :, :].rearrange("p h s -> p (h s)")[:, (half * 4 + k) * P:(half * 4 + k + 1) * P],
                                       4, probs_ready, n + 1, pt_full)
                if here is not None and not second:
                    make_scores(b, t, here)
                if isinstance(here, int) and here == 0:
                    turn_ahead(ahead)
                if gated:
                    if done:
                        pe.wait_ge(pt_ready, done[2] * 2 + 1)
                    transpose_tile(turn[0], lambda k: ln[3][4][:, k * P:(k + 1) * P], KT, xn_ready[3], gated[2] + 1, xt3_full)
                if made_tile:
                    if done:
                        pe.wait_ge(pt_ready, done[2] * 2 + 2)
                    transpose_tile(turn[1], lambda k: hidden[:, k * P:(k + 1) * P], KT, hidden_ready, made_tile[2] + 1, ht_full)
                if done:
                    db, dt_, n = done
                    if dt_ == 0:
                        pe.wait_ge(vw_lo_by_pool, db + 1)
                        pe.wait_ge(vw_lo_by_dve, db + 1)
                    pe.wait_ge(pt_ready, n * 2 + 2)
                    if not (isinstance(n, int) and n == 0):
                        pe.wait_ge(x2_ready, n)
                    for g in range(PAIRS):
                        last = product(nc, attended[:, :], [p[:, g, :] for p in (pt_hi, pt_lo)],
                                       [w[:, g * D:(g + 1) * D] for w in (vw_hi, vw_lo)], g == 0, g == PAIRS - 1)
                    last.then_inc(attended_full, 1)
                if ahead and not (isinstance(here, int) and here == 0):
                    if gated:
                        pe.wait_ge(xt3_ready, gated[2] + 1)
                    elif done:
                        pe.wait_ge(pt_ready, done[2] * 2 + 1)
                    turn_ahead(ahead)
                if made_tile:
                    n = made_tile[2]
                    pe.wait_ge(ht_ready, n + 1)
                    if not (isinstance(n, int) and n == 0):
                        pe.wait_ge(out_ready, n)
                    for k in range(KT):
                        last = product(nc, made[:, :], [h[:, k, :] for h in (ht_hi, ht_lo)],
                                       [w[:, k, D:2 * D] for w in (we_hi, we_lo)], k == 0, k == KT - 1)
                    last.then_inc(made_full, 1)
                if gated:
                    n = gated[2]
                    pe.wait_ge(xt3_ready, n + 1)
                    if not (isinstance(n, int) and n == 0):
                        pe.wait_ge(hidden_ready, n)
                    if isinstance(n, int) and n == 0:
                        pe.wait_ge(we_lo_ready, 1 + KT)
                    for k in range(KT):
                        nc.tensor.matmul(gate[:, 0:2 * E], xt3_hi[:, k, :], wg[:, k, :, :].rearrange("p h e -> p (h e)"),
                                         start=k == 0, stop=False)
                        nc.tensor.matmul(gate[:, 0:E], xt3_lo[:, k, :], wg[:, k, 0, :], start=False, stop=k == KT - 1)
                    for k in range(KT):
                        last = product(nc, hid[:, :], [x[:, k, :] for x in (xt3_hi, xt3_lo)],
                                       [w[:, k, 0:D] for w in (we_hi, we_lo)], k == 0, k == KT - 1)
                    last.then_inc(hid_full, 1)

            pe.wait_ge(consts_pool, 2 + E + 1)
            turn_ahead((0, 0, 0))
            run(pe, step)


def build(nc, x, mask, w_group, ctx_t, w_self, bias_self, bo, w_experts, w_gate, out):
    m_dram = nc.dram_tensor("m_dram", [B, P, XG, KT * 2 * S], F32, kind="Internal").ap()
    vw_dram = nc.dram_tensor("vw_dram", [B, P, XG, D], F32, kind="Internal").ap()
    x1_dram = nc.dram_tensor("x1_dram", [B, T, D], F32, kind="Internal").ap()
    with ExitStack() as ctx:
        shared = ctx.enter_context(nc.sbuf_tensor("shared", [P, XG * D], F32))
        vw_stored = ctx.enter_context(nc.semaphore("vw_stored"))
        with ExitStack() as inner:
            self_split = [inner.enter_context(nc.sbuf_tensor(f"w_self_{n}", [P, KT, 4 * D], F32R)) for n in ("hi", "lo")]
            x_in, xn = (inner.enter_context(nc.sbuf_tensor(n, [P, TT, D], F32)) for n in ("x_in", "xn"))
            ident = inner.enter_context(nc.sbuf_tensor("ident", [P, P], F32))
            vw_out = shared[:, :].rearrange("p (b h e) -> p b h e", b=B // 2, h=XH // XG)
            cross_products(nc, w_group, ctx_t, m_dram, vw_dram, w_self, self_split, x, x_in, xn, ident, vw_out, vw_stored)
            self_attention(nc, x, self_split, bias_self, bo, x1_dram, x_in, xn, ident, vw_stored, m_dram, shared[:, :])
        cross_attention_and_experts(nc, x1_dram, shared, m_dram, vw_dram, mask, w_experts, w_gate, out)


def kernel(x, ctx_1024, mask_BxS2_bf1, L0_attn_Wq, L0_attn_bq, L0_attn_Wk, L0_attn_bk, L0_attn_Wv, L0_attn_bv, L0_attn_Wo,
           L0_attn_bo, L0_xattn_Wq, L0_xattn_Wk, L0_xattn_Wv, L0_xattn_Wo, L0_ffn_A, L0_ffn_Bw, L0_ffn_Wg):
    import numpy as np
    import concourse.bacc as bacc
    from concourse.bass_utils import run_bass_kernel_spmd

    def rows(a):
        return a.reshape(-1, P, a.shape[-1]).transpose(1, 0, 2)

    heads = [np.asarray(w).transpose(1, 0, 2).reshape(D, H * HD) for w in (L0_attn_Wq, L0_attn_Wk, L0_attn_Wv)]
    w_self = rows(np.concatenate(heads + [np.asarray(L0_attn_Wo)], axis=1))
    bias_self = np.stack([np.asarray(v).reshape(QUADS, P).T for v in (L0_attn_bq, L0_attn_bk, L0_attn_bv)], axis=1)
    wk, wv = (np.asarray(w).reshape(CT, P, XG, XD).transpose(2, 1, 0, 3).reshape(XG, P, CT * XD) for w in (L0_xattn_Wk, L0_xattn_Wv))
    wq = np.asarray(L0_xattn_Wq).reshape(D, XG, XH // XG, XD).transpose(1, 3, 2, 0).reshape(XG, P, -1)
    wo = np.asarray(L0_xattn_Wo).reshape(XG, XH // XG, XD, D).transpose(0, 2, 1, 3).reshape(XG, P, -1)
    w_group = np.concatenate([wk, wv, wq, wo], axis=2)
    ctx_t = rows(np.asarray(ctx_1024).reshape(B * S, DC).T)
    w_experts = rows(np.concatenate([np.asarray(L0_ffn_A).reshape(E * R, D).T,
                                     np.asarray(L0_ffn_Bw).transpose(0, 2, 1).reshape(E * R, D)], axis=1))
    w_gate = rows(np.asarray(L0_ffn_Wg).T)
    arrays = {"x": x, "mask": np.asarray(mask_BxS2_bf1).view(np.uint8).reshape(1, B * S), "w_group": w_group, "ctx_t": ctx_t,
              "w_self": w_self, "bias_self": bias_self, "bo": np.asarray(L0_attn_bo).reshape(1, D), "w_experts": w_experts,
              "w_gate": w_gate}
    arrays = {k: np.ascontiguousarray(a) for k, a in arrays.items()}
    nc = bacc.Bacc("TRN2", target_bir_lowering=False, num_devices=1, dynamic_dma_scratch_size=1024)
    aps = {k: nc.dram_tensor(k + "_dram", a.shape, mybir.dt.from_np(a.dtype), kind="ExternalInput").ap() for k, a in arrays.items()}
    out = nc.dram_tensor("out_dram", [B, T, D], F32, kind="ExternalOutput").ap()
    build(nc, out=out, **aps)
    got = run_bass_kernel_spmd(nc, [{k + "_dram": a for k, a in arrays.items()}], core_ids=[0])
    return got.results[0]["out_dram"]
```
